# Optimizing a Trainium2 kernel written in Bass

```python
import numpy as np
import jax
import jax.numpy as jnp

def _softmax(x, axis=-1):
    return jax.nn.softmax(x, axis=axis)

def _gelu(x):
    return jax.nn.gelu(x, approximate=True)

def _silu(x):
    return jax.nn.silu(x)

def _sigmoid(x):
    return jax.nn.sigmoid(x)

def _layernorm(x, axis=-1, eps=1e-05):
    m = jnp.mean(x, axis=axis, keepdims=True)
    v = jnp.var(x, axis=axis, keepdims=True)
    return (x - m) / jnp.sqrt(v + eps)

def _scatter_add(tgt, idx, src, axis=0):
    return tgt.at[idx].add(src)

def _segment_sum(src, seg, n):
    return jax.ops.segment_sum(src, seg, n)
kernel_name = 'mk_vit_tower_d1_tok_img1024_r4_246456'

def setup_inputs(seed: int=0):
    np.random.seed(seed)
    _w = jnp.asarray

    def _rec_inputs():
        import jax
        import jax.numpy as jnp
        _rk = jax.random.key(seed)
        x = -0.00016672 + 0.999947 * jax.random.normal(jax.random.fold_in(_rk, 1), (64, 96, 96, 3), jnp.float32)
        return x
    x = _rec_inputs()

    def _L0_tok_setup():
        import jax, jax.numpy as jnp
        import numpy as np
        P = 16
        E = 256

        def patchify(images, patch_size):
            B, H, W, C = images.shape
            hp, wp = (H // patch_size, W // patch_size)
            x = images.reshape(B, hp, patch_size, wp, patch_size, C)
            x = x.transpose(0, 1, 3, 2, 4, 5)
            return x.reshape(B, hp * wp, patch_size * patch_size * C)
        key = jax.random.key(seed)
        k_img, k_w, k_b, k_pos = jax.random.split(key, 4)
        B, H, W, C = (64, 96, 96, 3)
        patch_dim = P * P * C
        patch_count = H // P * (W // P)
        images = jax.random.normal(k_img, (B, H, W, C), dtype=jnp.float32)
        W_proj = jax.random.normal(k_w, (E, patch_dim), dtype=jnp.float32) * patch_dim ** (-0.5)
        b_proj = jax.random.normal(k_b, (E,), dtype=jnp.float32) * 0.02
        pos_emb = jax.random.normal(k_pos, (patch_count, E), dtype=jnp.float32) * 0.02
        return {'images': images, 'W_proj': W_proj, 'b_proj': b_proj, 'pos_emb': pos_emb}
    _L0_tok_all = _L0_tok_setup()
    _L0_tok_in = {k: v for k, v in _L0_tok_all.items() if k in ('W_proj', 'b_proj', 'pos_emb')}
    del _L0_tok_all

    def _L0_attn_setup():
        import jax, jax.numpy as jnp
        import numpy as np
        B, T, D, H, K, V, F = (4, 1024, 256, 8, 128, 128, 1024)
        EPS = 1e-05

        def layernorm(x, w, b):
            m = jnp.mean(x, -1, keepdims=True)
            v = jnp.var(x, -1, keepdims=True)
            return (x - m) * jax.lax.rsqrt(v + EPS) * w + b

        def l2norm(x):
            return x * jax.lax.rsqrt(jnp.sum(x * x, -1, keepdims=True) + 1e-06)

        def gdn_recurrence(q, k, v, alpha, beta):
            qT = jnp.moveaxis(q, 1, 0)
            kT = jnp.moveaxis(k, 1, 0)
            vT = jnp.moveaxis(v, 1, 0)
            aT = jnp.moveaxis(alpha, 1, 0)
            bT = jnp.moveaxis(beta, 1, 0)

            def step(S, inp):
                q_t, k_t, v_t, a_t, b_t = inp
                kS = jnp.einsum('bhk,bhkv->bhv', k_t, S)
                bk = (b_t[..., None] * k_t)[..., :, None]
                S = a_t[..., None, None] * (S - bk * kS[..., None, :]) + bk * v_t[..., None, :]
                o = jnp.einsum('bhk,bhkv->bhv', q_t, S)
                return (S, o)
            S0 = jnp.zeros((q.shape[0], H, K, V), q.dtype)
            _, oT = jax.lax.scan(step, S0, (qT, kT, vT, aT, bT))
            return jnp.moveaxis(oT, 0, 1)
        key = jax.random.key(seed)
        ks = jax.random.split(key, 12)
        s = 0.02
        return {'x': jax.random.normal(ks[0], (B, T, D), jnp.float32), 'Wq': jax.random.normal(ks[1], (D, H * K), jnp.float32) * s, 'Wk': jax.random.normal(ks[2], (D, H * K), jnp.float32) * s, 'Wv': jax.random.normal(ks[3], (D, H * V), jnp.float32) * s, 'Wb': jax.random.normal(ks[4], (D, H), jnp.float32) * s, 'Wa': jax.random.normal(ks[5], (D, H), jnp.float32) * s, 'Wo': jax.random.normal(ks[6], (H * V, D), jnp.float32) * s, 'ln1_w': jnp.ones((D,), jnp.float32), 'ln1_b': jnp.zeros((D,), jnp.float32), 'ln2_w': jnp.ones((D,), jnp.float32), 'ln2_b': jnp.zeros((D,), jnp.float32), 'W1': jax.random.normal(ks[7], (D, F), jnp.float32) * s, 'b1': jnp.zeros((F,), jnp.float32), 'W2': jax.random.normal(ks[8], (F, D), jnp.float32) * s, 'b2': jnp.zeros((D,), jnp.float32)}
    _L0_attn_all = _L0_attn_setup()
    _L0_attn_in = {k: v for k, v in _L0_attn_all.items() if k in ('Wq', 'Wk', 'Wv', 'Wb', 'Wa', 'Wo', 'ln1_w', 'ln1_b', 'ln2_w', 'ln2_b', 'W1', 'b1', 'W2', 'b2')}
    del _L0_attn_all

    def _L0_ffn_setup():
        import jax, jax.numpy as jnp
        import numpy as np
        EPS = 1e-09
        RMS_EPS = 1e-06
        TOP_K = 2
        LOOPS = 2

        def _rmsnorm(x, w):
            var = jnp.mean(x * x, axis=-1, keepdims=True)
            return x * jax.lax.rsqrt(var + RMS_EPS) * w

        def _swiglu(x, w1, w3, w2):
            h = jax.nn.silu(x @ w1) * (x @ w3)
            return h @ w2
        key = jax.random.key(seed)
        ks = jax.random.split(key, 5)
        B, S, D, F, E = (4, 512, 256, 512, 8)
        z = jax.random.normal(ks[0], (B, S, D), dtype=jnp.float32)
        norm_w = jnp.ones((D,), dtype=jnp.float32)
        router_w = jax.random.normal(ks[1], (D, E), dtype=jnp.float32) * 0.02
        w1 = jax.random.normal(ks[2], (E, D, F), dtype=jnp.float32) * 0.02
        w3 = jax.random.normal(ks[3], (E, D, F), dtype=jnp.float32) * 0.02
        w2 = jax.random.normal(ks[4], (E, F, D), dtype=jnp.float32) * 0.02
        return {'z': z, 'norm_w': norm_w, 'router_w': router_w, 'w1': w1, 'w3': w3, 'w2': w2}
    _L0_ffn_all = _L0_ffn_setup()
    _L0_ffn_in = {k: v for k, v in _L0_ffn_all.items() if k in ('norm_w', 'router_w', 'w1', 'w3', 'w2')}
    del _L0_ffn_all
    return {'x': x, 'L0_tok_W_proj': _L0_tok_in['W_proj'], 'L0_tok_b_proj': _L0_tok_in['b_proj'], 'L0_tok_pos_emb': _L0_tok_in['pos_emb'], 'L0_attn_Wq': _L0_attn_in['Wq'], 'L0_attn_Wk': _L0_attn_in['Wk'], 'L0_attn_Wv': _L0_attn_in['Wv'], 'L0_attn_Wb': _L0_attn_in['Wb'], 'L0_attn_Wa': _L0_attn_in['Wa'], 'L0_attn_Wo': _L0_attn_in['Wo'], 'L0_attn_ln1_w': _L0_attn_in['ln1_w'], 'L0_attn_ln1_b': _L0_attn_in['ln1_b'], 'L0_attn_ln2_w': _L0_attn_in['ln2_w'], 'L0_attn_ln2_b': _L0_attn_in['ln2_b'], 'L0_attn_W1': _L0_attn_in['W1'], 'L0_attn_b1': _L0_attn_in['b1'], 'L0_attn_W2': _L0_attn_in['W2'], 'L0_attn_b2': _L0_attn_in['b2'], 'L0_ffn_norm_w': _L0_ffn_in['norm_w'], 'L0_ffn_router_w': _L0_ffn_in['router_w'], 'L0_ffn_w1': _L0_ffn_in['w1'], 'L0_ffn_w3': _L0_ffn_in['w3'], 'L0_ffn_w2': _L0_ffn_in['w2']}

def reference(x, L0_tok_W_proj, L0_tok_b_proj, L0_tok_pos_emb, L0_attn_Wq, L0_attn_Wk, L0_attn_Wv, L0_attn_Wb, L0_attn_Wa, L0_attn_Wo, L0_attn_ln1_w, L0_attn_ln1_b, L0_attn_ln2_w, L0_attn_ln2_b, L0_attn_W1, L0_attn_b1, L0_attn_W2, L0_attn_b2, L0_ffn_norm_w, L0_ffn_router_w, L0_ffn_w1, L0_ffn_w3, L0_ffn_w2):
    import jax
    import jax.numpy as jnp

    def _L0_tok_ref(images, W_proj, b_proj, pos_emb):
        import jax, jax.numpy as jnp
        import numpy as np
        P = 16
        E = 256

        def patchify(images, patch_size):
            B, H, W, C = images.shape
            hp, wp = (H // patch_size, W // patch_size)
            x = images.reshape(B, hp, patch_size, wp, patch_size, C)
            x = x.transpose(0, 1, 3, 2, 4, 5)
            return x.reshape(B, hp * wp, patch_size * patch_size * C)
        patches = patchify(images, P)
        out = jnp.einsum('bnd,ed->bne', patches, W_proj) + b_proj + pos_emb[None, :, :]
        return out

    def _L0_attn_ref(x, Wq, Wk, Wv, Wb, Wa, Wo, ln1_w, ln1_b, ln2_w, ln2_b, W1, b1, W2, b2):
        import jax, jax.numpy as jnp
        import numpy as np
        B, T, D, H, K, V, F = (4, 1024, 256, 8, 128, 128, 1024)
        EPS = 1e-05

        def layernorm(x, w, b):
            m = jnp.mean(x, -1, keepdims=True)
            v = jnp.var(x, -1, keepdims=True)
            return (x - m) * jax.lax.rsqrt(v + EPS) * w + b

        def l2norm(x):
            return x * jax.lax.rsqrt(jnp.sum(x * x, -1, keepdims=True) + 1e-06)

        def gdn_recurrence(q, k, v, alpha, beta):
            qT = jnp.moveaxis(q, 1, 0)
            kT = jnp.moveaxis(k, 1, 0)
            vT = jnp.moveaxis(v, 1, 0)
            aT = jnp.moveaxis(alpha, 1, 0)
            bT = jnp.moveaxis(beta, 1, 0)

            def step(S, inp):
                q_t, k_t, v_t, a_t, b_t = inp
                kS = jnp.einsum('bhk,bhkv->bhv', k_t, S)
                bk = (b_t[..., None] * k_t)[..., :, None]
                S = a_t[..., None, None] * (S - bk * kS[..., None, :]) + bk * v_t[..., None, :]
                o = jnp.einsum('bhk,bhkv->bhv', q_t, S)
                return (S, o)
            S0 = jnp.zeros((q.shape[0], H, K, V), q.dtype)
            _, oT = jax.lax.scan(step, S0, (qT, kT, vT, aT, bT))
            return jnp.moveaxis(oT, 0, 1)
        b, t, _ = x.shape
        n = layernorm(x, ln1_w, ln1_b)
        q = l2norm(jax.nn.silu(n @ Wq).reshape(b, t, H, K))
        k = l2norm(jax.nn.silu(n @ Wk).reshape(b, t, H, K))
        v = jax.nn.silu(n @ Wv).reshape(b, t, H, V)
        beta = jax.nn.sigmoid(n @ Wb)
        alpha = jax.nn.sigmoid(n @ Wa)
        o = gdn_recurrence(q, k, v, alpha, beta).reshape(b, t, H * V) @ Wo
        x = x + o
        h = layernorm(x, ln2_w, ln2_b)
        x = x + (jax.nn.gelu(h @ W1 + b1, approximate=False) @ W2 + b2)
        return x

    def _L0_ffn_ref(z, norm_w, router_w, w1, w3, w2):
        import jax, jax.numpy as jnp
        import numpy as np
        EPS = 1e-09
        RMS_EPS = 1e-06
        TOP_K = 2
        LOOPS = 2

        def _rmsnorm(x, w):
            var = jnp.mean(x * x, axis=-1, keepdims=True)
            return x * jax.lax.rsqrt(var + RMS_EPS) * w

        def _swiglu(x, w1, w3, w2):
            h = jax.nn.silu(x @ w1) * (x @ w3)
            return h @ w2
        B, S, D = z.shape
        E = router_w.shape[-1]
        T = B * S
        for _ in range(LOOPS):
            z_norm = _rmsnorm(z, norm_w)
            logits = z_norm @ router_w
            scores = jax.nn.softmax(logits, axis=-1)
            topk_vals, topk_idx = jax.lax.top_k(scores, TOP_K)
            topk_vals = topk_vals / (jnp.sum(topk_vals, axis=-1, keepdims=True) + EPS)
            cw = jnp.sum(jax.nn.one_hot(topk_idx, E, dtype=z.dtype) * topk_vals[..., None], axis=-2)
            flat_z = z_norm.reshape(T, D)
            flat_cw = cw.reshape(T, E)
            mixed = jnp.zeros((T, D), dtype=z.dtype)
            for e in range(E):
                mixed = mixed + flat_cw[:, e:e + 1] * _swiglu(flat_z, w1[e], w3[e], w2[e])
            z = z + mixed.reshape(B, S, D)
        return z
    h = _L0_tok_ref(x, L0_tok_W_proj, L0_tok_b_proj, L0_tok_pos_emb)
    h = h + _L0_attn_ref(_layernorm(h, axis=-1), L0_attn_Wq, L0_attn_Wk, L0_attn_Wv, L0_attn_Wb, L0_attn_Wa, L0_attn_Wo, L0_attn_ln1_w, L0_attn_ln1_b, L0_attn_ln2_w, L0_attn_ln2_b, L0_attn_W1, L0_attn_b1, L0_attn_W2, L0_attn_b2)
    h = h + _L0_ffn_ref(_layernorm(h, axis=-1), L0_ffn_norm_w, L0_ffn_router_w, L0_ffn_w1, L0_ffn_w3, L0_ffn_w2)
    return h

_drawn_inputs = setup_inputs


def setup_inputs(seed=0):
    import zlib

    import numpy as np

    out = dict(_drawn_inputs(seed))
    spreads = {'L0_attn_ln1_w': (1.0, 0.6),
     'L0_attn_ln1_b': (0.0, 0.8),
     'L0_attn_ln2_w': (1.0, 0.6),
     'L0_attn_ln2_b': (0.0, 0.8),
     'L0_attn_b1': (0.0, 0.453),
     'L0_attn_b2': (0.0, 0.1),
     'L0_ffn_norm_w': (1.0, 0.6)}
    factors = {'L0_tok_b_proj': 2.764,
     'L0_tok_pos_emb': 2.834,
     'L0_attn_Wq': 8.0,
     'L0_attn_Wk': 8.0,
     'L0_attn_Wv': 8.0,
     'L0_attn_Wb': 8.0,
     'L0_attn_Wa': 8.0,
     'L0_attn_Wo': 8.0,
     'L0_ffn_router_w': 5.207,
     'L0_ffn_w1': 4.558,
     'L0_ffn_w3': 4.502,
     'L0_ffn_w2': 4.504}
    for name, (base, spread) in spreads.items():
        noise = np.random.default_rng([zlib.crc32(name.encode()), seed]).standard_normal(out[name].shape)
        drawn = base * np.exp(spread * noise) if base else spread * noise
        out[name] = jnp.asarray(drawn.astype(out[name].dtype))
    for name, factor in factors.items():
        out[name] = (out[name] * factor).astype(out[name].dtype)
    return out
```

```python
from contextlib import ExitStack

import concourse.bass as bass
from concourse import mybir

ALU = mybir.AluOpType
ACT = mybir.ActivationFunctionType
F32 = mybir.dt.float32
F16 = mybir.dt.float16
AX_X = mybir.AxisListType.X

IMAGES = 64
SEQ = 36
D = 256
PATCH = 768
H, DK = 8, 128
F = 1024
E, FE = 8, 512
UNIT_IMAGES = 8
UNITS = IMAGES // UNIT_IMAGES
UT = UNIT_IMAGES * SEQ
TPU = 3
TT = UT // TPU
TILES = UNITS * TPU
KD = D // 128
KP = PATCH // 128
BATCH_IMAGES = 128 // H
BATCHES = IMAGES // BATCH_IMAGES
GROUPS = [(0, 3), (3, 3), (6, 2)]
EPS = 1e-5
LOOPS = 2
L2_EPS = 1e-6
WS = 64.0
OS = 16.0
QS = 256.0


class Chain:

    def __init__(self, engine, sem, per_turn=0):
        self.engine, self.sem, self.per_turn, self.n = engine, sem, per_turn, 0
        self.base = 0

    def turn(self, base):
        self.base, self.n = base, 0

    def link(self, ins):
        self.n += 1
        ins.then_inc(self.sem, 1)
        self.engine.wait_ge(self.sem, self.base + self.n)


def settle(engine, sem):
    engine.wait_ge(sem, 0)


def passes(hi_a, lo_a, hi_b, lo_b):
    return [(hi_a, hi_b), (lo_a, hi_b), (hi_a, lo_b)]


def load_weights(nc, ctx, m, jobs):
    with ExitStack() as own:
        stage = [own.enter_context(nc.sbuf_tensor(f"w{m.round}_stage{i}", [128, 2048], F32)) for i in range(2)]
        loaded = [own.enter_context(nc.semaphore(f"w{m.round}_loaded{i}")) for i in range(2)]
        hi_done = own.enter_context(nc.semaphore(f"w{m.round}_hi_done"))
        lo_done = own.enter_context(nc.semaphore(f"w{m.round}_lo_done"))
        consts = own.enter_context(nc.semaphore(f"w{m.round}_consts"))
        pieces = []
        for src, hi, lo, n in jobs:
            for a in range(0, n, 2048):
                b = min(n, a + 2048)
                pieces.append((src[:, a:b], hi[:, a:b], lo[:, a:b], b - a))
        block = own.enter_context(nc.Block())

        @block.sync
        def _(sp):
            for t, (src, _, _, n) in enumerate(pieces):
                if t >= 2:
                    sp.wait_ge(lo_done, t - 1)
                sp.dma_start(stage[t % 2][:, 0:n], src).then_inc(loaded[t % 2], 16)
            for dst, src in m.plain:
                sp.dma_start(dst, src).then_inc(consts, 16)
            sp.wait_ge(consts, 16 * len(m.plain))

        @block.scalar
        def _(act):
            for t, (_, hi, _, n) in enumerate(pieces):
                act.wait_ge(loaded[t % 2], 16 * (t // 2 + 1))
                nc.scalar.activation(hi, stage[t % 2][:, 0:n], ACT.Copy, scale=WS).then_inc(hi_done, 1)

        @block.vector
        def _(dve):
            for t, (_, hi, lo, n) in enumerate(pieces):
                dve.wait_ge(hi_done, t + 1)
                nc.vector.scalar_tensor_tensor(lo, stage[t % 2][:, 0:n], WS, hi, ALU.mult, ALU.subtract).then_inc(lo_done, 1)
            dve.wait_ge(lo_done, len(pieces))

        if not m.first:
            @block.gpsimd
            def _(pool):
                zeroed, filled = (own.enter_context(nc.semaphore(n)) for n in ("w_zeroed", "w_filled"))
                zeros = own.enter_context(nc.sbuf_tensor("w_zeros", [128, D], F32))
                nc.gpsimd.memset(zeros[:], 0.0).then_inc(zeroed, 1)
                pool.wait_ge(zeroed, 1)
                slots = m.x_slots.rearrange("(q p) d -> q p d", p=128)
                with nc.gpsimd.Fori(0, SLOT_TILES) as q:
                    nc.gpsimd.dma_start(slots[q], zeros[:]).then_inc(filled, 16)
                pool.wait_ge(filled, 16 * SLOT_TILES)
                route_constants(nc, pool, m, own.enter_context(nc.semaphore(f"w{m.round}_route")))
        else:
            @block.gpsimd
            def _(pool):
                made = own.enter_context(nc.semaphore(f"w{m.round}_made"))
                nc.gpsimd.memset(m.ident[:], 0.0).then_inc(made, 1)
                nc.gpsimd.memset(m.later[:], 1.0).then_inc(made, 1)
                nc.gpsimd.memset(m.same[:], 0.0).then_inc(made, 1)
                nc.gpsimd.memset(m.head_ones[:], 0.0).then_inc(made, 1)
                nc.gpsimd.memset(m.minus_half[:], -0.5).then_inc(made, 1)
                pool.wait_ge(made, 5)
                nc.gpsimd.affine_select(out=m.ident[:], in_=m.ident[:], compare_op=ALU.not_equal, fill=1.0,
                                        base=0, pattern=[[-1, 128]], channel_multiplier=1).then_inc(made, 1)
                nc.gpsimd.affine_select(out=m.later[:], in_=m.later[:], compare_op=ALU.is_gt, fill=0.0,
                                        base=0, pattern=[[-1, SEQ], [1, SEQ]], channel_multiplier=0).then_inc(made, 1)
                nc.gpsimd.affine_select(out=m.same[:], in_=m.same[:], compare_op=ALU.not_equal, fill=1.0,
                                        base=0, pattern=[[-1, SEQ], [1, SEQ]], channel_multiplier=0).then_inc(made, 1)
                nc.gpsimd.affine_select(out=m.head_ones[:], in_=m.head_ones[:], compare_op=ALU.not_equal, fill=1.0,
                                        base=0, pattern=[[-1, H], [1, H]], channel_multiplier=0).then_inc(made, 1)
                pool.wait_ge(made, 9)
                for g in range(3):
                    nc.gpsimd.memset(m.wbd[g][:], 0.0).then_inc(made, 1)
                for p in range(2):
                    nc.gpsimd.memset(m.qk_hi[p][:], 0.0).then_inc(made, 1)
                    nc.gpsimd.memset(m.qk_lo[p][:], 0.0).then_inc(made, 1)
                pool.wait_ge(made, 16)


def route_constants(nc, pool, m, made):
    nc.gpsimd.memset(m.earlier[:], 1.0).then_inc(made, 1)
    nc.gpsimd.memset(m.all_ones[:], 1.0).then_inc(made, 1)
    nc.gpsimd.memset(m.not_first[:], 1.0).then_inc(made, 1)
    nc.gpsimd.memset(m.ones_row[:], 1.0).then_inc(made, 1)
    exact = dict(allow_small_or_imprecise_dtypes=True)
    nc.gpsimd.iota(m.expert_no[:], [[1, E]], base=0, channel_multiplier=0, **exact).then_inc(made, 1)
    nc.gpsimd.iota(m.by128[:], [[128, IMAGES * SEQ // 128]], base=0, channel_multiplier=0, **exact).then_inc(made, 1)
    nc.gpsimd.iota(m.tile_no[:], [[1, SLOT_TILES]], base=0, channel_multiplier=0, **exact).then_inc(made, 1)
    pool.wait_ge(made, 7)
    nc.gpsimd.affine_select(out=m.earlier[:], in_=m.earlier[:], compare_op=ALU.is_gt, fill=0.0, base=0,
                            pattern=[[1, TT]], channel_multiplier=-1).then_inc(made, 1)
    nc.gpsimd.affine_select(out=m.not_first[:], in_=m.not_first[:], compare_op=ALU.is_gt, fill=0.0, base=0,
                            pattern=[[0, E], [1, TILES]], channel_multiplier=0).then_inc(made, 1)
    pool.wait_ge(made, 9)


def normalise(nc, dve, chain, m, src, dst, turn, k):
    nc.vector.memset(m.carry[:], 0.0)
    for j in range(TPU):
        ins = nc.vector.bn_stats(m.stats[:, j, :], src(j))
    chain.link(ins)
    nc.vector.memset(m.carry[:], 0.0)
    for j in range(TPU):
        ins = nc.vector.bn_aggr(m.mv[:, j, :], m.stats[:, j, :])
    chain.link(ins)
    nc.vector.tensor_scalar(m.vareps[:], m.mv[:, :, 1], EPS, None, ALU.add).then_inc(m.var_ready, 1)
    dve.wait_ge(m.root_ready, turn * m.roots_per_turn + k)
    for j in range(TPU):
        ins = nc.vector.tensor_scalar(dst(j), src(j), m.mv[:, j, 0:1], m.rstd[:, j:j + 1], ALU.subtract, ALU.mult)
    chain.link(ins)


def roots(nc, pool, m, turns, per_turn):
    with nc.gpsimd.Fori(0, turns) as u:
        for k in range(per_turn):
            pool.wait_ge(m.var_ready, u * per_turn + (k + 1))
            nc.gpsimd.tensor_tensor(m.rstd[0:TT, :], m.vareps[0:TT, :], m.minus_half[0:TT, 0:TPU],
                                    ALU.pow).then_inc(m.root_ready, 1)


def phase_tokens(nc, m):
    with ExitStack() as own:
        def sem(name):
            return own.enter_context(nc.semaphore(f"t{m.round}_" + name))

        def sb(name, shape, dt):
            return own.enter_context(nc.sbuf_tensor(f"t{m.round}_" + name, shape, dt))

        x_loaded, x_hi, x_lo = sem("x_loaded"), sem("x_hi"), sem("x_lo")
        tok_ready, tok_taken = sem("tok_ready"), sem("tok_taken")
        m.var_ready, m.root_ready = sem("var_ready"), sem("root_ready")
        n_ready, nt_ready, nt_hi, nt_lo, order = sem("n_ready"), sem("nt_ready"), sem("nt_hi"), sem("nt_lo"), sem("order")
        xin = sb("xin", [128, KP, UT], F32)
        xh, xl = sb("xh", [128, KP, UT], F16), sb("xl", [128, KP, UT], F16)
        n_tok = sb("n_tok", [TT, TPU, D], F32)
        tok_ps = m.ps[0:TT, 0:2, :].rearrange("p b n -> p (b n)")[:, 0:TPU * D]
        nt_ps = m.ps[:, 4:6, 0:UT]
        LINKS = 8
        m.roots_per_turn = 2
        block = own.enter_context(nc.Block())

        @block.sync
        def _(sp):
            sp.dma_start(xin[:], m.x[0]).then_inc(x_loaded, 16)
            with nc.sync.Fori(1, UNITS) as u:
                sp.wait_ge(x_hi, u)
                sp.wait_ge(x_lo, u)
                settle(sp, x_lo)
                sp.dma_start(xin[:], m.x[u]).then_inc(x_loaded, 16)

        @block.scalar
        def _(act):
            def split_x(u):
                act.wait_ge(x_loaded, 16 * u + 16)
                act.wait_ge(tok_ready, u)
                nc.scalar.activation(xh[:], xin[:], ACT.Copy).then_inc(x_hi, 1)

            def split_nt(u):
                act.wait_ge(nt_ready, u + 1)
                nc.scalar.activation(m.nt_hi[:, u, :, :], nt_ps, ACT.Copy).then_inc(nt_hi, 1)

            split_x(0)
            with nc.scalar.Fori(0, UNITS - 1) as u:
                split_x(u + 1)
                split_nt(u)
            split_nt(UNITS - 1)

        @block.gpsimd
        def _(pool):
            roots(nc, pool, m, UNITS, 2)

        @block.tensor
        def _(pe):
            def project(u):
                pe.wait_ge(x_hi, u + 1)
                pe.wait_ge(x_lo, u + 1)
                pe.wait_ge(tok_taken, u)
                for j in range(TPU):
                    terms = [t for k in range(KP) for t in passes(
                        xh[:, k, j * TT:(j + 1) * TT], xl[:, k, j * TT:(j + 1) * TT],
                        m.wp_hi[:, k * D:(k + 1) * D], m.wp_lo[:, k * D:(k + 1) * D])]
                    for i, (a, b) in enumerate(terms):
                        last = nc.tensor.matmul(tok_ps[:, j * D:(j + 1) * D], a, b, start=(i == 0), stop=(i == len(terms) - 1))
                last.then_inc(tok_ready, 1)

            def turn_over(u):
                pe.wait_ge(n_ready, u + 1)
                pe.wait_ge(nt_hi, u)
                pe.wait_ge(nt_lo, u)
                for k in range(KD):
                    for j in range(TPU):
                        last = nc.tensor.transpose(nt_ps[:, k, j * TT:(j + 1) * TT], n_tok[:, j, k * 128:(k + 1) * 128],
                                                   m.ident[0:TT, 0:TT])
                last.then_inc(nt_ready, 1)

            project(0)
            with nc.tensor.Fori(0, UNITS - 1) as u:
                project(u + 1)
                turn_over(u)
            turn_over(UNITS - 1)

        @block.vector
        def _(dve):
            chain = Chain(dve, order)

            def split_x(u):
                dve.wait_ge(x_hi, u + 1)
                dve.wait_ge(tok_ready, u)
                nc.vector.tensor_tensor(xl[:], xin[:], xh[:], ALU.subtract).then_inc(x_lo, 1)

            def norms(u):
                chain.turn(u * LINKS)
                dve.wait_ge(tok_ready, u + 1)
                nc.vector.scalar_tensor_tensor(m.h[:, u, :], tok_ps, 1.0 / WS, m.pos[:], ALU.mult, ALU.add).then_inc(tok_taken, 1)
                dve.wait_ge(tok_taken, u + 1)
                hv = lambda j: m.h[:, u, j * D:(j + 1) * D]
                nv = lambda j: m.n1[:, u, j * D:(j + 1) * D]
                chain.link(nc.vector.tensor_tensor(m.h[:, u, :], m.h[:, u, :], m.bproj[:], ALU.add))
                normalise(nc, dve, chain, m, hv, nv, u, 1)
                dve.wait_ge(nt_ready, u)
                normalise(nc, dve, chain, m, nv, lambda j: n_tok[:, j, :], u, 2)
                for j in range(TPU):
                    ins = nc.vector.tensor_tensor(n_tok[:, j, :], n_tok[:, j, :], m.ln1_w[:], ALU.mult)
                chain.link(ins)
                for j in range(TPU):
                    ins = nc.vector.tensor_tensor(n_tok[:, j, :], n_tok[:, j, :], m.ln1_b[:], ALU.add)
                ins.then_inc(n_ready, 1)
                assert chain.n == LINKS, chain.n

            def split_nt(u):
                dve.wait_ge(nt_hi, u + 1)
                nc.vector.tensor_tensor(m.nt_lo[:, u, :, :], nt_ps, m.nt_hi[:, u, :, :], ALU.subtract).then_inc(nt_lo, 1)

            split_x(0)
            with nc.vector.Fori(0, UNITS - 1) as u:
                split_x(u + 1)
                norms(u)
                split_nt(u)
            norms(UNITS - 1)
            split_nt(UNITS - 1)


def phase_grams(nc, m):
    with ExitStack() as own:
        def sem(name):
            return own.enter_context(nc.semaphore(f"g{m.round}_" + name))

        def sb(name, shape, dt):
            return own.enter_context(nc.sbuf_tensor(f"g{m.round}_" + name, shape, dt))

        qk_ready, qk_act, qk_hi, qk_lo, sq_ready = sem("qk_ready"), sem("qk_act"), sem("qk_hi"), sem("qk_lo"), sem("sq_ready")
        sq_used, gram_ready, gram_taken = sem("sq_used"), sem("gram_ready"), sem("gram_taken")
        stored = [sem("stored0"), sem("stored1")]
        small_ready, small_taken, small_stored = sem("small_ready"), sem("small_taken"), sem("small_stored")
        qks = [sb(f"qks{p}", [128, 2, UT], F32) for p in range(2)]
        sq = [sb(f"sq{p}", [128, UT], F32) for p in range(2)]
        gsb = [sb(f"gsb{p}", [128, 4, UNIT_IMAGES // 2, 2 * SEQ], F32) for p in range(2)]
        qn_sb = sb("qn_sb", [H, UT], F32)
        ba_sb = sb("ba_sb", [2 * H, UT], F32)
        PAIRS = UNIT_IMAGES // 2
        block = own.enter_context(nc.Block())

        @block.tensor
        def _(pe):
            def project(u, h):
                p = h % 2
                pe.wait_ge(qk_act, u * H + max(h - 1, 0))
                for c, (whi, wlo) in enumerate([(m.wq_hi, m.wq_lo), (m.wk_hi, m.wk_lo)]):
                    terms = [t for k in range(KD) for t in passes(
                        whi[:, k * H * DK + h * DK:k * H * DK + (h + 1) * DK],
                        wlo[:, k * H * DK + h * DK:k * H * DK + (h + 1) * DK],
                        m.nt_hi[:, u, k, :], m.nt_lo[:, u, k, :])]
                    for i, (a, b) in enumerate(terms):
                        last = nc.tensor.matmul(m.ps[:, 2 * p + c, 0:UT], a, b, start=(i == 0), stop=(i == len(terms) - 1))
                last.then_inc(qk_ready, 1)

            def gram(u, h):
                p = h % 2
                qh, ql = m.qk_hi[p], m.qk_lo[p]
                pe.wait_ge(qk_hi, u * H + h + 1)
                pe.wait_ge(qk_lo, u * H + h + 1)
                pe.wait_ge(gram_taken, u * H + max(h - 1, 0))
                for i in range(UNIT_IMAGES):
                    out = m.ps[64 * (i % 2):64 * (i % 2) + 64, 4 + p, (i // 2) * 72:(i // 2) * 72 + 72]
                    k0 = UT + i * SEQ
                    kh, kl = qh[:, k0:k0 + 64], ql[:, k0:k0 + 64]
                    rh = qh[:, 0:2 * UT].rearrange("p (c t) -> p c t", c=2)[:, :, i * SEQ:(i + 1) * SEQ]
                    rl = ql[:, 0:2 * UT].rearrange("p (c t) -> p c t", c=2)[:, :, i * SEQ:(i + 1) * SEQ]
                    for n, (a, b) in enumerate(passes(kh, kl, rh, rl)):
                        last = nc.tensor.matmul(out, a, b, start=(n == 0), stop=(n == 2))
                last.then_inc(gram_ready, 1)
                pe.wait_ge(sq_ready, u * H + h + 1)
                nc.tensor.matmul(m.ps[0:H, 6, 0:UT], m.head_ones[:, h, :], sq[p][:], start=(h == 0),
                                 stop=(h == H - 1)).then_inc(sq_used, 1)

            with nc.tensor.Fori(0, UNITS) as u:
                pe.wait_ge(small_taken, 2 * u)
                terms = [t for k in range(KD) for t in passes(
                    m.wba_hi[:, k * 16:(k + 1) * 16], m.wba_lo[:, k * 16:(k + 1) * 16],
                    m.nt_hi[:, u, k, :], m.nt_lo[:, u, k, :])]
                for i, (a, b) in enumerate(terms):
                    last = nc.tensor.matmul(m.ps[0:2 * H, 7, 0:UT], a, b, start=(i == 0), stop=(i == len(terms) - 1))
                last.then_inc(small_ready, 1)
                project(u, 0)
                for h in range(1, H):
                    project(u, h)
                    gram(u, h - 1)
                gram(u, H - 1)

        @block.scalar
        def _(act):
            with nc.scalar.Fori(0, UNITS) as u:
                for h in range(H):
                    p = h % 2
                    act.wait_ge(qk_ready, u * H + h + 1)
                    act.wait_ge(qk_lo, u * H + max(h - 1, 0))
                    act.wait_ge(sq_ready, u * H + max(h - 1, 0))
                    nc.scalar.activation(qks[p][:], m.ps[:, 2 * p:2 * p + 2, 0:UT], ACT.Silu, scale=1.0 / WS).then_inc(qk_act, 1)
                    act.wait_ge(qk_act, u * H + h + 1)
                    act.wait_ge(gram_ready, u * H + max(h - 1, 0))
                    nc.scalar.activation(m.qk_hi[p][:, 0:2 * UT].rearrange("p (c t) -> p c t", c=2), qks[p][:], ACT.Copy).then_inc(qk_hi, 1)

        @block.gpsimd
        def _(pool):
            with nc.gpsimd.Fori(0, UNITS) as u:
                for h in range(H):
                    pool.wait_ge(qk_act, u * H + h + 1)
                    pool.wait_ge(sq_used, u * H + max(h - 1, 0))
                    nc.gpsimd.tensor_tensor(sq[h % 2][:], qks[h % 2][:, 0, :], qks[h % 2][:, 0, :], ALU.mult).then_inc(sq_ready, 1)

        @block.vector
        def _(dve):
            def low(u, h):
                p = h % 2
                dve.wait_ge(qk_hi, u * H + h + 1)
                dve.wait_ge(gram_ready, u * H + max(h - 1, 0))
                nc.vector.tensor_tensor(m.qk_lo[p][:, 0:2 * UT].rearrange("p (c t) -> p c t", c=2), qks[p][:],
                                        m.qk_hi[p][:, 0:2 * UT].rearrange("p (c t) -> p c t", c=2), ALU.subtract).then_inc(qk_lo, 1)

            def take(u, h):
                if h % 4 == 0:
                    dve.wait_ge(stored[h // 4], u * 128)
                dve.wait_ge(gram_ready, u * H + h + 1)
                nc.vector.tensor_copy(gsb[h // 4][:, h % 4, :, :].rearrange("p c n -> p (c n)"),
                                      m.ps[:, 4 + h % 2, 0:PAIRS * 72]).then_inc(gram_taken, 1)

            with nc.vector.Fori(0, UNITS) as u:
                dve.wait_ge(small_ready, u + 1)
                dve.wait_ge(small_stored, u * 48)
                nc.vector.tensor_scalar(ba_sb[:], m.ps[0:2 * H, 7, 0:UT], 1.0 / WS, None, ALU.mult).then_inc(small_taken, 1)
                low(u, 0)
                for h in range(1, H):
                    low(u, h)
                    take(u, h - 1)
                take(u, H - 1)
                dve.wait_ge(sq_used, u * H + H)
                nc.vector.tensor_copy(qn_sb[:], m.ps[0:H, 6, 0:UT]).then_inc(small_taken, 1)

        @block.sync
        def _(sp):
            with nc.sync.Fori(0, UNITS) as u:
                sp.wait_ge(small_taken, 2 * u + 1)
                settle(sp, small_taken)
                for c, dst in enumerate([m.beta_d, m.alpha_d]):
                    sp.dma_start(dst[u].rearrange("i h t -> h i t"),
                                 ba_sb[c * H:(c + 1) * H, :].rearrange("h (i t) -> h i t", t=SEQ)).then_inc(small_stored, 16)
                for b in range(2):
                    sp.wait_ge(gram_taken, u * H + 4 * b + 4)
                    settle(sp, gram_taken)
                    for par in range(2):
                        dst = m.gram_d[u].rearrange("(c par) h s n -> par h s c n", par=2)
                        for hh in range(4):
                            sp.dma_start(dst[par, 4 * b + hh], gsb[b][64 * par:64 * par + SEQ, hh, :, :]).then_inc(stored[b], 16)
                sp.wait_ge(small_taken, 2 * u + 2)
                settle(sp, small_taken)
                sp.dma_start(m.qn_d[u].rearrange("i h t -> h i t"),
                             qn_sb[:].rearrange("h (i t) -> h i t", t=SEQ)).then_inc(small_stored, 16)
            sp.wait_ge(small_stored, 48 * UNITS)
            for b in range(2):
                sp.wait_ge(stored[b], 128 * UNITS)


def phase_solve(nc, m):
    with ExitStack() as own:
        def sem(name):
            return own.enter_context(nc.semaphore(f"s{m.round}_" + name))

        def sb(name, shape, dt):
            return own.enter_context(nc.sbuf_tensor(f"s{m.round}_" + name, shape, dt))

        loaded, gates, sums, inv, order = sem("loaded"), sem("gates"), sem("sums"), sem("inv"), sem("order")
        mixed, w_stored = sem("mixed"), sem("w_stored")
        NN = SEQ * SEQ
        gram = sb("gram", [128, SEQ, 2 * SEQ], F32)
        logit = sb("logit", [128, 2, SEQ], F32)
        gate = sb("gate", [128, 2, SEQ], F32)
        qn = sb("qn", [128, SEQ], F32)
        sq = sb("sq", [128, 2, SEQ], F32)
        rk = sb("rk", [128, 2, SEQ], F32)
        c = sb("c", [128, SEQ], F32)
        d0, d1, e = sb("d0", [128, SEQ, SEQ], F32), sb("d1", [128, SEQ, SEQ], F32), sb("e", [128, SEQ, SEQ], F32)
        at, wt = sb("at", [128, SEQ, SEQ], F32), sb("wt", [128, SEQ, SEQ], F32)
        tmp = [sb(f"tmp{i}", [128, NN // 3], F32) for i in range(3)]
        red = [sb(f"red{i}", [128, SEQ], F32) for i in range(3)]
        wo = sb("wo", [128, SEQ, 2 * SEQ], F16)
        mh = sb("mh", [128, 2 * SEQ], F32)
        THIRD = SEQ // 3
        LINKS = 10 + 3 * (SEQ - 1)
        block = own.enter_context(nc.Block())

        @block.scalar
        def _(act):
            with nc.scalar.Fori(0, BATCHES) as b:
                act.wait_ge(mixed, b)
                act.dma_start(gram[:], m.gram_b[b]).then_inc(loaded, 16)
                act.dma_start(logit[:, 0, :], m.beta_b[b]).then_inc(loaded, 16)
                act.dma_start(logit[:, 1, :], m.alpha_b[b]).then_inc(loaded, 16)
                act.dma_start(qn[:], m.qn_b[b]).then_inc(loaded, 16)
                act.wait_ge(loaded, 64 * b + 64)
                nc.scalar.activation(gate[:], logit[:], ACT.Sigmoid).then_inc(gates, 1)
                act.wait_ge(mixed, b + 1)
                act.dma_start(m.w_b[b], wo[:]).then_inc(w_stored, 16)
            act.wait_ge(w_stored, 16 * BATCHES)

        @block.gpsimd
        def _(pool):
            nc.gpsimd.memset(mh[:], -0.5).then_inc(inv, 1)
            pool.wait_ge(inv, 1)
            with nc.gpsimd.Fori(0, BATCHES) as b:
                pool.wait_ge(sums, b + 1)
                nc.gpsimd.tensor_tensor(rk[:].rearrange("p c t -> p (c t)"), sq[:].rearrange("p c t -> p (c t)"), mh[:],
                                        ALU.pow).then_inc(inv, 1)

        @block.vector
        def _(dve):
            chain = Chain(dve, order)
            flat = lambda a: a.rearrange("p s t -> p (s t)")
            with nc.vector.Fori(0, BATCHES) as b:
                chain.turn(b * LINKS)
                dve.wait_ge(loaded, 64 * b + 64)
                diag = flat(gram[:])[:, SEQ:SEQ + (SEQ - 1) * (2 * SEQ + 1) + 1:2 * SEQ + 1]
                chain.link(nc.vector.tensor_scalar(sq[:, 0, :], diag, L2_EPS, None, ALU.add))
                nc.vector.tensor_scalar(sq[:, 1, :], qn[:], L2_EPS, None, ALU.add).then_inc(sums, 1)
                dve.wait_ge(gates, b + 1)
                chain.link(nc.vector.tensor_tensor(d0[:], m.later[:], gate[:, 1, :].unsqueeze(1).to_broadcast([128, SEQ, SEQ]), ALU.mult))
                dve.wait_ge(inv, b + 2)
                chain.link(nc.vector.tensor_tensor(c[:], gate[:, 0, :], rk[:, 0, :], ALU.mult))
                chain.link(nc.vector.tensor_tensor(d1[:], m.same[:], c[:].unsqueeze(2).to_broadcast([128, SEQ, SEQ]), ALU.mult))
                chain.link(nc.vector.tensor_tensor_scan(flat(e[:]), flat(d0[:]), flat(d1[:]), 0.0, ALU.mult, ALU.add))
                chain.link(nc.vector.tensor_tensor(at[:], e[:], gram[:, :, SEQ:2 * SEQ], ALU.mult))
                chain.link(nc.vector.tensor_tensor(at[:], at[:], rk[:, 0, :].unsqueeze(1).to_broadcast([128, SEQ, SEQ]), ALU.mult))
                chain.link(nc.vector.tensor_tensor(wt[:], e[:], gram[:, :, 0:SEQ], ALU.mult))
                chain.link(nc.vector.tensor_tensor(wt[:], wt[:], rk[:, 1, :].unsqueeze(1).to_broadcast([128, SEQ, SEQ]), ALU.mult))
                for s in range(SEQ - 2, -1, -1):
                    blocks = [(i, max(s + 1, THIRD * i), THIRD * (i + 1)) for i in range(3) if s + 1 < THIRD * (i + 1)]
                    for i, lo, hi in blocks:
                        n, r = hi - lo, hi - (s + 1)
                        prod = tmp[i][:, 0:n * r].rearrange("p (t r) -> p t r", r=r)
                        ins = (nc.vector.tensor_tensor(prod, wt[:, s + 1:hi, lo:hi].rearrange("p r t -> p t r"),
                                                           at[:, s, s + 1:hi].unsqueeze(1).to_broadcast([128, n, r]), ALU.mult))
                    chain.link(ins)
                    for i, lo, hi in blocks:
                        n, r = hi - lo, hi - (s + 1)
                        ins = (nc.vector.tensor_reduce(red[i][:, 0:n], tmp[i][:, 0:n * r].rearrange("p (t r) -> p t r", r=r),
                                                           AX_X, ALU.add))
                    chain.link(ins)
                    for i, lo, hi in blocks:
                        ins = (nc.vector.tensor_tensor(wt[:, s, lo:hi], wt[:, s, lo:hi], red[i][:, 0:hi - lo], ALU.subtract))
                    chain.link(ins)
                dve.wait_ge(w_stored, 16 * b)
                chain.link(nc.vector.tensor_scalar(wo[:, :, 0:SEQ], wt[:], QS, None, ALU.mult))
                nc.vector.scalar_tensor_tensor(wo[:, :, SEQ:2 * SEQ], wt[:], QS, wo[:, :, 0:SEQ], ALU.mult, ALU.subtract).then_inc(mixed, 1)
                assert chain.n == LINKS, chain.n


def phase_mix(nc, m):
    with ExitStack() as own:
        def sem(name):
            return own.enter_context(nc.semaphore(f"m{m.round}_" + name))

        def sb(name, shape, dt):
            return own.enter_context(nc.sbuf_tensor(f"m{m.round}_" + name, shape, dt))

        w_loaded, v_ready, v_act, v_hi, v_lo = sem("w_loaded"), sem("v_ready"), sem("v_act"), sem("v_hi"), sem("v_lo")
        o_ready, o_hi, o_lo = sem("o_ready"), sem("o_hi"), sem("o_lo")
        wo_ready, x2_taken, n_ready, nt_ready, nt_hi, nt_lo = (sem("wo_ready"), sem("x2_taken"), sem("n_ready"),
                                                                sem("nt_ready"), sem("nt_hi"), sem("nt_lo"))
        a_ready, a_act, a_hi, a_lo, y_ready, order = sem("a_ready"), sem("a_act"), sem("a_hi"), sem("a_lo"), sem("y_ready"), sem("order")
        y_taken = sem("y_taken")
        m.var_ready, m.root_ready = sem("var_ready"), sem("root_ready")
        m.roots_per_turn = 2
        vs = sb("vs", [128, 2, 512], F32)
        v_h = [sb(f"v_h{g}", [128, 1024], F16) for g in range(3)]
        v_l = [sb(f"v_l{g}", [128, 1024], F16) for g in range(3)]
        ot_h, ot_l = sb("ot_h", [128, H, UT], F16), sb("ot_l", [128, H, UT], F16)
        x2 = sb("x2", [TT, TPU * D], F32)
        n_tok = sb("n_tok", [TT, TPU, D], F32)
        ht_h, ht_l = sb("ht_h", [128, KD, UT], F16), sb("ht_l", [128, KD, UT], F16)
        a_s = [sb(f"a_s{p}", [128, UT], F32) for p in range(2)]
        at_h, at_l = sb("at_h", [128, F // 128, UT], F16), sb("at_l", [128, F // 128, UT], F16)
        tok_ps = m.ps[0:TT, 4:6, :].rearrange("p b n -> p (b n)")[:, 0:TPU * D]
        nt_ps = m.ps[:, 6:8, 0:UT]
        FC = F // 128
        VH = len(GROUPS) * 2
        LINKS = 9
        block = own.enter_context(nc.Block())

        @block.sync
        def _(sp):
            with nc.sync.Fori(0, UNITS) as u:
                sp.wait_ge(o_ready, H * u)
                settle(sp, o_ready)
                for g, (i0, n) in enumerate(GROUPS):
                    for j in range(n):
                        sp.dma_start(m.wbd[g][SEQ * j:SEQ * (j + 1), :, j, :],
                                     m.w_d[u, i0 + j].rearrange("h s n -> s h n")).then_inc(w_loaded, 16)

        @block.gpsimd
        def _(pool):
            roots(nc, pool, m, UNITS, 2)

        @block.tensor
        def _(pe):
            def values(u):
                for g, (i0, n) in enumerate(GROUPS):
                    rows = n * SEQ
                    for half in range(2):
                        t = 2 * g + half
                        pe.wait_ge(v_act, u * VH + max(t - 1, 0))
                        terms = [x for k in range(KD) for x in passes(
                            m.nt_hi[:, u, k, i0 * SEQ:i0 * SEQ + rows], m.nt_lo[:, u, k, i0 * SEQ:i0 * SEQ + rows],
                            m.wv_hi[:, k * 1024 + half * 512:k * 1024 + half * 512 + 512],
                            m.wv_lo[:, k * 1024 + half * 512:k * 1024 + half * 512 + 512])]
                        for i, (a, b) in enumerate(terms):
                            last = nc.tensor.matmul(m.ps[0:rows, half, :], a, b, start=(i == 0), stop=(i == len(terms) - 1))
                        last.then_inc(v_ready, 1)

            def mix(u, fed):
                pe.wait_ge(w_loaded, 128 * u + 128)
                pe.wait_ge(v_hi, u * VH + VH)
                pe.wait_ge(v_lo, u * VH + VH)
                pe.wait_ge(a_act, fed * FC)
                for h in range(H):
                    pe.wait_ge(o_lo, u * H + max(h - 1, 0))
                    pe.wait_ge(o_hi, u * H + max(h - 1, 0))
                    for g, (i0, n) in enumerate(GROUPS):
                        rows = n * SEQ
                        out = m.ps[:, 2 + h % 2, i0 * SEQ:i0 * SEQ + rows]
                        w = m.wbd[g][0:rows, h, 0:n, :]
                        for i, (a, b) in enumerate(passes(v_h[g][0:rows, h * DK:(h + 1) * DK], v_l[g][0:rows, h * DK:(h + 1) * DK],
                                                          w[:, :, 0:SEQ], w[:, :, SEQ:2 * SEQ])):
                            last = nc.tensor.matmul(out, a, b, start=(i == 0), stop=(i == 2))
                    last.then_inc(o_ready, 1)

            def out_project(u):
                pe.wait_ge(o_hi, u * H + H)
                pe.wait_ge(o_lo, u * H + H)
                pe.wait_ge(y_taken, u)
                for j in range(TPU):
                    terms = [x for h in range(H) for x in passes(
                        ot_h[:, h, j * TT:(j + 1) * TT], ot_l[:, h, j * TT:(j + 1) * TT],
                        m.wo_hi[:, h * D:(h + 1) * D], m.wo_lo[:, h * D:(h + 1) * D])]
                    for i, (a, b) in enumerate(terms):
                        last = nc.tensor.matmul(tok_ps[:, j * D:(j + 1) * D], a, b, start=(i == 0), stop=(i == len(terms) - 1))
                last.then_inc(wo_ready, 1)

            def feed(u, mixed):
                pe.wait_ge(n_ready, u + 1)
                pe.wait_ge(nt_hi, u)
                pe.wait_ge(nt_lo, u)
                for k in range(KD):
                    for j in range(TPU):
                        last = nc.tensor.transpose(nt_ps[:, k, j * TT:(j + 1) * TT], n_tok[:, j, k * 128:(k + 1) * 128],
                                                   m.ident[0:TT, 0:TT])
                last.then_inc(nt_ready, 1)
                pe.wait_ge(nt_hi, u + 1)
                pe.wait_ge(nt_lo, u + 1)
                for f in range(FC):
                    if f == 0:
                        pe.wait_ge(o_hi, mixed * H)
                        pe.wait_ge(o_lo, mixed * H)
                    pe.wait_ge(a_act, u * FC + max(f - 1, 0))
                    terms = [x for k in range(KD) for x in passes(
                        m.w1_hi[:, k * F + f * 128:k * F + f * 128 + 128], m.w1_lo[:, k * F + f * 128:k * F + f * 128 + 128],
                        ht_h[:, k, :], ht_l[:, k, :])]
                    for i, (a, b) in enumerate(terms):
                        last = nc.tensor.matmul(m.ps[:, 2 + f % 2, 0:UT], a, b, start=(i == 0), stop=(i == len(terms) - 1))
                    last.then_inc(a_ready, 1)
                pe.wait_ge(a_hi, u * FC + FC)
                pe.wait_ge(a_lo, u * FC + FC)
                pe.wait_ge(x2_taken, u + 1)
                for j in range(TPU):
                    terms = [x for f in range(FC) for x in passes(
                        at_h[:, f, j * TT:(j + 1) * TT], at_l[:, f, j * TT:(j + 1) * TT],
                        m.w2_hi[:, f * D:(f + 1) * D], m.w2_lo[:, f * D:(f + 1) * D])]
                    for i, (a, b) in enumerate(terms):
                        last = nc.tensor.matmul(tok_ps[:, j * D:(j + 1) * D], a, b, start=(i == 0), stop=(i == len(terms) - 1))
                last.then_inc(y_ready, 1)

            values(0)
            mix(0, 0)
            with nc.tensor.Fori(0, UNITS - 1) as u:
                out_project(u)
                values(u + 1)
                mix(u + 1, u)
                feed(u, u + 2)
            out_project(UNITS - 1)
            feed(UNITS - 1, UNITS)

        @block.scalar
        def _(act):
            def values(u):
                for t in range(VH):
                    g, half = t // 2, t % 2
                    rows = GROUPS[g][1] * SEQ
                    act.wait_ge(v_ready, u * VH + t + 1)
                    act.wait_ge(v_lo, u * VH + max(t - 1, 0))
                    nc.scalar.activation(vs[0:rows, half, :], m.ps[0:rows, half, :], ACT.Silu, scale=1.0 / WS).then_inc(v_act, 1)
                    act.wait_ge(v_act, u * VH + t + 1)
                    if t == 0:
                        act.wait_ge(o_ready, u * H)
                    nc.scalar.activation(v_h[g][0:rows, half * 512:half * 512 + 512], vs[0:rows, half, :], ACT.Copy).then_inc(v_hi, 1)

            def heads(u):
                act.wait_ge(wo_ready, u)
                for h in range(H):
                    act.wait_ge(o_ready, u * H + h + 1)
                    nc.scalar.activation(ot_h[:, h, :], m.ps[:, 2 + h % 2, 0:UT], ACT.Copy, scale=OS / QS).then_inc(o_hi, 1)

            def feed(u):
                act.wait_ge(nt_ready, u + 1)
                act.wait_ge(a_ready, u * FC)
                nc.scalar.activation(ht_h[:], nt_ps, ACT.Copy).then_inc(nt_hi, 1)
                act.wait_ge(y_ready, u)
                for f in range(FC):
                    act.wait_ge(a_ready, u * FC + f + 1)
                    act.wait_ge(a_lo, u * FC + max(f - 1, 0))
                    nc.scalar.activation(a_s[f % 2][:], m.ps[:, 2 + f % 2, 0:UT], ACT.Gelu, scale=1.0 / WS,
                                         bias=m.b1[:, f:f + 1]).then_inc(a_act, 1)
                    act.wait_ge(a_act, u * FC + f + 1)
                    nc.scalar.activation(at_h[:, f, :], a_s[f % 2][:], ACT.Copy).then_inc(a_hi, 1)

            values(0)
            heads(0)
            with nc.scalar.Fori(0, UNITS - 1) as u:
                values(u + 1)
                heads(u + 1)
                feed(u)
            feed(UNITS - 1)

        @block.vector
        def _(dve):
            chain = Chain(dve, order)

            def values(u):
                for t in range(VH):
                    g, half = t // 2, t % 2
                    rows = GROUPS[g][1] * SEQ
                    dve.wait_ge(v_hi, u * VH + t + 1)
                    nc.vector.tensor_tensor(v_l[g][0:rows, half * 512:half * 512 + 512], vs[0:rows, half, :],
                                            v_h[g][0:rows, half * 512:half * 512 + 512], ALU.subtract).then_inc(v_lo, 1)

            def heads(u):
                for h in range(H):
                    dve.wait_ge(o_hi, u * H + h + 1)
                    nc.vector.scalar_tensor_tensor(ot_l[:, h, :], m.ps[:, 2 + h % 2, 0:UT], OS / QS, ot_h[:, h, :],
                                                   ALU.mult, ALU.subtract).then_inc(o_lo, 1)

            def second_norm(u):
                chain.turn(u * LINKS)
                dve.wait_ge(wo_ready, u + 1)
                nc.vector.scalar_tensor_tensor(x2[:], tok_ps, 1.0 / (WS * OS), m.n1[:, u, :], ALU.mult, ALU.add).then_inc(x2_taken, 1)
                dve.wait_ge(x2_taken, u + 1)
                normalise(nc, dve, chain, m, lambda j: x2[:, j * D:(j + 1) * D], lambda j: n_tok[:, j, :], u, 1)
                for j in range(TPU):
                    ins = nc.vector.tensor_tensor(n_tok[:, j, :], n_tok[:, j, :], m.ln2_w[:], ALU.mult)
                chain.link(ins)
                for j in range(TPU):
                    ins = nc.vector.tensor_tensor(n_tok[:, j, :], n_tok[:, j, :], m.ln2_b[:], ALU.add)
                ins.then_inc(n_ready, 1)
                chain.link(nc.vector.tensor_tensor(m.h[:, u, :], m.h[:, u, :], x2[:], ALU.add))
                for j in range(TPU):
                    ins = nc.vector.tensor_tensor(m.h[:, u, j * D:(j + 1) * D], m.h[:, u, j * D:(j + 1) * D], m.b2[:], ALU.add)
                chain.link(ins)

            def feed(u):
                dve.wait_ge(nt_hi, u + 1)
                nc.vector.tensor_tensor(ht_l[:], nt_ps, ht_h[:], ALU.subtract).then_inc(nt_lo, 1)
                for f in range(FC):
                    dve.wait_ge(a_hi, u * FC + f + 1)
                    nc.vector.tensor_tensor(at_l[:, f, :], a_s[f % 2][:], at_h[:, f, :], ALU.subtract).then_inc(a_lo, 1)
                dve.wait_ge(y_ready, u + 1)
                nc.vector.scalar_tensor_tensor(m.h[:, u, :], tok_ps, 1.0 / WS, m.h[:, u, :], ALU.mult, ALU.add).then_inc(y_taken, 1)
                dve.wait_ge(y_taken, u + 1)
                normalise(nc, dve, chain, m, lambda j: m.h[:, u, j * D:(j + 1) * D],
                          lambda j: m.n1[:, u, j * D:(j + 1) * D], u, 2)
                assert chain.n == LINKS, chain.n

            values(0)
            heads(0)
            with nc.vector.Fori(0, UNITS - 1) as u:
                second_norm(u)
                values(u + 1)
                heads(u + 1)
                feed(u)
            second_norm(UNITS - 1)
            feed(UNITS - 1)


RMS_EPS = 1e-6
GATE_EPS = 1e-9
SLOT_TILES = (2 * IMAGES * SEQ + E * 127) // 128
ROWS = SLOT_TILES * 128


def phase_route(nc, m):
    with ExitStack() as own:
        def sem(name):
            return own.enter_context(nc.semaphore(f"r{m.round}_" + name))

        def sb(name, shape, dt):
            return own.enter_context(nc.sbuf_tensor(f"r{m.round}_" + name, shape, dt))

        sum_ready, root_ready, zn_ready, nt_ready, nt_hi, nt_lo = (sem("sum_ready"), sem("root_ready"), sem("zn_ready"),
                                                                     sem("nt_ready"), sem("nt_hi"), sem("nt_lo"))
        logit_ready, logit_taken, shifted, exp_ready, order = (sem("logit_ready"), sem("logit_taken"), sem("shifted"),
                                                                sem("exp_ready"), sem("order"))
        picked, counted, placed, sent = sem("picked"), sem("counted"), sem("placed"), sem("sent")
        scratch = sb("scratch", [TT, TPU, D], F32)
        ss, ssv, rms = sb("ss", [TT, TPU], F32), sb("ssv", [TT, TPU], F32), sb("rms", [TT, TPU], F32)
        zn = sb("zn", [TT, TILES, D], F32)
        stage = sb("stage", [TT, TPU, D], F32)
        zt_h, zt_l = sb("zt_h", [128, KD, UT], F16), sb("zt_l", [128, KD, UT], F16)
        logit = sb("logit", [TT, TILES, E], F32)
        top, index = sb("top", [TT, TILES, 8], F32), sb("index", [TT, TILES, 8], mybir.dt.uint32)
        ex, total, inv = sb("ex", [TT, TILES, E], F32), sb("total", [TT, TILES], F32), sb("inv", [TT, TILES], F32)
        s1, s2, den = sb("s1", [TT, TILES], F32), sb("s2", [TT, TILES], F32), sb("den", [TT, TILES], F32)
        pick = sb("pick", [TT, TILES, 2], F32)
        mask = [sb(f"mask{c}", [TT, E, TILES], F32) for c in range(2)]
        both = sb("both", [TT, E, TILES], F32)
        counts, running = sb("counts", [128, E, TILES], F32), sb("running", [128, E, TILES], F32)
        place, chosen, slot_f = sb("place", [TT, E, TILES], F32), sb("chosen", [TT, E, TILES], F32), sb("slot_f", [TT, TILES], F32)
        TPE = IMAGES * SEQ // 128
        more = sb("more", [TT, E, TPE], F32)
        tiles, upto, before = sb("tiles", [TT, E], F32), sb("upto", [TT, E], F32), sb("before", [TT, E], F32)
        past, tab = sb("past", [1, SLOT_TILES, E], F32), sb("tab", [1, SLOT_TILES], F32)
        nt_ps = m.ps[:, 0:2, 0:UT]
        log_ps = m.ps[0:TT, 2, 0:TPU * E]
        pre_ps, cnt_ps = m.ps[0:TT, 3, 0:E * TILES], m.ps[:, 4, 0:E * TILES]
        flat = lambda a: a.rearrange("p a b -> p (a b)")
        LINKS = 2
        block = own.enter_context(nc.Block())

        @block.gpsimd
        def _(pool):
            with nc.gpsimd.Fori(0, UNITS) as u:
                pool.wait_ge(sum_ready, u + 1)
                nc.gpsimd.tensor_tensor(rms[:], ssv[:], m.minus_half[0:TT, 0:TPU], ALU.pow).then_inc(root_ready, 1)
            pool.wait_ge(placed, 1)
            for t in range(TILES):
                for c in range(2):
                    nc.gpsimd.indirect_dma_start(m.x_slots, bass.IndirectOffsetOnAxis(ap=m.slot[c][:, t:t + 1], axis=0),
                                                 zn[:, t, :], None).then_inc(sent, 16)
            pool.wait_ge(sent, 16 * 2 * TILES)

        @block.tensor
        def _(pe):
            with nc.tensor.Fori(0, UNITS) as u:
                pe.wait_ge(zn_ready, u + 1)
                pe.wait_ge(nt_hi, u)
                pe.wait_ge(nt_lo, u)
                for k in range(KD):
                    for j in range(TPU):
                        last = nc.tensor.transpose(nt_ps[:, k, j * TT:(j + 1) * TT], stage[:, j, k * 128:(k + 1) * 128],
                                                   m.ident[0:TT, 0:TT])
                last.then_inc(nt_ready, 1)
                pe.wait_ge(nt_hi, u + 1)
                pe.wait_ge(nt_lo, u + 1)
                pe.wait_ge(logit_taken, u)
                for j in range(TPU):
                    terms = [x for k in range(KD) for x in passes(
                        zt_h[:, k, j * TT:(j + 1) * TT], zt_l[:, k, j * TT:(j + 1) * TT],
                        m.router_hi[:, k * E:(k + 1) * E], m.router_lo[:, k * E:(k + 1) * E])]
                    for i, (a, b) in enumerate(terms):
                        last = nc.tensor.matmul(log_ps[:, j * E:(j + 1) * E], a, b, start=(i == 0), stop=(i == len(terms) - 1))
                last.then_inc(logit_ready, 1)
            pe.wait_ge(picked, 1)
            nc.tensor.matmul(pre_ps, m.earlier[:], flat(both[:]), start=True, stop=True)
            nc.tensor.matmul(cnt_ps, m.all_ones[:], flat(both[:]), start=True, stop=True).then_inc(counted, 1)

        @block.scalar
        def _(act):
            with nc.scalar.Fori(0, UNITS) as u:
                act.wait_ge(nt_ready, u + 1)
                act.wait_ge(logit_ready, u)
                nc.scalar.activation(zt_h[:], nt_ps, ACT.Copy).then_inc(nt_hi, 1)
            act.wait_ge(shifted, 1)
            nc.scalar.activation(ex[:], ex[:], ACT.Exp).then_inc(exp_ready, 1)

        @block.vector
        def _(dve):
            chain = Chain(dve, order)
            with nc.vector.Fori(0, UNITS) as u:
                chain.turn(u * LINKS)
                zu = lambda j: m.n1[:, u, j * D:(j + 1) * D]
                for j in range(TPU):
                    ins = nc.vector.scalar_tensor_tensor(scratch[:, j, :], zu(j), 1.0, zu(j), ALU.mult, ALU.mult,
                                                         accum_out=ss[:, j:j + 1])
                chain.link(ins)
                nc.vector.tensor_scalar(ssv[:], ss[:], 1.0 / D, RMS_EPS, ALU.mult, ALU.add).then_inc(sum_ready, 1)
                dve.wait_ge(root_ready, u + 1)
                dve.wait_ge(nt_ready, u)
                for j in range(TPU):
                    ins = nc.vector.scalar_tensor_tensor(stage[:, j, :], zu(j), rms[:, j:j + 1], m.norm_w[:], ALU.mult, ALU.mult)
                ins.then_inc(zn_ready, 1)
                dve.wait_ge(zn_ready, u + 1)
                chain.link(nc.vector.tensor_copy(zn[:].rearrange("p (u j) d -> p u (j d)", j=TPU)[:, u, :], flat(stage[:])))
                dve.wait_ge(nt_hi, u + 1)
                nc.vector.tensor_tensor(zt_l[:], nt_ps, zt_h[:], ALU.subtract).then_inc(nt_lo, 1)
                dve.wait_ge(logit_ready, u + 1)
                nc.vector.tensor_scalar(logit[:].rearrange("p (u j) e -> p u (j e)", j=TPU)[:, u, :], log_ps, 1.0 / WS, None,
                                        ALU.mult).then_inc(logit_taken, 1)
                assert chain.n == LINKS, chain.n
            chain.turn(UNITS * LINKS)
            dve.wait_ge(logit_taken, UNITS)
            for t in range(TILES):
                ins = nc.vector.max(top[:, t, :], logit[:, t, :])
            chain.link(ins)
            for t in range(TILES):
                ins = nc.vector.max_index(index[:, t, :], top[:, t, :], logit[:, t, :])
            chain.link(ins)
            nc.vector.tensor_tensor(ex[:], logit[:], top[:, :, 0:1].to_broadcast([TT, TILES, E]), ALU.subtract).then_inc(shifted, 1)
            chain.link(nc.vector.tensor_copy(pick[:], index[:, :, 0:2]))
            for c in range(2):
                ins = nc.vector.tensor_tensor(mask[c][:], pick[:, :, c].unsqueeze(1).to_broadcast([TT, E, TILES]),
                                              m.expert_no[:].unsqueeze(2).to_broadcast([TT, E, TILES]), ALU.is_equal)
            chain.link(ins)
            nc.vector.tensor_tensor(both[:], mask[0][:], mask[1][:], ALU.add).then_inc(picked, 1)
            dve.wait_ge(exp_ready, 1)
            chain.link(nc.vector.tensor_reduce(total[:], ex[:], AX_X, ALU.add))
            chain.link(nc.vector.reciprocal(inv[:], total[:]))
            for c, s in enumerate((s1, s2)):
                chain.link(nc.vector.tensor_tensor(chosen[:].rearrange("p e t -> p t e"), ex[:], mask[c][:].rearrange("p e t -> p t e"), ALU.mult))
                chain.link(nc.vector.tensor_reduce(s[:], chosen[:].rearrange("p e t -> p t e"), AX_X, ALU.add))
                chain.link(nc.vector.tensor_tensor(s[:], s[:], inv[:], ALU.mult))
            chain.link(nc.vector.scalar_tensor_tensor(den[:], s1[:], GATE_EPS, s2[:], ALU.add, ALU.add))
            chain.link(nc.vector.reciprocal(inv[:], den[:]))
            chain.link(nc.vector.tensor_tensor(m.gate[0][:], s1[:], inv[:], ALU.mult))
            chain.link(nc.vector.tensor_tensor(m.gate[1][:], s2[:], inv[:], ALU.mult))
            dve.wait_ge(counted, 1)
            chain.link(nc.vector.tensor_copy(flat(counts[:]), cnt_ps))
            chain.link(nc.vector.tensor_tensor_scan(flat(running[:]), flat(m.not_first[:]), flat(counts[:]), 0.0, ALU.mult, ALU.add))
            n_e = running[0:TT, :, TILES - 1]
            chain.link(nc.vector.tensor_tensor(more[:], n_e.unsqueeze(2).to_broadcast([TT, E, TPE]),
                                               m.by128[:].unsqueeze(1).to_broadcast([TT, E, TPE]), ALU.is_gt))
            chain.link(nc.vector.tensor_reduce(tiles[:], more[:], AX_X, ALU.add))
            chain.link(nc.vector.tensor_tensor_scan(upto[:], m.ones_row[:], tiles[:], 0.0, ALU.mult, ALU.add))
            chain.link(nc.vector.tensor_tensor(before[:], upto[:], tiles[:], ALU.subtract))
            chain.link(nc.vector.tensor_scalar(before[:], before[:], 128.0, None, ALU.mult))
            chain.link(nc.vector.tensor_tensor(flat(place[:]), pre_ps, flat(running[0:TT]), ALU.add))
            chain.link(nc.vector.tensor_tensor(place[:], place[:], counts[0:TT], ALU.subtract))
            chain.link(nc.vector.tensor_tensor(place[:], place[:], before[:].unsqueeze(2).to_broadcast([TT, E, TILES]), ALU.add))
            for c in range(2):
                chain.link(nc.vector.tensor_tensor(chosen[:], mask[c][:], place[:], ALU.mult))
                chain.link(nc.vector.tensor_reduce(slot_f[:], chosen[:].rearrange("p e t -> p t e"), AX_X, ALU.add))
                ins = nc.vector.tensor_copy(m.slot[c][:], slot_f[:])
                chain.link(ins) if c == 0 else ins.then_inc(placed, 1)
            shape = [1, SLOT_TILES, E]
            chain.link(nc.vector.tensor_tensor(past[:], m.tile_no[:].unsqueeze(2).to_broadcast(shape),
                                               upto[0:1].unsqueeze(1).to_broadcast(shape), ALU.is_ge))
            chain.link(nc.vector.tensor_reduce(tab[:], past[:], AX_X, ALU.add))
            chain.link(nc.vector.tensor_scalar(tab[:], tab[:], float(E - 1), None, ALU.min))
            nc.vector.tensor_copy(m.table[:], tab[:])


def phase_experts(nc, m):
    with ExitStack() as own:
        def sem(name):
            return own.enter_context(nc.semaphore(f"e{m.round}_" + name))

        def sb(name, shape, dt):
            return own.enter_context(nc.sbuf_tensor(f"e{m.round}_" + name, shape, dt))

        loaded = [sem("loaded0"), sem("loaded1")]
        stored = [sem("stored0"), sem("stored1")]
        xt_ready, xt_hi, xt_lo, up_ready = sem("xt_ready"), sem("xt_hi"), sem("xt_lo"), sem("up_ready")
        silu_ready, g_ready, gt_ready, gt_hi, gt_lo, y_ready, y_taken = (
            sem("silu_ready"), sem("g_ready"), sem("gt_ready"), sem("gt_hi"), sem("gt_lo"), sem("y_ready"), sem("y_taken"))
        xs = [sb(f"xs{p}", [128, D], F32) for p in range(2)]
        xt_h, xt_l = [sb(f"xt_h{p}", [128, D], F16) for p in range(2)], [sb(f"xt_l{p}", [128, D], F16) for p in range(2)]
        si = [sb(f"si{p}", [128, FE], F32) for p in range(2)]
        g = [sb(f"g{p}", [128, FE], F32) for p in range(2)]
        gt_h, gt_l = sb("gt_h", [128, FE], F16), sb("gt_l", [128, FE], F16)
        ys = [sb(f"ys{p}", [128, D], F32) for p in range(2)]
        Q = SLOT_TILES
        assert Q % 2 == 1
        slots_in, slots_out = (t.rearrange("(q p) d -> q p d", p=128) for t in (m.x_slots, m.y_slots))
        XT, GT, Y = 4, 5, 6
        block = own.enter_context(nc.Block())

        def by_pairs(engine, tile):
            with engine.Fori(0, (Q - 1) // 2) as i:
                tile(i * 2 + 1, 1)
                tile(i * 2 + 2, 0)

        @block.sync
        def _(sp):
            def load(q, p):
                sp.wait_ge(xt_ready, q - 1)
                settle(sp, xt_ready)
                sp.dma_start(xs[p][:], slots_in[q]).then_inc(loaded[p], 16)

            sp.dma_start(xs[0][:], slots_in[0]).then_inc(loaded[0], 16)
            by_pairs(nc.sync, load)

        @block.gpsimd
        def _(pool):
            def store(q, p):
                pool.wait_ge(y_taken, q + 1)
                settle(pool, y_taken)
                nc.gpsimd.dma_start(slots_out[q], ys[p][:]).then_inc(stored[p], 16)

            pool.wait_ge(y_taken, 1)
            nc.gpsimd.dma_start(slots_out[0], ys[0][:]).then_inc(stored[0], 16)
            by_pairs(nc.gpsimd, store)
            pool.wait_ge(stored[0], 16 * (Q // 2 + 1))
            pool.wait_ge(stored[1], 16 * (Q // 2))

        @block.tensor
        def _(pe):
            def expert(q):
                return nc.tensor.value_load(m.table[0:1, bass.ds(q, 1)], min_val=0, max_val=E - 1)

            def up(q, p, half):
                e = expert(q)
                pe.wait_ge(loaded[p], 16 * half + 16)
                pe.wait_ge(xt_hi, q)
                pe.wait_ge(xt_lo, q)
                for k in range(KD):
                    last = nc.tensor.transpose(m.ps[:, XT, k * 128:(k + 1) * 128], xs[p][:, k * 128:(k + 1) * 128], m.ident[:])
                last.then_inc(xt_ready, 1)
                pe.wait_ge(xt_hi, q + 1)
                pe.wait_ge(xt_lo, q + 1)
                for c, (whi, wlo) in enumerate([(m.e1_hi, m.e1_lo), (m.e3_hi, m.e3_lo)]):
                    n = 0
                    for k in range(KD):
                        for a, b in passes(xt_h[p][:, k * 128:(k + 1) * 128], xt_l[p][:, k * 128:(k + 1) * 128], whi, wlo):
                            last = nc.tensor.matmul(m.ps[:, 2 * p + c, :], a, b[:, bass.ds(e * (KD * FE) + k * FE, FE)],
                                                    start=(n == 0), stop=(n == 3 * KD - 1))
                            n += 1
                last.then_inc(up_ready, 1)

            def down(q, p):
                e = expert(q)
                pe.wait_ge(g_ready, q + 1)
                pe.wait_ge(gt_hi, q)
                pe.wait_ge(gt_lo, q)
                for f in range(FE // 128):
                    last = nc.tensor.transpose(m.ps[:, GT, f * 128:(f + 1) * 128], g[p][:, f * 128:(f + 1) * 128], m.ident[:])
                last.then_inc(gt_ready, 1)
                pe.wait_ge(gt_hi, q + 1)
                pe.wait_ge(gt_lo, q + 1)
                pe.wait_ge(y_taken, q)
                n = 0
                for f in range(FE // 128):
                    for a, b in passes(gt_h[:, f * 128:(f + 1) * 128], gt_l[:, f * 128:(f + 1) * 128], m.e2_hi, m.e2_lo):
                        last = nc.tensor.matmul(m.ps[:, Y, 0:D], a, b[:, bass.ds(e * (FE // 128 * D) + f * D, D)],
                                                start=(n == 0), stop=(n == 3 * FE // 128 - 1))
                        n += 1
                last.then_inc(y_ready, 1)

            up(0, 0, 0)
            with nc.tensor.Fori(0, (Q - 1) // 2) as i:
                up(i * 2 + 1, 1, i)
                down(i * 2, 0)
                up(i * 2 + 2, 0, i + 1)
                down(i * 2 + 1, 1)
            down(Q - 1, 0)

        @block.scalar
        def _(act):
            def rows_in(q, p):
                act.wait_ge(xt_ready, q + 1)
                nc.scalar.activation(xt_h[p][:], m.ps[:, XT, 0:D], ACT.Copy).then_inc(xt_hi, 1)

            def gate(q, p):
                act.wait_ge(up_ready, q + 1)
                nc.scalar.activation(si[p][:], m.ps[:, 2 * p, :], ACT.Silu, scale=1.0 / WS).then_inc(silu_ready, 1)

            def turned(q, p):
                act.wait_ge(gt_ready, q + 1)
                act.wait_ge(y_ready, q)
                nc.scalar.activation(gt_h[:], m.ps[:, GT, :], ACT.Copy).then_inc(gt_hi, 1)

            rows_in(0, 0)
            gate(0, 0)
            with nc.scalar.Fori(0, (Q - 1) // 2) as i:
                for q, p in ((i * 2, 0), (i * 2 + 1, 1)):
                    rows_in(q + 1, 1 - p)
                    turned(q, p)
                    gate(q + 1, 1 - p)
            turned(Q - 1, 0)

        @block.vector
        def _(dve):
            def rows_in(q, p):
                dve.wait_ge(xt_hi, q + 1)
                nc.vector.tensor_tensor(xt_l[p][:], m.ps[:, XT, 0:D], xt_h[p][:], ALU.subtract).then_inc(xt_lo, 1)

            def gate(q, p):
                dve.wait_ge(silu_ready, q + 1)
                nc.vector.scalar_tensor_tensor(g[p][:], m.ps[:, 2 * p + 1, :], 1.0 / WS, si[p][:], ALU.mult, ALU.mult).then_inc(g_ready, 1)

            def turned(q, p):
                dve.wait_ge(gt_hi, q + 1)
                nc.vector.tensor_tensor(gt_l[:], m.ps[:, GT, :], gt_h[:], ALU.subtract).then_inc(gt_lo, 1)

            def out(q, p, half):
                dve.wait_ge(stored[p], 16 * half)
                dve.wait_ge(y_ready, q + 1)
                nc.vector.tensor_scalar(ys[p][:], m.ps[:, Y, 0:D], 1.0 / WS, None, ALU.mult).then_inc(y_taken, 1)

            rows_in(0, 0)
            gate(0, 0)
            with nc.vector.Fori(0, (Q - 1) // 2) as i:
                for q, p in ((i * 2, 0), (i * 2 + 1, 1)):
                    rows_in(q + 1, 1 - p)
                    turned(q, p)
                    gate(q + 1, 1 - p)
                    out(q, p, i)
            turned(Q - 1, 0)
            out(Q - 1, 0, (Q - 1) // 2)


def phase_combine(nc, m):
    with ExitStack() as own:
        def sem(name):
            return own.enter_context(nc.semaphore(f"c{m.round}_" + name))

        NB = 6
        rows = [[own.enter_context(nc.sbuf_tensor(f"c{m.round}_rows{b}_{c}", [TT, D], F32)) for c in range(2)] for b in range(NB)]
        got = [sem(f"got{b}") for b in range(NB)]
        half_done, used = sem("half_done"), sem("used")
        block = own.enter_context(nc.Block())

        @block.gpsimd
        def _(pool):
            for t in range(TILES):
                if t >= NB:
                    pool.wait_ge(used, t - NB + 1)
                for c in range(2):
                    nc.gpsimd.indirect_dma_start(rows[t % NB][c][:], None, m.y_slots,
                                                 bass.IndirectOffsetOnAxis(ap=m.slot[c][:, t:t + 1], axis=0)).then_inc(got[t % NB], 16)

        @block.vector
        def _(dve):
            for t in range(TILES):
                z = m.n1[:, t // TPU, (t % TPU) * D:(t % TPU + 1) * D]
                dve.wait_ge(got[t % NB], 32 * (t // NB + 1))
                nc.vector.scalar_tensor_tensor(z, rows[t % NB][0][:], m.gate[0][:, t:t + 1], z, ALU.mult, ALU.add).then_inc(half_done, 1)
                dve.wait_ge(half_done, t + 1)
                nc.vector.scalar_tensor_tensor(z, rows[t % NB][1][:], m.gate[1][:, t:t + 1], z, ALU.mult, ALU.add).then_inc(used, 1)
            dve.wait_ge(used, TILES)


def phase_out(nc, m):
    with nc.semaphore("out_done") as done, nc.semaphore("out_sum") as added, nc.Block() as block:
        @block.vector
        def _(dve):
            with nc.vector.Fori(0, UNITS) as u:
                nc.vector.tensor_tensor(m.h[:, u, :], m.h[:, u, :], m.n1[:, u, :], ALU.add).then_inc(added, 1)

        @block.sync
        def _(sp):
            with nc.sync.Fori(0, UNITS) as u:
                sp.wait_ge(added, u + 1)
                settle(sp, added)
                sp.dma_start(m.out[u], m.h[:, u, :]).then_inc(done, 16)
            sp.wait_ge(done, 16 * UNITS)


class Memory:
    pass


def build(nc, a, out):
    ctx = ExitStack()
    with ctx:
        m = Memory()
        m.out = out

        def sb(name, shape, dt):
            return ctx.enter_context(nc.sbuf_tensor(name, shape, dt))

        m.x = a["x"]
        m.round = 0
        m.ps = ctx.enter_context(nc.psum_tensor("ps", [128, 8, 512], F32))
        m.ident, m.minus_half = sb("ident", [128, 128], F32), sb("minus_half", [128, 4], F32)
        m.h, m.n1 = sb("h", [TT, UNITS, TPU * D], F32), sb("n1", [TT, UNITS, TPU * D], F32)
        m.stats, m.mv = sb("stats", [TT, TPU, 6], F32), sb("mv", [TT, TPU, 2], F32)
        m.carry = sb("carry", [TT, 1], F32)
        m.vareps, m.rstd = sb("vareps", [TT, TPU], F32), sb("rstd", [TT, TPU], F32)

        def dram(name, shape, dt):
            return nc.dram_tensor(name, shape, dt, kind="Internal").ap()

        m.gram_d = dram("gram_d", (UNITS, UNIT_IMAGES, H, SEQ, 2 * SEQ), F32)
        m.w_d = dram("w_d", (UNITS, UNIT_IMAGES, H, SEQ, 2 * SEQ), F16)
        m.beta_d, m.alpha_d, m.qn_d = (dram(n, (UNITS, UNIT_IMAGES, H, SEQ), F32) for n in ("beta_d", "alpha_d", "qn_d"))
        batch = "(b v) i h t -> b (v i h) t"
        m.gram_b = m.gram_d.rearrange("(b v) i h s n -> b (v i h) s n", v=2)
        m.w_b = m.w_d.rearrange("(b v) i h s n -> b (v i h) s n", v=2)
        m.beta_b, m.alpha_b, m.qn_b = (t.rearrange(batch, v=2) for t in (m.beta_d, m.alpha_d, m.qn_d))

        with ExitStack() as att:
            def sa(name, shape, dt):
                return att.enter_context(nc.sbuf_tensor(name, shape, dt))

            m.nt_hi, m.nt_lo = sa("nt_hi", [128, UNITS, KD, UT], F16), sa("nt_lo", [128, UNITS, KD, UT], F16)
            m.later, m.same = sa("later", [128, SEQ, SEQ], F32), sa("same", [128, SEQ, SEQ], F32)
            m.head_ones = sa("head_ones", [128, H, H], F32)
            m.wbd = [sa(f"wbd{g}", [SEQ * n, H, n, 2 * SEQ], F16) for g, (_, n) in enumerate(GROUPS)]
            m.qk_hi = [sa(f"qk_hi{p}", [128, 2 * UT + 28], F16) for p in range(2)]
            m.qk_lo = [sa(f"qk_lo{p}", [128, 2 * UT + 28], F16) for p in range(2)]
            jobs, pairs = [], {}
            for name in ("wp", "wq", "wk", "wv", "wba", "wo", "w1", "w2"):
                n = a[name].shape[1]
                pairs[name] = sa(name + "_hi", [128, n], F16), sa(name + "_lo", [128, n], F16)
                jobs.append((a[name], *pairs[name], n))
            m.wp_hi, m.wp_lo = pairs["wp"]
            m.wq_hi, m.wq_lo = pairs["wq"]
            m.wk_hi, m.wk_lo = pairs["wk"]
            m.wv_hi, m.wv_lo = pairs["wv"]
            m.wba_hi, m.wba_lo = pairs["wba"]
            m.wo_hi, m.wo_lo = pairs["wo"]
            m.w1_hi, m.w1_lo = pairs["w1"]
            m.w2_hi, m.w2_lo = pairs["w2"]
            m.pos, m.bproj = sa("pos", [TT, TPU * D], F32), sa("bproj", [TT, TPU * D], F32)
            m.ln1_w, m.ln1_b, m.ln2_w, m.ln2_b, m.b2 = (sa(n, [TT, D], F32) for n in ("ln1_w", "ln1_b", "ln2_w", "ln2_b", "b2"))
            m.b1 = sa("b1", [128, F // 128], F32)
            m.plain = [(m.pos[:], a["pos"]), (m.bproj[:], a["bproj"]), (m.ln1_w[:], a["ln1_w"]), (m.ln1_b[:], a["ln1_b"]),
                       (m.ln2_w[:], a["ln2_w"]), (m.ln2_b[:], a["ln2_b"]), (m.b2[:], a["b2"]), (m.b1[:], a["b1"])]
            m.first = True
            load_weights(nc, ctx, m, jobs)
            phase_tokens(nc, m)
            phase_grams(nc, m)
            phase_solve(nc, m)
            phase_mix(nc, m)
        with ExitStack() as moe:
            def sm(name, shape, dt):
                return moe.enter_context(nc.sbuf_tensor(name, shape, dt))

            m.x_slots, m.y_slots = dram("x_slots", (ROWS, D), F32), dram("y_slots", (ROWS, D), F32)
            jobs, pairs = [], {}
            for name in ("e1", "e3", "e2", "router"):
                n = a[name].shape[1]
                pairs[name] = sm(name + "_hi", [128, n], F16), sm(name + "_lo", [128, n], F16)
                jobs.append((a[name], *pairs[name], n))
            m.e1_hi, m.e1_lo = pairs["e1"]
            m.e3_hi, m.e3_lo = pairs["e3"]
            m.e2_hi, m.e2_lo = pairs["e2"]
            m.router_hi, m.router_lo = pairs["router"]
            m.norm_w = sm("norm_w", [TT, D], F32)
            m.gate = [sm(f"gate{c}", [TT, TILES], F32) for c in range(2)]
            m.slot = [sm(f"slot{c}", [TT, TILES], mybir.dt.uint32) for c in range(2)]
            m.table = sm("table", [1, SLOT_TILES], mybir.dt.int32)
            m.earlier, m.all_ones = sm("earlier", [TT, TT], F32), sm("all_ones", [TT, 128], F32)
            m.expert_no = sm("expert_no", [TT, E], F32)
            m.not_first = sm("not_first", [128, E, TILES], F32)
            m.by128, m.tile_no, m.ones_row = sm("by128", [TT, IMAGES * SEQ // 128], F32), sm("tile_no", [1, SLOT_TILES], F32), sm("ones_row", [TT, E], F32)
            m.plain = [(m.norm_w[:], a["norm_w"])]
            m.first, m.round = False, 1
            load_weights(nc, ctx, m, jobs)
            for m.round in range(1, LOOPS + 1):
                phase_route(nc, m)
                phase_experts(nc, m)
                phase_combine(nc, m)
        phase_out(nc, m)


def kernel(x, L0_tok_W_proj, L0_tok_b_proj, L0_tok_pos_emb, L0_attn_Wq, L0_attn_Wk, L0_attn_Wv, L0_attn_Wb, L0_attn_Wa,
           L0_attn_Wo, L0_attn_ln1_w, L0_attn_ln1_b, L0_attn_ln2_w, L0_attn_ln2_b, L0_attn_W1, L0_attn_b1, L0_attn_W2,
           L0_attn_b2, L0_ffn_norm_w, L0_ffn_router_w, L0_ffn_w1, L0_ffn_w3, L0_ffn_w2):
    import numpy as np
    import concourse.bacc as bacc
    from concourse.bass_utils import run_bass_kernel_spmd

    def rows(w):
        w = np.asarray(w)
        return np.ascontiguousarray(w.reshape(-1, 128, w.shape[1]).transpose(1, 0, 2).reshape(128, -1))

    def experts(w):
        w = np.asarray(w)
        return np.ascontiguousarray(w.reshape(E, -1, 128, w.shape[2]).transpose(2, 0, 1, 3).reshape(128, -1))

    def spread(v, reps=1):
        v = np.asarray(v)
        return np.ascontiguousarray(np.broadcast_to(v, (TT, reps, v.shape[0])).reshape(TT, -1))

    xs = np.asarray(x).reshape(UNITS, UNIT_IMAGES, 6, 16, 6, 48).transpose(0, 3, 5, 1, 2, 4).reshape(UNITS, KP, 128, UT)
    token = (np.arange(TPU)[None, :] * TT + np.arange(TT)[:, None]) % SEQ
    arrays = {
        "x": np.ascontiguousarray(xs.transpose(0, 2, 1, 3)),
        "wp": rows(np.asarray(L0_tok_W_proj).T),
        "pos": np.ascontiguousarray(np.asarray(L0_tok_pos_emb)[token].reshape(TT, TPU * D)),
        "bproj": spread(L0_tok_b_proj, TPU),
        "wq": rows(L0_attn_Wq), "wk": rows(L0_attn_Wk), "wv": rows(L0_attn_Wv),
        "wba": rows(np.concatenate([np.asarray(L0_attn_Wb), np.asarray(L0_attn_Wa)], axis=1)),
        "wo": rows(L0_attn_Wo), "w1": rows(L0_attn_W1), "w2": rows(L0_attn_W2),
        "ln1_w": spread(L0_attn_ln1_w), "ln1_b": spread(L0_attn_ln1_b),
        "ln2_w": spread(L0_attn_ln2_w), "ln2_b": spread(L0_attn_ln2_b), "b2": spread(L0_attn_b2),
        "e1": experts(L0_ffn_w1), "e3": experts(L0_ffn_w3), "e2": experts(L0_ffn_w2),
        "router": rows(L0_ffn_router_w), "norm_w": spread(L0_ffn_norm_w),
        "b1": np.ascontiguousarray(np.asarray(L0_attn_b1).reshape(-1, 128).T),
    }
    nc = bacc.Bacc("TRN2", target_bir_lowering=False, num_devices=1)
    aps = {k: nc.dram_tensor(k + "_dram", v.shape, mybir.dt.from_np(v.dtype), kind="ExternalInput").ap() for k, v in arrays.items()}
    out = nc.dram_tensor("out_dram", (UNITS, TT, TPU * D), F32, kind="ExternalOutput").ap()
    build(nc, aps, out)
    r = run_bass_kernel_spmd(nc, [{k + "_dram": v for k, v in arrays.items()}], core_ids=[0])
    y = np.asarray(r.results[0]["out_dram"])
    return y.reshape(UNITS, TT, TPU, D).transpose(0, 2, 1, 3).reshape(IMAGES, SEQ, D)
```

```python
from contextlib import ExitStack

import concourse.bass as bass
from concourse import mybir

ALU = mybir.AluOpType
ACT = mybir.ActivationFunctionType
F32 = mybir.dt.float32
F16 = mybir.dt.float16
U32 = mybir.dt.uint32
AX_X = mybir.AxisListType.X

IMAGES = 64
SEQ = 36
D = 256
PATCH = 768
H, DK = 8, 128
F = 1024
E, FE = 8, 512
UNIT_IMAGES = 8
UNITS = IMAGES // UNIT_IMAGES
UT = UNIT_IMAGES * SEQ
TPU = 3
TT = UT // TPU
TILES = UNITS * TPU
KD = D // 128
KP = PATCH // 128
BATCH_IMAGES = 128 // H
BATCHES = IMAGES // BATCH_IMAGES
GROUPS = [(0, 3), (3, 3), (6, 2)]
EPS = 1e-5
LOOPS = 2
L2_EPS = 1e-6
WS = 64.0
OS = 16.0
QS = 256.0


ONE = 1
DMA_SEMAPHORES = ("gathered", "scattered", "back", "stored", "out_stored", "loaded")
SEMAPHORES = {}
for _r in range(1, LOOPS + 1):
    SEMAPHORES[f"moe{_r}"] = """sq_act sum_ready root_ready zn_ready zn_copied zt_ready zt_hi zt_lo zn_used logit_ready shifted exp_ready
        order picked counted spread_ready spread_used listed places_ready gathered0 gathered1 gathered2 gathered3 xt_ready xt_hi
        xt_lo up1_ready up3_ready silu_ready g_ready gt_ready gt_hi gt_lo y_ready y_taken scattered0 scattered1 back0 back1
        half_done used base_ready out_stored stored0 stored1""".split()


class Chain:

    def __init__(self, engine, sem, per_turn=0):
        self.engine, self.sem, self.per_turn, self.n = engine, sem, per_turn, 0
        self.base = 0

    def turn(self, base):
        self.base, self.n = base, 0

    def link(self, ins):
        self.n += 1
        ins.then_inc(self.sem, 1)
        self.engine.wait_ge(self.sem, self.base + self.n)


def settle(engine, sem):
    engine.wait_ge(sem, 0)


def passes(hi_a, lo_a, hi_b, lo_b):
    return [(hi_a, hi_b), (lo_a, hi_b), (hi_a, lo_b)]


def load_weights(nc, ctx, m, jobs):
    with ExitStack() as own:
        stage = [own.enter_context(nc.sbuf_tensor(f"w{m.round}_stage{i}", [128, 2048], F32)) for i in range(2)]
        loaded = [own.enter_context(nc.semaphore(f"w{m.round}_loaded{i}")) for i in range(2)]
        hi_done = own.enter_context(nc.semaphore(f"w{m.round}_hi_done"))
        lo_done = own.enter_context(nc.semaphore(f"w{m.round}_lo_done"))
        consts = own.enter_context(nc.semaphore(f"w{m.round}_consts"))
        pieces = []
        for src, hi, lo, n in jobs:
            for a in range(0, n, 2048):
                b = min(n, a + 2048)
                pieces.append((src[:, a:b], hi[:, a:b], lo[:, a:b], b - a))
        block = own.enter_context(nc.Block())

        @block.sync
        def _(sp):
            for t, (src, _, _, n) in enumerate(pieces):
                if t >= 2:
                    sp.wait_ge(lo_done, t - 1)
                sp.dma_start(stage[t % 2][:, 0:n], src).then_inc(loaded[t % 2], 16)
            if m.first:
                for phase, names in SEMAPHORES.items():
                    for name, s in zip(names, m.sems[phase]):
                        if not name.startswith(DMA_SEMAPHORES):
                            sp.sem_inc(s, ONE)
            for dst, src in m.plain:
                sp.dma_start(dst, src).then_inc(consts, 16)
            sp.wait_ge(consts, 16 * len(m.plain))

        @block.scalar
        def _(act):
            for t, (_, hi, _, n) in enumerate(pieces):
                act.wait_ge(loaded[t % 2], 16 * (t // 2 + 1))
                nc.scalar.activation(hi, stage[t % 2][:, 0:n], ACT.Copy, scale=WS).then_inc(hi_done, 1)

        @block.vector
        def _(dve):
            for t, (_, hi, lo, n) in enumerate(pieces):
                dve.wait_ge(hi_done, t + 1)
                nc.vector.scalar_tensor_tensor(lo, stage[t % 2][:, 0:n], WS, hi, ALU.mult, ALU.subtract).then_inc(lo_done, 1)
            dve.wait_ge(lo_done, len(pieces))

        if not m.first:
            @block.gpsimd
            def _(pool):
                route_constants(nc, pool, m, own.enter_context(nc.semaphore(f"w{m.round}_route")))
        else:
            @block.gpsimd
            def _(pool):
                made = own.enter_context(nc.semaphore(f"w{m.round}_made"))
                nc.gpsimd.memset(m.ident[:], 0.0).then_inc(made, 1)
                nc.gpsimd.memset(m.later[:], 1.0).then_inc(made, 1)
                nc.gpsimd.memset(m.same[:], 0.0).then_inc(made, 1)
                nc.gpsimd.memset(m.head_ones[:], 0.0).then_inc(made, 1)
                nc.gpsimd.memset(m.minus_half[:], -0.5).then_inc(made, 1)
                pool.wait_ge(made, 5)
                nc.gpsimd.affine_select(out=m.ident[:], in_=m.ident[:], compare_op=ALU.not_equal, fill=1.0,
                                        base=0, pattern=[[-1, 128]], channel_multiplier=1).then_inc(made, 1)
                nc.gpsimd.affine_select(out=m.later[:], in_=m.later[:], compare_op=ALU.is_gt, fill=0.0,
                                        base=0, pattern=[[-1, SEQ], [1, SEQ]], channel_multiplier=0).then_inc(made, 1)
                nc.gpsimd.affine_select(out=m.same[:], in_=m.same[:], compare_op=ALU.not_equal, fill=1.0,
                                        base=0, pattern=[[-1, SEQ], [1, SEQ]], channel_multiplier=0).then_inc(made, 1)
                nc.gpsimd.affine_select(out=m.head_ones[:], in_=m.head_ones[:], compare_op=ALU.not_equal, fill=1.0,
                                        base=0, pattern=[[-1, H], [1, H]], channel_multiplier=0).then_inc(made, 1)
                pool.wait_ge(made, 9)
                for g in range(3):
                    nc.gpsimd.memset(m.wbd[g][:], 0.0).then_inc(made, 1)
                for p in range(2):
                    nc.gpsimd.memset(m.qk_hi[p][:], 0.0).then_inc(made, 1)
                    nc.gpsimd.memset(m.qk_lo[p][:], 0.0).then_inc(made, 1)
                pool.wait_ge(made, 16)


def route_constants(nc, pool, m, made):
    nc.gpsimd.memset(m.earlier[:], 1.0).then_inc(made, 1)
    nc.gpsimd.memset(m.all_ones[:], 1.0).then_inc(made, 1)
    nc.gpsimd.memset(m.not_first[:], 1.0).then_inc(made, 1)
    nc.gpsimd.memset(m.ones_row[:], 1.0).then_inc(made, 1)
    exact = dict(allow_small_or_imprecise_dtypes=True)
    nc.gpsimd.iota(m.expert_no[:], [[1, E]], base=0, channel_multiplier=0, **exact).then_inc(made, 1)
    nc.gpsimd.iota(m.by128[:], [[128, IMAGES * SEQ // 128]], base=0, channel_multiplier=0, **exact).then_inc(made, 1)
    nc.gpsimd.iota(m.tile_no[:], [[1, SLOT_TILES]], base=0, channel_multiplier=0, **exact).then_inc(made, 1)
    nc.gpsimd.iota(m.row_no[:], [[1, 128]], base=0, channel_multiplier=0, **exact).then_inc(made, 1)
    nc.gpsimd.iota(m.name_of[:], [[1, 2], [2 * TT, TILES]], base=1, channel_multiplier=2, **exact).then_inc(made, 1)
    nc.gpsimd.iota(m.spare_row[:], [[128, SLOT_TILES]], base=2 * IMAGES * SEQ, channel_multiplier=1, **exact).then_inc(made, 1)
    pool.wait_ge(made, 10)
    nc.gpsimd.affine_select(out=m.earlier[:], in_=m.earlier[:], compare_op=ALU.is_gt, fill=0.0, base=0,
                            pattern=[[1, TT]], channel_multiplier=-1).then_inc(made, 1)
    nc.gpsimd.affine_select(out=m.not_first[:], in_=m.not_first[:], compare_op=ALU.is_gt, fill=0.0, base=0,
                            pattern=[[0, E], [1, TILES]], channel_multiplier=0).then_inc(made, 1)
    pool.wait_ge(made, 12)


def normalise(nc, dve, chain, m, src, dst, turn, k):
    nc.vector.memset(m.carry[:], 0.0)
    for j in range(TPU):
        ins = nc.vector.bn_stats(m.stats[:, j, :], src(j))
    chain.link(ins)
    nc.vector.memset(m.carry[:], 0.0)
    for j in range(TPU):
        ins = nc.vector.bn_aggr(m.mv[:, j, :], m.stats[:, j, :])
    chain.link(ins)
    nc.vector.tensor_scalar(m.vareps[:], m.mv[:, :, 1], EPS, None, ALU.add).then_inc(m.var_ready, 1)
    dve.wait_ge(m.root_ready, turn * m.roots_per_turn + k)
    for j in range(TPU):
        ins = nc.vector.tensor_scalar(dst(j), src(j), m.mv[:, j, 0:1], m.rstd[:, j:j + 1], ALU.subtract, ALU.mult)
    chain.link(ins)


def roots(nc, pool, m, turns, per_turn):
    with nc.gpsimd.Fori(0, turns) as u:
        for k in range(per_turn):
            pool.wait_ge(m.var_ready, u * per_turn + (k + 1))
            nc.gpsimd.tensor_tensor(m.rstd[0:TT, :], m.vareps[0:TT, :], m.minus_half[0:TT, 0:TPU],
                                    ALU.pow).then_inc(m.root_ready, 1)


def phase_tokens(nc, m):
    with ExitStack() as own:
        def sem(name):
            return own.enter_context(nc.semaphore(f"t{m.round}_" + name))

        def sb(name, shape, dt):
            return own.enter_context(nc.sbuf_tensor(f"t{m.round}_" + name, shape, dt))

        x_loaded, x_hi, x_lo = sem("x_loaded"), sem("x_hi"), sem("x_lo")
        tok_ready, tok_taken = sem("tok_ready"), sem("tok_taken")
        m.var_ready, m.root_ready = sem("var_ready"), sem("root_ready")
        n_ready, nt_ready, nt_hi, nt_lo, order = sem("n_ready"), sem("nt_ready"), sem("nt_hi"), sem("nt_lo"), sem("order")
        xin = sb("xin", [128, KP, UT], F32)
        xh, xl = sb("xh", [128, KP, UT], F16), sb("xl", [128, KP, UT], F16)
        n_tok = sb("n_tok", [TT, TPU, D], F32)
        tok_ps = m.ps[0:TT, 0:2, :].rearrange("p b n -> p (b n)")[:, 0:TPU * D]
        nt_ps = m.ps[:, 4:6, 0:UT]
        LINKS = 8
        m.roots_per_turn = 2
        block = own.enter_context(nc.Block())

        @block.sync
        def _(sp):
            sp.dma_start(xin[:], m.x[0]).then_inc(x_loaded, 16)
            with nc.sync.Fori(1, UNITS) as u:
                sp.wait_ge(x_hi, u)
                sp.wait_ge(x_lo, u)
                settle(sp, x_lo)
                sp.dma_start(xin[:], m.x[u]).then_inc(x_loaded, 16)

        @block.scalar
        def _(act):
            def split_x(u):
                act.wait_ge(x_loaded, 16 * u + 16)
                act.wait_ge(tok_ready, u)
                nc.scalar.activation(xh[:], xin[:], ACT.Copy).then_inc(x_hi, 1)

            def split_nt(u):
                act.wait_ge(nt_ready, u + 1)
                nc.scalar.activation(m.nt_hi[:, u, :, :], nt_ps, ACT.Copy).then_inc(nt_hi, 1)

            split_x(0)
            with nc.scalar.Fori(0, UNITS - 1) as u:
                split_x(u + 1)
                split_nt(u)
            split_nt(UNITS - 1)

        @block.gpsimd
        def _(pool):
            roots(nc, pool, m, UNITS, 2)

        @block.tensor
        def _(pe):
            def project(u):
                pe.wait_ge(x_hi, u + 1)
                pe.wait_ge(x_lo, u + 1)
                pe.wait_ge(tok_taken, u)
                for j in range(TPU):
                    terms = [t for k in range(KP) for t in passes(
                        xh[:, k, j * TT:(j + 1) * TT], xl[:, k, j * TT:(j + 1) * TT],
                        m.wp_hi[:, k * D:(k + 1) * D], m.wp_lo[:, k * D:(k + 1) * D])]
                    for i, (a, b) in enumerate(terms):
                        last = nc.tensor.matmul(tok_ps[:, j * D:(j + 1) * D], a, b, start=(i == 0), stop=(i == len(terms) - 1))
                last.then_inc(tok_ready, 1)

            def turn_over(u):
                pe.wait_ge(n_ready, u + 1)
                pe.wait_ge(nt_hi, u)
                pe.wait_ge(nt_lo, u)
                for k in range(KD):
                    for j in range(TPU):
                        last = nc.tensor.transpose(nt_ps[:, k, j * TT:(j + 1) * TT], n_tok[:, j, k * 128:(k + 1) * 128],
                                                   m.ident[0:TT, 0:TT])
                last.then_inc(nt_ready, 1)

            project(0)
            with nc.tensor.Fori(0, UNITS - 1) as u:
                project(u + 1)
                turn_over(u)
            turn_over(UNITS - 1)

        @block.vector
        def _(dve):
            chain = Chain(dve, order)

            def split_x(u):
                dve.wait_ge(x_hi, u + 1)
                dve.wait_ge(tok_ready, u)
                nc.vector.tensor_tensor(xl[:], xin[:], xh[:], ALU.subtract).then_inc(x_lo, 1)

            def norms(u):
                chain.turn(u * LINKS)
                dve.wait_ge(tok_ready, u + 1)
                nc.vector.scalar_tensor_tensor(m.h[:, u, :], tok_ps, 1.0 / WS, m.pos[:], ALU.mult, ALU.add).then_inc(tok_taken, 1)
                dve.wait_ge(tok_taken, u + 1)
                hv = lambda j: m.h[:, u, j * D:(j + 1) * D]
                nv = lambda j: m.n1[:, u, j * D:(j + 1) * D]
                chain.link(nc.vector.tensor_tensor(m.h[:, u, :], m.h[:, u, :], m.bproj[:], ALU.add))
                normalise(nc, dve, chain, m, hv, nv, u, 1)
                dve.wait_ge(nt_ready, u)
                normalise(nc, dve, chain, m, nv, lambda j: n_tok[:, j, :], u, 2)
                for j in range(TPU):
                    ins = nc.vector.tensor_tensor(n_tok[:, j, :], n_tok[:, j, :], m.ln1_w[:], ALU.mult)
                chain.link(ins)
                for j in range(TPU):
                    ins = nc.vector.tensor_tensor(n_tok[:, j, :], n_tok[:, j, :], m.ln1_b[:], ALU.add)
                ins.then_inc(n_ready, 1)
                assert chain.n == LINKS, chain.n

            def split_nt(u):
                dve.wait_ge(nt_hi, u + 1)
                nc.vector.tensor_tensor(m.nt_lo[:, u, :, :], nt_ps, m.nt_hi[:, u, :, :], ALU.subtract).then_inc(nt_lo, 1)

            split_x(0)
            with nc.vector.Fori(0, UNITS - 1) as u:
                split_x(u + 1)
                norms(u)
                split_nt(u)
            norms(UNITS - 1)
            split_nt(UNITS - 1)


def phase_grams(nc, m):
    with ExitStack() as own:
        def sem(name):
            return own.enter_context(nc.semaphore(f"g{m.round}_" + name))

        def sb(name, shape, dt):
            return own.enter_context(nc.sbuf_tensor(f"g{m.round}_" + name, shape, dt))

        qk_ready, qk_act, qk_hi, qk_lo, sq_ready = sem("qk_ready"), sem("qk_act"), sem("qk_hi"), sem("qk_lo"), sem("sq_ready")
        sq_used, gram_ready, gram_taken = sem("sq_used"), sem("gram_ready"), sem("gram_taken")
        stored = [sem("stored0"), sem("stored1")]
        small_ready, small_taken, small_stored = sem("small_ready"), sem("small_taken"), sem("small_stored")
        qks = [sb(f"qks{p}", [128, 2, UT], F32) for p in range(2)]
        sq = [sb(f"sq{p}", [128, UT], F32) for p in range(2)]
        gsb = [sb(f"gsb{p}", [128, 4, UNIT_IMAGES // 2, 2 * SEQ], F32) for p in range(2)]
        qn_sb = sb("qn_sb", [H, UT], F32)
        ba_sb = sb("ba_sb", [2 * H, UT], F32)
        PAIRS = UNIT_IMAGES // 2
        block = own.enter_context(nc.Block())

        @block.tensor
        def _(pe):
            def project(u, h):
                p = h % 2
                pe.wait_ge(qk_act, u * H + max(h - 1, 0))
                for c, (whi, wlo) in enumerate([(m.wq_hi, m.wq_lo), (m.wk_hi, m.wk_lo)]):
                    terms = [t for k in range(KD) for t in passes(
                        whi[:, k * H * DK + h * DK:k * H * DK + (h + 1) * DK],
                        wlo[:, k * H * DK + h * DK:k * H * DK + (h + 1) * DK],
                        m.nt_hi[:, u, k, :], m.nt_lo[:, u, k, :])]
                    for i, (a, b) in enumerate(terms):
                        last = nc.tensor.matmul(m.ps[:, 2 * p + c, 0:UT], a, b, start=(i == 0), stop=(i == len(terms) - 1))
                last.then_inc(qk_ready, 1)

            def gram(u, h):
                p = h % 2
                qh, ql = m.qk_hi[p], m.qk_lo[p]
                pe.wait_ge(qk_hi, u * H + h + 1)
                pe.wait_ge(qk_lo, u * H + h + 1)
                pe.wait_ge(gram_taken, u * H + max(h - 1, 0))
                for i in range(UNIT_IMAGES):
                    out = m.ps[64 * (i % 2):64 * (i % 2) + 64, 4 + p, (i // 2) * 72:(i // 2) * 72 + 72]
                    k0 = UT + i * SEQ
                    kh, kl = qh[:, k0:k0 + 64], ql[:, k0:k0 + 64]
                    rh = qh[:, 0:2 * UT].rearrange("p (c t) -> p c t", c=2)[:, :, i * SEQ:(i + 1) * SEQ]
                    rl = ql[:, 0:2 * UT].rearrange("p (c t) -> p c t", c=2)[:, :, i * SEQ:(i + 1) * SEQ]
                    for n, (a, b) in enumerate(passes(kh, kl, rh, rl)):
                        last = nc.tensor.matmul(out, a, b, start=(n == 0), stop=(n == 2))
                last.then_inc(gram_ready, 1)
                pe.wait_ge(sq_ready, u * H + h + 1)
                nc.tensor.matmul(m.ps[0:H, 6, 0:UT], m.head_ones[:, h, :], sq[p][:], start=(h == 0),
                                 stop=(h == H - 1)).then_inc(sq_used, 1)

            with nc.tensor.Fori(0, UNITS) as u:
                pe.wait_ge(small_taken, 2 * u)
                terms = [t for k in range(KD) for t in passes(
                    m.wba_hi[:, k * 16:(k + 1) * 16], m.wba_lo[:, k * 16:(k + 1) * 16],
                    m.nt_hi[:, u, k, :], m.nt_lo[:, u, k, :])]
                for i, (a, b) in enumerate(terms):
                    last = nc.tensor.matmul(m.ps[0:2 * H, 7, 0:UT], a, b, start=(i == 0), stop=(i == len(terms) - 1))
                last.then_inc(small_ready, 1)
                project(u, 0)
                for h in range(1, H):
                    project(u, h)
                    gram(u, h - 1)
                gram(u, H - 1)

        @block.scalar
        def _(act):
            with nc.scalar.Fori(0, UNITS) as u:
                for h in range(H):
                    p = h % 2
                    act.wait_ge(qk_ready, u * H + h + 1)
                    act.wait_ge(qk_lo, u * H + max(h - 1, 0))
                    act.wait_ge(sq_ready, u * H + max(h - 1, 0))
                    nc.scalar.activation(qks[p][:], m.ps[:, 2 * p:2 * p + 2, 0:UT], ACT.Silu, scale=1.0 / WS).then_inc(qk_act, 1)
                    act.wait_ge(qk_act, u * H + h + 1)
                    act.wait_ge(gram_ready, u * H + max(h - 1, 0))
                    nc.scalar.activation(m.qk_hi[p][:, 0:2 * UT].rearrange("p (c t) -> p c t", c=2), qks[p][:], ACT.Copy).then_inc(qk_hi, 1)

        @block.gpsimd
        def _(pool):
            with nc.gpsimd.Fori(0, UNITS) as u:
                for h in range(H):
                    pool.wait_ge(qk_act, u * H + h + 1)
                    pool.wait_ge(sq_used, u * H + max(h - 1, 0))
                    nc.gpsimd.tensor_tensor(sq[h % 2][:], qks[h % 2][:, 0, :], qks[h % 2][:, 0, :], ALU.mult).then_inc(sq_ready, 1)

        @block.vector
        def _(dve):
            def low(u, h):
                p = h % 2
                dve.wait_ge(qk_hi, u * H + h + 1)
                dve.wait_ge(gram_ready, u * H + max(h - 1, 0))
                nc.vector.tensor_tensor(m.qk_lo[p][:, 0:2 * UT].rearrange("p (c t) -> p c t", c=2), qks[p][:],
                                        m.qk_hi[p][:, 0:2 * UT].rearrange("p (c t) -> p c t", c=2), ALU.subtract).then_inc(qk_lo, 1)

            def take(u, h):
                if h % 4 == 0:
                    dve.wait_ge(stored[h // 4], u * 128)
                dve.wait_ge(gram_ready, u * H + h + 1)
                nc.vector.tensor_copy(gsb[h // 4][:, h % 4, :, :].rearrange("p c n -> p (c n)"),
                                      m.ps[:, 4 + h % 2, 0:PAIRS * 72]).then_inc(gram_taken, 1)

            with nc.vector.Fori(0, UNITS) as u:
                dve.wait_ge(small_ready, u + 1)
                dve.wait_ge(small_stored, u * 48)
                nc.vector.tensor_scalar(ba_sb[:], m.ps[0:2 * H, 7, 0:UT], 1.0 / WS, None, ALU.mult).then_inc(small_taken, 1)
                low(u, 0)
                for h in range(1, H):
                    low(u, h)
                    take(u, h - 1)
                take(u, H - 1)
                dve.wait_ge(sq_used, u * H + H)
                nc.vector.tensor_copy(qn_sb[:], m.ps[0:H, 6, 0:UT]).then_inc(small_taken, 1)

        @block.sync
        def _(sp):
            with nc.sync.Fori(0, UNITS) as u:
                sp.wait_ge(small_taken, 2 * u + 1)
                settle(sp, small_taken)
                for c, dst in enumerate([m.beta_d, m.alpha_d]):
                    sp.dma_start(dst[u].rearrange("i h t -> h i t"),
                                 ba_sb[c * H:(c + 1) * H, :].rearrange("h (i t) -> h i t", t=SEQ)).then_inc(small_stored, 16)
                for b in range(2):
                    sp.wait_ge(gram_taken, u * H + 4 * b + 4)
                    settle(sp, gram_taken)
                    for par in range(2):
                        dst = m.gram_d[u].rearrange("(c par) h s n -> par h s c n", par=2)
                        for hh in range(4):
                            sp.dma_start(dst[par, 4 * b + hh], gsb[b][64 * par:64 * par + SEQ, hh, :, :]).then_inc(stored[b], 16)
                sp.wait_ge(small_taken, 2 * u + 2)
                settle(sp, small_taken)
                sp.dma_start(m.qn_d[u].rearrange("i h t -> h i t"),
                             qn_sb[:].rearrange("h (i t) -> h i t", t=SEQ)).then_inc(small_stored, 16)
            sp.wait_ge(small_stored, 48 * UNITS)
            for b in range(2):
                sp.wait_ge(stored[b], 128 * UNITS)


def phase_solve(nc, m):
    with ExitStack() as own:
        def sem(name):
            return own.enter_context(nc.semaphore(f"s{m.round}_" + name))

        def sb(name, shape, dt):
            return own.enter_context(nc.sbuf_tensor(f"s{m.round}_" + name, shape, dt))

        loaded, gates, sums, inv, order = sem("loaded"), sem("gates"), sem("sums"), sem("inv"), sem("order")
        mixed, w_stored = sem("mixed"), sem("w_stored")
        NN = SEQ * SEQ
        gram = sb("gram", [128, SEQ, 2 * SEQ], F32)
        logit = sb("logit", [128, 2, SEQ], F32)
        gate = sb("gate", [128, 2, SEQ], F32)
        qn = sb("qn", [128, SEQ], F32)
        sq = sb("sq", [128, 2, SEQ], F32)
        rk = sb("rk", [128, 2, SEQ], F32)
        c = sb("c", [128, SEQ], F32)
        d0, d1, e = sb("d0", [128, SEQ, SEQ], F32), sb("d1", [128, SEQ, SEQ], F32), sb("e", [128, SEQ, SEQ], F32)
        at, wt = sb("at", [128, SEQ, SEQ], F32), sb("wt", [128, SEQ, SEQ], F32)
        tmp = [sb(f"tmp{i}", [128, NN // 3], F32) for i in range(3)]
        red = [sb(f"red{i}", [128, SEQ], F32) for i in range(3)]
        wo = sb("wo", [128, SEQ, 2 * SEQ], F16)
        mh = sb("mh", [128, 2 * SEQ], F32)
        THIRD = SEQ // 3
        LINKS = 10 + 3 * (SEQ - 1)
        block = own.enter_context(nc.Block())

        @block.scalar
        def _(act):
            with nc.scalar.Fori(0, BATCHES) as b:
                act.wait_ge(mixed, b)
                act.dma_start(gram[:], m.gram_b[b]).then_inc(loaded, 16)
                act.dma_start(logit[:, 0, :], m.beta_b[b]).then_inc(loaded, 16)
                act.dma_start(logit[:, 1, :], m.alpha_b[b]).then_inc(loaded, 16)
                act.dma_start(qn[:], m.qn_b[b]).then_inc(loaded, 16)
                act.wait_ge(loaded, 64 * b + 64)
                nc.scalar.activation(gate[:], logit[:], ACT.Sigmoid).then_inc(gates, 1)
                act.wait_ge(mixed, b + 1)
                act.dma_start(m.w_b[b], wo[:]).then_inc(w_stored, 16)
            act.wait_ge(w_stored, 16 * BATCHES)

        @block.gpsimd
        def _(pool):
            nc.gpsimd.memset(mh[:], -0.5).then_inc(inv, 1)
            pool.wait_ge(inv, 1)
            with nc.gpsimd.Fori(0, BATCHES) as b:
                pool.wait_ge(sums, b + 1)
                nc.gpsimd.tensor_tensor(rk[:].rearrange("p c t -> p (c t)"), sq[:].rearrange("p c t -> p (c t)"), mh[:],
                                        ALU.pow).then_inc(inv, 1)

        @block.vector
        def _(dve):
            chain = Chain(dve, order)
            flat = lambda a: a.rearrange("p s t -> p (s t)")
            with nc.vector.Fori(0, BATCHES) as b:
                chain.turn(b * LINKS)
                dve.wait_ge(loaded, 64 * b + 64)
                diag = flat(gram[:])[:, SEQ:SEQ + (SEQ - 1) * (2 * SEQ + 1) + 1:2 * SEQ + 1]
                chain.link(nc.vector.tensor_scalar(sq[:, 0, :], diag, L2_EPS, None, ALU.add))
                nc.vector.tensor_scalar(sq[:, 1, :], qn[:], L2_EPS, None, ALU.add).then_inc(sums, 1)
                dve.wait_ge(gates, b + 1)
                chain.link(nc.vector.tensor_tensor(d0[:], m.later[:], gate[:, 1, :].unsqueeze(1).to_broadcast([128, SEQ, SEQ]), ALU.mult))
                dve.wait_ge(inv, b + 2)
                chain.link(nc.vector.tensor_tensor(c[:], gate[:, 0, :], rk[:, 0, :], ALU.mult))
                chain.link(nc.vector.tensor_tensor(d1[:], m.same[:], c[:].unsqueeze(2).to_broadcast([128, SEQ, SEQ]), ALU.mult))
                chain.link(nc.vector.tensor_tensor_scan(flat(e[:]), flat(d0[:]), flat(d1[:]), 0.0, ALU.mult, ALU.add))
                chain.link(nc.vector.tensor_tensor(at[:], e[:], gram[:, :, SEQ:2 * SEQ], ALU.mult))
                chain.link(nc.vector.tensor_tensor(at[:], at[:], rk[:, 0, :].unsqueeze(1).to_broadcast([128, SEQ, SEQ]), ALU.mult))
                chain.link(nc.vector.tensor_tensor(wt[:], e[:], gram[:, :, 0:SEQ], ALU.mult))
                chain.link(nc.vector.tensor_tensor(wt[:], wt[:], rk[:, 1, :].unsqueeze(1).to_broadcast([128, SEQ, SEQ]), ALU.mult))
                for s in range(SEQ - 2, -1, -1):
                    blocks = [(i, max(s + 1, THIRD * i), THIRD * (i + 1)) for i in range(3) if s + 1 < THIRD * (i + 1)]
                    for i, lo, hi in blocks:
                        n, r = hi - lo, hi - (s + 1)
                        prod = tmp[i][:, 0:n * r].rearrange("p (t r) -> p t r", r=r)
                        ins = (nc.vector.tensor_tensor(prod, wt[:, s + 1:hi, lo:hi].rearrange("p r t -> p t r"),
                                                           at[:, s, s + 1:hi].unsqueeze(1).to_broadcast([128, n, r]), ALU.mult))
                    chain.link(ins)
                    for i, lo, hi in blocks:
                        n, r = hi - lo, hi - (s + 1)
                        ins = (nc.vector.tensor_reduce(red[i][:, 0:n], tmp[i][:, 0:n * r].rearrange("p (t r) -> p t r", r=r),
                                                           AX_X, ALU.add))
                    chain.link(ins)
                    for i, lo, hi in blocks:
                        ins = (nc.vector.tensor_tensor(wt[:, s, lo:hi], wt[:, s, lo:hi], red[i][:, 0:hi - lo], ALU.subtract))
                    chain.link(ins)
                dve.wait_ge(w_stored, 16 * b)
                chain.link(nc.vector.tensor_scalar(wo[:, :, 0:SEQ], wt[:], QS, None, ALU.mult))
                nc.vector.scalar_tensor_tensor(wo[:, :, SEQ:2 * SEQ], wt[:], QS, wo[:, :, 0:SEQ], ALU.mult, ALU.subtract).then_inc(mixed, 1)
                assert chain.n == LINKS, chain.n


def phase_mix(nc, m):
    with ExitStack() as own:
        def sem(name):
            return own.enter_context(nc.semaphore(f"m{m.round}_" + name))

        def sb(name, shape, dt):
            return own.enter_context(nc.sbuf_tensor(f"m{m.round}_" + name, shape, dt))

        w_loaded, v_ready, v_act, v_hi, v_lo = sem("w_loaded"), sem("v_ready"), sem("v_act"), sem("v_hi"), sem("v_lo")
        o_ready, o_hi, o_lo = sem("o_ready"), sem("o_hi"), sem("o_lo")
        wo_ready, x2_taken, n_ready, nt_ready, nt_hi, nt_lo = (sem("wo_ready"), sem("x2_taken"), sem("n_ready"),
                                                                sem("nt_ready"), sem("nt_hi"), sem("nt_lo"))
        a_ready, a_act, a_hi, a_lo, y_ready, order = sem("a_ready"), sem("a_act"), sem("a_hi"), sem("a_lo"), sem("y_ready"), sem("order")
        y_taken = sem("y_taken")
        m.var_ready, m.root_ready = sem("var_ready"), sem("root_ready")
        m.roots_per_turn = 2
        vs = sb("vs", [128, 2, 512], F32)
        v_h = [sb(f"v_h{g}", [128, 1024], F16) for g in range(3)]
        v_l = [sb(f"v_l{g}", [128, 1024], F16) for g in range(3)]
        ot_h, ot_l = sb("ot_h", [128, H, UT], F16), sb("ot_l", [128, H, UT], F16)
        x2 = sb("x2", [TT, TPU * D], F32)
        n_tok = sb("n_tok", [TT, TPU, D], F32)
        ht_h, ht_l = sb("ht_h", [128, KD, UT], F16), sb("ht_l", [128, KD, UT], F16)
        a_s = [sb(f"a_s{p}", [128, UT], F32) for p in range(2)]
        at_h, at_l = sb("at_h", [128, F // 128, UT], F16), sb("at_l", [128, F // 128, UT], F16)
        tok_ps = m.ps[0:TT, 4:6, :].rearrange("p b n -> p (b n)")[:, 0:TPU * D]
        nt_ps = m.ps[:, 6:8, 0:UT]
        FC = F // 128
        VH = len(GROUPS) * 2
        LINKS = 9
        block = own.enter_context(nc.Block())

        @block.sync
        def _(sp):
            with nc.sync.Fori(0, UNITS) as u:
                sp.wait_ge(o_ready, H * u)
                settle(sp, o_ready)
                for g, (i0, n) in enumerate(GROUPS):
                    for j in range(n):
                        sp.dma_start(m.wbd[g][SEQ * j:SEQ * (j + 1), :, j, :],
                                     m.w_d[u, i0 + j].rearrange("h s n -> s h n")).then_inc(w_loaded, 16)

        @block.gpsimd
        def _(pool):
            roots(nc, pool, m, UNITS, 2)

        @block.tensor
        def _(pe):
            def values(u):
                for g, (i0, n) in enumerate(GROUPS):
                    rows = n * SEQ
                    for half in range(2):
                        t = 2 * g + half
                        pe.wait_ge(v_act, u * VH + max(t - 1, 0))
                        terms = [x for k in range(KD) for x in passes(
                            m.nt_hi[:, u, k, i0 * SEQ:i0 * SEQ + rows], m.nt_lo[:, u, k, i0 * SEQ:i0 * SEQ + rows],
                            m.wv_hi[:, k * 1024 + half * 512:k * 1024 + half * 512 + 512],
                            m.wv_lo[:, k * 1024 + half * 512:k * 1024 + half * 512 + 512])]
                        for i, (a, b) in enumerate(terms):
                            last = nc.tensor.matmul(m.ps[0:rows, half, :], a, b, start=(i == 0), stop=(i == len(terms) - 1))
                        last.then_inc(v_ready, 1)

            def mix(u, fed):
                pe.wait_ge(w_loaded, 128 * u + 128)
                pe.wait_ge(v_hi, u * VH + VH)
                pe.wait_ge(v_lo, u * VH + VH)
                pe.wait_ge(a_act, fed * FC)
                for h in range(H):
                    pe.wait_ge(o_lo, u * H + max(h - 1, 0))
                    pe.wait_ge(o_hi, u * H + max(h - 1, 0))
                    for g, (i0, n) in enumerate(GROUPS):
                        rows = n * SEQ
                        out = m.ps[:, 2 + h % 2, i0 * SEQ:i0 * SEQ + rows]
                        w = m.wbd[g][0:rows, h, 0:n, :]
                        for i, (a, b) in enumerate(passes(v_h[g][0:rows, h * DK:(h + 1) * DK], v_l[g][0:rows, h * DK:(h + 1) * DK],
                                                          w[:, :, 0:SEQ], w[:, :, SEQ:2 * SEQ])):
                            last = nc.tensor.matmul(out, a, b, start=(i == 0), stop=(i == 2))
                    last.then_inc(o_ready, 1)

            def out_project(u):
                pe.wait_ge(o_hi, u * H + H)
                pe.wait_ge(o_lo, u * H + H)
                pe.wait_ge(y_taken, u)
                for j in range(TPU):
                    terms = [x for h in range(H) for x in passes(
                        ot_h[:, h, j * TT:(j + 1) * TT], ot_l[:, h, j * TT:(j + 1) * TT],
                        m.wo_hi[:, h * D:(h + 1) * D], m.wo_lo[:, h * D:(h + 1) * D])]
                    for i, (a, b) in enumerate(terms):
                        last = nc.tensor.matmul(tok_ps[:, j * D:(j + 1) * D], a, b, start=(i == 0), stop=(i == len(terms) - 1))
                last.then_inc(wo_ready, 1)

            def feed(u, mixed):
                pe.wait_ge(n_ready, u + 1)
                pe.wait_ge(nt_hi, u)
                pe.wait_ge(nt_lo, u)
                for k in range(KD):
                    for j in range(TPU):
                        last = nc.tensor.transpose(nt_ps[:, k, j * TT:(j + 1) * TT], n_tok[:, j, k * 128:(k + 1) * 128],
                                                   m.ident[0:TT, 0:TT])
                last.then_inc(nt_ready, 1)
                pe.wait_ge(nt_hi, u + 1)
                pe.wait_ge(nt_lo, u + 1)
                for f in range(FC):
                    if f == 0:
                        pe.wait_ge(o_hi, mixed * H)
                        pe.wait_ge(o_lo, mixed * H)
                    pe.wait_ge(a_act, u * FC + max(f - 1, 0))
                    terms = [x for k in range(KD) for x in passes(
                        m.w1_hi[:, k * F + f * 128:k * F + f * 128 + 128], m.w1_lo[:, k * F + f * 128:k * F + f * 128 + 128],
                        ht_h[:, k, :], ht_l[:, k, :])]
                    for i, (a, b) in enumerate(terms):
                        last = nc.tensor.matmul(m.ps[:, 2 + f % 2, 0:UT], a, b, start=(i == 0), stop=(i == len(terms) - 1))
                    last.then_inc(a_ready, 1)
                pe.wait_ge(a_hi, u * FC + FC)
                pe.wait_ge(a_lo, u * FC + FC)
                pe.wait_ge(x2_taken, u + 1)
                for j in range(TPU):
                    terms = [x for f in range(FC) for x in passes(
                        at_h[:, f, j * TT:(j + 1) * TT], at_l[:, f, j * TT:(j + 1) * TT],
                        m.w2_hi[:, f * D:(f + 1) * D], m.w2_lo[:, f * D:(f + 1) * D])]
                    for i, (a, b) in enumerate(terms):
                        last = nc.tensor.matmul(tok_ps[:, j * D:(j + 1) * D], a, b, start=(i == 0), stop=(i == len(terms) - 1))
                last.then_inc(y_ready, 1)

            values(0)
            mix(0, 0)
            with nc.tensor.Fori(0, UNITS - 1) as u:
                out_project(u)
                values(u + 1)
                mix(u + 1, u)
                feed(u, u + 2)
            out_project(UNITS - 1)
            feed(UNITS - 1, UNITS)

        @block.scalar
        def _(act):
            def values(u):
                for t in range(VH):
                    g, half = t // 2, t % 2
                    rows = GROUPS[g][1] * SEQ
                    act.wait_ge(v_ready, u * VH + t + 1)
                    act.wait_ge(v_lo, u * VH + max(t - 1, 0))
                    nc.scalar.activation(vs[0:rows, half, :], m.ps[0:rows, half, :], ACT.Silu, scale=1.0 / WS).then_inc(v_act, 1)
                    act.wait_ge(v_act, u * VH + t + 1)
                    if t == 0:
                        act.wait_ge(o_ready, u * H)
                    nc.scalar.activation(v_h[g][0:rows, half * 512:half * 512 + 512], vs[0:rows, half, :], ACT.Copy).then_inc(v_hi, 1)

            def heads(u):
                act.wait_ge(wo_ready, u)
                for h in range(H):
                    act.wait_ge(o_ready, u * H + h + 1)
                    nc.scalar.activation(ot_h[:, h, :], m.ps[:, 2 + h % 2, 0:UT], ACT.Copy, scale=OS / QS).then_inc(o_hi, 1)

            def feed(u):
                act.wait_ge(nt_ready, u + 1)
                act.wait_ge(a_ready, u * FC)
                nc.scalar.activation(ht_h[:], nt_ps, ACT.Copy).then_inc(nt_hi, 1)
                act.wait_ge(y_ready, u)
                for f in range(FC):
                    act.wait_ge(a_ready, u * FC + f + 1)
                    act.wait_ge(a_lo, u * FC + max(f - 1, 0))
                    nc.scalar.activation(a_s[f % 2][:], m.ps[:, 2 + f % 2, 0:UT], ACT.Gelu, scale=1.0 / WS,
                                         bias=m.b1[:, f:f + 1]).then_inc(a_act, 1)
                    act.wait_ge(a_act, u * FC + f + 1)
                    nc.scalar.activation(at_h[:, f, :], a_s[f % 2][:], ACT.Copy).then_inc(a_hi, 1)

            values(0)
            heads(0)
            with nc.scalar.Fori(0, UNITS - 1) as u:
                values(u + 1)
                heads(u + 1)
                feed(u)
            feed(UNITS - 1)

        @block.vector
        def _(dve):
            chain = Chain(dve, order)

            def values(u):
                for t in range(VH):
                    g, half = t // 2, t % 2
                    rows = GROUPS[g][1] * SEQ
                    dve.wait_ge(v_hi, u * VH + t + 1)
                    nc.vector.tensor_tensor(v_l[g][0:rows, half * 512:half * 512 + 512], vs[0:rows, half, :],
                                            v_h[g][0:rows, half * 512:half * 512 + 512], ALU.subtract).then_inc(v_lo, 1)

            def heads(u):
                for h in range(H):
                    dve.wait_ge(o_hi, u * H + h + 1)
                    nc.vector.scalar_tensor_tensor(ot_l[:, h, :], m.ps[:, 2 + h % 2, 0:UT], OS / QS, ot_h[:, h, :],
                                                   ALU.mult, ALU.subtract).then_inc(o_lo, 1)

            def second_norm(u):
                chain.turn(u * LINKS)
                dve.wait_ge(wo_ready, u + 1)
                nc.vector.scalar_tensor_tensor(x2[:], tok_ps, 1.0 / (WS * OS), m.n1[:, u, :], ALU.mult, ALU.add).then_inc(x2_taken, 1)
                dve.wait_ge(x2_taken, u + 1)
                normalise(nc, dve, chain, m, lambda j: x2[:, j * D:(j + 1) * D], lambda j: n_tok[:, j, :], u, 1)
                for j in range(TPU):
                    ins = nc.vector.tensor_tensor(n_tok[:, j, :], n_tok[:, j, :], m.ln2_w[:], ALU.mult)
                chain.link(ins)
                for j in range(TPU):
                    ins = nc.vector.tensor_tensor(n_tok[:, j, :], n_tok[:, j, :], m.ln2_b[:], ALU.add)
                ins.then_inc(n_ready, 1)
                chain.link(nc.vector.tensor_tensor(m.h[:, u, :], m.h[:, u, :], x2[:], ALU.add))
                for j in range(TPU):
                    ins = nc.vector.tensor_tensor(m.h[:, u, j * D:(j + 1) * D], m.h[:, u, j * D:(j + 1) * D], m.b2[:], ALU.add)
                chain.link(ins)

            def feed(u):
                dve.wait_ge(nt_hi, u + 1)
                nc.vector.tensor_tensor(ht_l[:], nt_ps, ht_h[:], ALU.subtract).then_inc(nt_lo, 1)
                for f in range(FC):
                    dve.wait_ge(a_hi, u * FC + f + 1)
                    nc.vector.tensor_tensor(at_l[:, f, :], a_s[f % 2][:], at_h[:, f, :], ALU.subtract).then_inc(a_lo, 1)
                dve.wait_ge(y_ready, u + 1)
                nc.vector.scalar_tensor_tensor(m.h[:, u, :], tok_ps, 1.0 / WS, m.h[:, u, :], ALU.mult, ALU.add).then_inc(y_taken, 1)
                dve.wait_ge(y_taken, u + 1)
                normalise(nc, dve, chain, m, lambda j: m.h[:, u, j * D:(j + 1) * D],
                          lambda j: m.n1[:, u, j * D:(j + 1) * D], u, 2)
                assert chain.n == LINKS, chain.n

            values(0)
            heads(0)
            with nc.vector.Fori(0, UNITS - 1) as u:
                second_norm(u)
                values(u + 1)
                heads(u + 1)
                feed(u)
            second_norm(UNITS - 1)
            feed(UNITS - 1)


RMS_EPS = 1e-6
GATE_EPS = 1e-9
SLOT_TILES = (2 * IMAGES * SEQ + E * 127) // 128
ROWS = SLOT_TILES * 128


def phase_moe(nc, m, last_round):
    sems = m.sems[f"moe{m.round}"]
    with ExitStack() as own:
        def sb(name, shape, dt):
            return own.enter_context(nc.sbuf_tensor(f"e{m.round}_" + name, shape, dt))

        (sq_act, sum_ready, root_ready, zn_ready, zn_copied, zt_ready, zt_hi, zt_lo, zn_used, logit_ready, shifted, exp_ready, order, picked, counted,
         spread_ready, spread_used, listed, places_ready, gathered0, gathered1, gathered2, gathered3, xt_ready, xt_hi, xt_lo,
         up1_ready, up3_ready, silu_ready, g_ready, gt_ready, gt_hi, gt_lo, y_ready, y_taken, scattered0, scattered1,
         back0, back1, half_done, used, base_ready, out_stored, stored0, stored1) = sems
        gathered, scattered, back, zn_stored = [gathered0, gathered1, gathered2, gathered3], [scattered0, scattered1], [back0, back1], [stored0, stored1]
        ss, ssv, rms = sb("ss", [TT, TILES], F32), sb("ssv", [TT, TILES], F32), sb("rms", [TT, TILES], F32)
        wide = [sb(f"wide{i}", [TT, TPU * 2 * D], F32) for i in range(2)]
        stage = [w[:, 0:TPU * D].rearrange("p (j d) -> p j d", d=D) for w in wide]
        yb = [w[:].rearrange("p (j c d) -> p j c d", c=2, d=D) for w in wide]
        scratch = [sb(f"scratch{i}", [TT, D], F32) for i in range(3)]
        zt_h, zt_l = [sb(f"zt_h{i}", [128, KD, UT], F16) for i in range(2)], [sb(f"zt_l{i}", [128, KD, UT], F16) for i in range(2)]
        logit, ex = sb("logit", [TT, TILES, E], F32), sb("ex", [TT, TILES, E], F32)
        top, index = sb("top", [TT, TILES, 8], F32), sb("index", [TT, TILES, 8], U32)
        total, inv, den = sb("total", [TT, TILES], F32), sb("inv", [TT, TILES], F32), sb("den", [TT, TILES], F32)
        score = sb("score", [TT, 2, TILES], F32)
        pick = sb("pick", [TT, TILES, 2], F32)
        mask = [sb(f"mask{c}", [TT, E, TILES], F32) for c in range(2)]
        both = sb("both", [TT, E, TILES], F32)
        counts, running = sb("counts", [TT, E, TILES], F32), sb("running", [TT, E, TILES], F32)
        place, chosen = sb("place", [TT, E, TILES], F32), sb("chosen", [TT, E, TILES], F32)
        slot_f, slot_i = sb("slot_f", [TT, 2, TILES], F32), sb("slot_i", [TT, 2, TILES], U32)
        part_i, row_f, tile_f = sb("part_i", [TT, 2, TILES], U32), sb("row_f", [TT, 2, TILES], F32), sb("tile_f", [TT, 2, TILES], F32)
        TPE = IMAGES * SEQ // 128
        more = sb("more", [TT, E, TPE], F32)
        tiles, upto, before = sb("tiles", [TT, E], F32), sb("upto", [TT, E], F32), sb("before", [TT, E], F32)
        past, tab = sb("past", [1, SLOT_TILES, E], F32), sb("tab", [1, SLOT_TILES], F32)
        table = sb("table", [1, SLOT_TILES], mybir.dt.int32)
        TC = 4
        at_row = [sb(f"at_row{i}", [TT, TC, 128], F32) for i in range(2)]
        at_tile = [sb(f"at_tile{i}", [TT, TC, SLOT_TILES], F32) for i in range(2)]
        who, empty, goes = sb("who", [128, SLOT_TILES], F32), sb("empty", [128, SLOT_TILES], F32), sb("goes", [128, SLOT_TILES], F32)
        token, target = sb("token", [128, SLOT_TILES], U32), sb("target", [128, SLOT_TILES], U32)
        gate = [sb(f"gate{c}", [TT, TILES], F32) for c in range(2)]
        xs = [sb(f"xs{p}", [128, D], F32) for p in range(4)]
        xt_h, xt_l = [sb(f"xt_h{p}", [128, D], F16) for p in range(2)], [sb(f"xt_l{p}", [128, D], F16) for p in range(2)]
        si = [sb(f"si{p}", [128, FE], F32) for p in range(2)]
        g = [sb(f"g{p}", [128, FE], F32) for p in range(2)]
        gt_h, gt_l = sb("gt_h", [128, FE], F16), sb("gt_l", [128, FE], F16)
        ys = [sb(f"ys{p}", [128, D], F32) for p in range(2)]
        Q = SLOT_TILES
        assert Q % 2 == 1
        XT, GT, Y = 4, 5, 6
        log_ps, pre_ps, cnt_ps = m.ps[0:TT, 4, 0:TILES * E], m.ps[0:TT, 5, 0:E * TILES], m.ps[0:TT, 6, 0:E * TILES]
        who_ps = m.ps[:, 7, 0:Q]
        flat = lambda a: a.rearrange("p a b -> p (a b)")
        STEPS = [(c, t) for c in range(2) for t in range(0, TILES, TC)]
        total_out = m.h if last_round else m.n1
        zn_rows = m.zn_d.rearrange("(u j p) d -> u p j d", j=TPU, p=TT)
        y_rows = m.y_d[0:2 * IMAGES * SEQ, :].rearrange("(u j p c) d -> u p j c d", j=TPU, p=TT, c=2)
        block = own.enter_context(nc.Block())

        @block.sync
        def _(sp):
            with nc.sync.Fori(0, UNITS // 2) as i:
                for b in range(2):
                    sp.wait_ge(zn_ready, i * 2 + (b + 1 + ONE))
                    settle(sp, zn_ready)
                    sp.dma_start(zn_rows[i * 2 + b], stage[b]).then_inc(zn_stored[b], 16)
            for p in range(2):
                sp.wait_ge(scattered[p], 16 * ((Q + 1 - p) // 2))
            for u in range(UNITS):
                if u >= 2:
                    sp.wait_ge(used, u - 1 + ONE)
                sp.dma_start(yb[u % 2], y_rows[u]).then_inc(back[u % 2], 16)
            if last_round:
                for u in range(UNITS):
                    sp.wait_ge(used, u + 1 + ONE)
                    sp.dma_start(m.out[u], m.h[:, u, :]).then_inc(out_stored, 16)
                sp.wait_ge(out_stored, 16 * UNITS)

        @block.gpsimd
        def _(pool):
            pool.wait_ge(sum_ready, 1 + ONE)
            nc.gpsimd.tensor_tensor(rms[:], ssv[:], m.minus_half[0:TT, 0:TILES], ALU.pow).then_inc(root_ready, 1)
            if last_round:
                for u in range(UNITS):
                    last = nc.gpsimd.tensor_tensor(m.h[:, u, :], m.h[:, u, :], m.n1[:, u, :], ALU.add)
                last.then_inc(base_ready, 1)
            for b in range(2):
                pool.wait_ge(zn_stored[b], 16 * UNITS // 2)
            pool.wait_ge(places_ready, 1 + ONE)

            def gather(q):
                if q >= 4:
                    pool.wait_ge(xt_ready, q - 3 + ONE)
                nc.gpsimd.indirect_dma_start(xs[q % 4][:], None, m.zn_d,
                                             bass.IndirectOffsetOnAxis(ap=token[:, q:q + 1], axis=0)).then_inc(gathered[q % 4], 16)

            for q in range(4):
                gather(q)
            for q in range(Q):
                pool.wait_ge(y_taken, q + 1 + ONE)
                nc.gpsimd.indirect_dma_start(m.y_d, bass.IndirectOffsetOnAxis(ap=target[:, q:q + 1], axis=0),
                                             ys[q % 2][:], None).then_inc(scattered[q % 2], 16)
                if q + 4 < Q:
                    gather(q + 4)
            for p in range(2):
                pool.wait_ge(scattered[p], 16 * ((Q + 1 - p) // 2))

        def expert_loop(engine, body):
            body(0, 0, None, True, True)
            body(1, 1, None, True, True)
            with engine.Fori(1, (Q - 3) // 2) as i:
                body(i * 2, 0, i, True, True)
                body(i * 2 + 1, 1, i, True, True)
            body(Q - 3, 0, (Q - 3) // 2, True, True)
            body(Q - 2, 1, (Q - 3) // 2, False, True)
            body(Q - 1, 0, (Q - 1) // 2, False, False)

        @block.tensor
        def _(pe):
            def turn_over(u, b):
                pe.wait_ge(zn_ready, u + (1 + ONE))
                for k in range(KD):
                    for j in range(TPU):
                        last = nc.tensor.transpose(m.ps[:, 2 * b + k, j * TT:(j + 1) * TT], stage[b][:, j, k * 128:(k + 1) * 128],
                                                   m.ident[0:TT, 0:TT])
                last.then_inc(zt_ready, 1)

            def logits(u, b):
                pe.wait_ge(zt_hi, u + (1 + ONE))
                pe.wait_ge(zt_lo, u + (1 + ONE))
                for j in range(TPU):
                    terms = [x for k in range(KD) for x in passes(
                        zt_h[b][:, k, j * TT:(j + 1) * TT], zt_l[b][:, k, j * TT:(j + 1) * TT],
                        m.router_hi[:, k * E:(k + 1) * E], m.router_lo[:, k * E:(k + 1) * E])]
                    for i, (x, w) in enumerate(terms):
                        last = nc.tensor.matmul(log_ps[:, (u * TPU + j) * E:(u * TPU + j + 1) * E], x, w,
                                                start=(i == 0), stop=(i == len(terms) - 1))
                last.then_inc(logit_ready, 1)

            turn_over(0, 0)
            for u in range(1, UNITS):
                if u >= 2:
                    pe.wait_ge(zt_lo, u - 1 + ONE)
                    pe.wait_ge(zt_hi, u - 1 + ONE)
                turn_over(u, u % 2)
                logits(u - 1, (u - 1) % 2)
            logits(UNITS - 1, (UNITS - 1) % 2)
            pe.wait_ge(picked, 1 + ONE)
            nc.tensor.matmul(pre_ps, m.earlier[:], flat(both[:]), start=True, stop=True)
            nc.tensor.matmul(cnt_ps, m.all_ones[:], flat(both[:]), start=True, stop=True).then_inc(counted, 1)
            for n, (c, t0) in enumerate(STEPS):
                pe.wait_ge(spread_ready, n + 1 + ONE)
                for t in range(TC):
                    last = nc.tensor.matmul(who_ps, at_row[n % 2][:, t, :], at_tile[n % 2][:, t, :],
                                            start=(n == 0 and t == 0), stop=(n == len(STEPS) - 1 and t == TC - 1))
                last.then_inc(spread_used, 1)

            def expert(q):
                return nc.tensor.value_load(table[0:1, bass.ds(q, 1)], min_val=0, max_val=E - 1)

            def rows_over(q, buf, nth):
                pe.wait_ge(gathered[buf], nth * 16 + 16)
                pe.wait_ge(xt_hi, q + ONE)
                pe.wait_ge(xt_lo, q + ONE)
                for k in range(KD):
                    last = nc.tensor.transpose(m.ps[:, XT, k * 128:(k + 1) * 128], xs[buf][:, k * 128:(k + 1) * 128], m.ident[:])
                last.then_inc(xt_ready, 1)

            def up(q, p, c, e):
                pe.wait_ge(xt_hi, q + (1 + ONE))
                pe.wait_ge(xt_lo, q + (1 + ONE))
                whi, wlo = ((m.e1_hi, m.e1_lo), (m.e3_hi, m.e3_lo))[c]
                n = 0
                for k in range(KD):
                    for x, w in passes(xt_h[p][:, k * 128:(k + 1) * 128], xt_l[p][:, k * 128:(k + 1) * 128], whi, wlo):
                        last = nc.tensor.matmul(m.ps[:, 2 * p + c, :], x, w[:, bass.ds(e * (KD * FE) + k * FE, FE)],
                                                start=(n == 0), stop=(n == 3 * KD - 1))
                        n += 1
                last.then_inc((up1_ready, up3_ready)[c], 1)

            def inner_over(q, p):
                pe.wait_ge(g_ready, q + (1 + ONE))
                pe.wait_ge(gt_hi, q + ONE)
                pe.wait_ge(gt_lo, q + ONE)
                for f in range(FE // 128):
                    last = nc.tensor.transpose(m.ps[:, GT, f * 128:(f + 1) * 128], g[p][:, f * 128:(f + 1) * 128], m.ident[:])
                last.then_inc(gt_ready, 1)

            def down(q, e):
                pe.wait_ge(gt_hi, q + (1 + ONE))
                pe.wait_ge(gt_lo, q + (1 + ONE))
                pe.wait_ge(y_taken, q + ONE)
                n = 0
                for f in range(FE // 128):
                    for x, w in passes(gt_h[:, f * 128:(f + 1) * 128], gt_l[:, f * 128:(f + 1) * 128], m.e2_hi, m.e2_lo):
                        last = nc.tensor.matmul(m.ps[:, Y, 0:D], x, w[:, bass.ds(e * (FE // 128 * D) + f * D, D)],
                                                start=(n == 0), stop=(n == 3 * FE // 128 - 1))
                        n += 1
                last.then_inc(y_ready, 1)

            pe.wait_ge(places_ready, 1 + ONE)
            for q in range(2):
                rows_over(q, q, 0)
            e0 = expert(0)
            up(0, 0, 0, e0)
            up(0, 0, 1, e0)

            def turn(q, p, rows_buf, nth, more_rows, more_up):
                if more_rows:
                    rows_over(q + 2, rows_buf, nth)
                if more_up:
                    e_next = expert(q + 1)
                    up(q + 1, 1 - p, 0, e_next)
                inner_over(q, p)
                if more_up:
                    up(q + 1, 1 - p, 1, e_next)
                down(q, expert(q))

            assert (Q - 3) % 4 == 0
            with nc.tensor.Fori(0, (Q - 3) // 4) as i:
                for r in range(4):
                    turn(i * 4 + r, r % 2, (r + 2) % 4, i + (r + 2) // 4, True, True)
            turn(Q - 3, 0, 2, (Q - 3) // 4, True, True)
            turn(Q - 2, 1, 0, 0, False, True)
            turn(Q - 1, 0, 0, 0, False, False)

        @block.scalar
        def _(act):
            for u in range(UNITS):
                last = nc.scalar.activation(scratch[2][:], m.n1[:, u, 2 * D:3 * D], ACT.Square, accum_out=ss[:, u * TPU + 2:u * TPU + 3])
                last.then_inc(sq_act, 1)
                act.wait_ge(sq_act, u + 1 + ONE)
            for u in range(UNITS):
                act.wait_ge(zt_ready, u + 1 + ONE)
                if u >= 2:
                    act.wait_ge(logit_ready, u - 1 + ONE)
                nc.scalar.activation(zt_h[u % 2][:], m.ps[:, 2 * (u % 2):2 * (u % 2) + 2, 0:UT], ACT.Copy).then_inc(zt_hi, 1)
            act.wait_ge(shifted, 1 + ONE)
            nc.scalar.activation(ex[:], ex[:], ACT.Exp).then_inc(exp_ready, 1)

            def rows_in(q, p):
                act.wait_ge(xt_ready, q + (1 + ONE))
                nc.scalar.activation(xt_h[p][:], m.ps[:, XT, 0:D], ACT.Copy).then_inc(xt_hi, 1)

            def gated(q, p):
                act.wait_ge(up1_ready, q + (1 + ONE))
                nc.scalar.activation(si[p][:], m.ps[:, 2 * p, :], ACT.Silu, scale=1.0 / WS).then_inc(silu_ready, 1)

            def body(q, p, i, more_rows, more_up):
                if more_rows:
                    act.wait_ge(up3_ready, q + (1 + ONE))
                    rows_in(q + 2, p)
                act.wait_ge(gt_ready, q + (1 + ONE))
                act.wait_ge(y_ready, q + ONE)
                nc.scalar.activation(gt_h[:], m.ps[:, GT, :], ACT.Copy).then_inc(gt_hi, 1)
                if more_up:
                    gated(q + 1, 1 - p)

            rows_in(0, 0)
            rows_in(1, 1)
            gated(0, 0)
            expert_loop(nc.scalar, body)

        @block.vector
        def _(dve):
            chain = Chain(dve, order)
            chain.turn(ONE)
            for u in range(UNITS):
                for j in range(2):
                    z = m.n1[:, u, j * D:(j + 1) * D]
                    ins = nc.vector.scalar_tensor_tensor(scratch[j][:], z, 1.0, z, ALU.mult, ALU.mult,
                                                         accum_out=ss[:, u * TPU + j:u * TPU + j + 1])
                chain.link(ins)
            dve.wait_ge(sq_act, UNITS + ONE)
            nc.vector.tensor_scalar(ssv[:], ss[:], 1.0 / D, RMS_EPS, ALU.mult, ALU.add).then_inc(sum_ready, 1)
            dve.wait_ge(root_ready, 1 + ONE)

            def normed(u):
                b = u % 2
                if u >= 2:
                    dve.wait_ge(zt_ready, u - 1 + ONE)
                    dve.wait_ge(zn_stored[b], 16 * (u // 2))
                for j in range(TPU):
                    ins = nc.vector.scalar_tensor_tensor(stage[b][:, j, :], m.n1[:, u, j * D:(j + 1) * D],
                                                         rms[:, u * TPU + j:u * TPU + j + 1], m.norm_w[:], ALU.mult, ALU.mult)
                ins.then_inc(zn_ready, 1)

            normed(0)
            for u in range(UNITS):
                if u + 1 < UNITS:
                    normed(u + 1)
                dve.wait_ge(zt_hi, u + 1 + ONE)
                nc.vector.tensor_tensor(zt_l[u % 2][:], m.ps[:, 2 * (u % 2):2 * (u % 2) + 2, 0:UT], zt_h[u % 2][:], ALU.subtract).then_inc(zt_lo, 1)
            dve.wait_ge(logit_ready, UNITS + ONE)
            chain.link(nc.vector.tensor_scalar(flat(logit[:]), log_ps, 1.0 / WS, None, ALU.mult))
            for t in range(TILES):
                ins = nc.vector.max(top[:, t, :], logit[:, t, :])
            chain.link(ins)
            for t in range(TILES):
                ins = nc.vector.max_index(index[:, t, :], top[:, t, :], logit[:, t, :])
            chain.link(ins)
            chain.link(nc.vector.tensor_copy(pick[:], index[:, :, 0:2]))
            for c in range(2):
                ins = nc.vector.tensor_tensor(mask[c][:], pick[:, :, c].unsqueeze(1).to_broadcast([TT, E, TILES]),
                                              m.expert_no[:].unsqueeze(2).to_broadcast([TT, E, TILES]), ALU.is_equal)
            chain.link(ins)
            nc.vector.tensor_tensor(both[:], mask[0][:], mask[1][:], ALU.add).then_inc(picked, 1)
            nc.vector.tensor_tensor(ex[:], logit[:], top[:, :, 0:1].to_broadcast([TT, TILES, E]), ALU.subtract).then_inc(shifted, 1)
            dve.wait_ge(counted, 1 + ONE)
            chain.link(nc.vector.tensor_copy(flat(counts[:]), cnt_ps))
            chain.link(nc.vector.tensor_tensor_scan(flat(running[:]), flat(m.not_first[:]), flat(counts[:]), 0.0, ALU.mult, ALU.add))
            n_e = running[:, :, TILES - 1]
            chain.link(nc.vector.tensor_tensor(more[:], n_e.unsqueeze(2).to_broadcast([TT, E, TPE]),
                                               m.by128[:].unsqueeze(1).to_broadcast([TT, E, TPE]), ALU.is_gt))
            chain.link(nc.vector.tensor_reduce(tiles[:], more[:], AX_X, ALU.add))
            chain.link(nc.vector.tensor_tensor_scan(upto[:], m.ones_row[:], tiles[:], 0.0, ALU.mult, ALU.add))
            chain.link(nc.vector.tensor_tensor(before[:], upto[:], tiles[:], ALU.subtract))
            chain.link(nc.vector.tensor_scalar(before[:], before[:], 128.0, None, ALU.mult))
            chain.link(nc.vector.tensor_tensor(flat(place[:]), pre_ps, flat(running[:]), ALU.add))
            chain.link(nc.vector.tensor_tensor(place[:], place[:], counts[:], ALU.subtract))
            chain.link(nc.vector.tensor_tensor(place[:], place[:], before[:].unsqueeze(2).to_broadcast([TT, E, TILES]), ALU.add))
            for c in range(2):
                chain.link(nc.vector.tensor_tensor(chosen[:], mask[c][:], place[:], ALU.mult))
                chain.link(nc.vector.tensor_reduce(slot_f[:, c, :], chosen[:].rearrange("p e t -> p t e"), AX_X, ALU.add))
            chain.link(nc.vector.tensor_copy(slot_i[:], slot_f[:]))
            chain.link(nc.vector.tensor_scalar(part_i[:], slot_i[:], 127, None, ALU.bitwise_and))
            chain.link(nc.vector.tensor_copy(row_f[:], part_i[:]))
            chain.link(nc.vector.tensor_scalar(slot_i[:], slot_i[:], 7, None, ALU.logical_shift_right))
            chain.link(nc.vector.tensor_copy(tile_f[:], slot_i[:]))
            for n, (c, t0) in enumerate(STEPS):
                if n >= 2:
                    dve.wait_ge(spread_used, n - 1 + ONE)
                nc.vector.tensor_tensor(at_row[n % 2][:], m.row_no[:].unsqueeze(1).to_broadcast([TT, TC, 128]),
                                        row_f[:, c, t0:t0 + TC].unsqueeze(2).to_broadcast([TT, TC, 128]), ALU.is_equal)
                chain.link(nc.vector.tensor_tensor(at_tile[n % 2][:], m.tile_no[:].unsqueeze(1).to_broadcast([TT, TC, Q]),
                                                   tile_f[:, c, t0:t0 + TC].unsqueeze(2).to_broadcast([TT, TC, Q]), ALU.is_equal))
                nc.vector.tensor_tensor(at_tile[n % 2][:], at_tile[n % 2][:], m.name_of[:, c, t0:t0 + TC].unsqueeze(2).to_broadcast([TT, TC, Q]),
                                        ALU.mult).then_inc(spread_ready, 1)
            shape = [1, SLOT_TILES, E]
            chain.link(nc.vector.tensor_tensor(past[:], m.tile_no[0:1].unsqueeze(2).to_broadcast(shape),
                                               upto[0:1].unsqueeze(1).to_broadcast(shape), ALU.is_ge))
            chain.link(nc.vector.tensor_reduce(tab[:], past[:], AX_X, ALU.add))
            chain.link(nc.vector.tensor_scalar(tab[:], tab[:], float(E - 1), None, ALU.min))
            chain.link(nc.vector.tensor_copy(table[:], tab[:]))
            dve.wait_ge(spread_used, len(STEPS) + ONE)
            chain.link(nc.vector.tensor_copy(who[:], who_ps))
            chain.link(nc.vector.tensor_scalar(empty[:], who[:], 0.0, None, ALU.is_equal))
            chain.link(nc.vector.scalar_tensor_tensor(goes[:], who[:], -1.0, empty[:], ALU.add, ALU.add))
            chain.link(nc.vector.tensor_copy(token[:], goes[:]))
            chain.link(nc.vector.tensor_scalar(token[:], token[:], 1, None, ALU.logical_shift_right))
            chain.link(nc.vector.tensor_tensor(empty[:], empty[:], m.spare_row[:], ALU.mult))
            chain.link(nc.vector.tensor_tensor(goes[:], goes[:], empty[:], ALU.add))
            nc.vector.tensor_copy(target[:], goes[:]).then_inc(places_ready, 1)
            dve.wait_ge(exp_ready, 1 + ONE)
            chain.link(nc.vector.tensor_reduce(total[:], ex[:], AX_X, ALU.add))
            chain.link(nc.vector.reciprocal(inv[:], total[:]))
            for c in range(2):
                chain.link(nc.vector.tensor_tensor(chosen[:].rearrange("p e t -> p t e"), ex[:], mask[c][:].rearrange("p e t -> p t e"), ALU.mult))
                chain.link(nc.vector.tensor_reduce(score[:, c, :], chosen[:].rearrange("p e t -> p t e"), AX_X, ALU.add))
                chain.link(nc.vector.tensor_tensor(score[:, c, :], score[:, c, :], inv[:], ALU.mult))
            chain.link(nc.vector.scalar_tensor_tensor(den[:], score[:, 0, :], GATE_EPS, score[:, 1, :], ALU.add, ALU.add))
            chain.link(nc.vector.reciprocal(den[:], den[:]))
            for c in range(2):
                chain.link(nc.vector.tensor_tensor(gate[c][:], score[:, c, :], den[:], ALU.mult))

            def rows_in(q, p):
                dve.wait_ge(xt_hi, q + (1 + ONE))
                nc.vector.tensor_tensor(xt_l[p][:], m.ps[:, XT, 0:D], xt_h[p][:], ALU.subtract).then_inc(xt_lo, 1)

            def gated(q, p):
                dve.wait_ge(silu_ready, q + (1 + ONE))
                dve.wait_ge(up3_ready, q + (1 + ONE))
                nc.vector.scalar_tensor_tensor(g[p][:], m.ps[:, 2 * p + 1, :], 1.0 / WS, si[p][:], ALU.mult, ALU.mult).then_inc(g_ready, 1)

            def body(q, p, i, more_rows, more_up):
                if more_rows:
                    rows_in(q + 2, p)
                dve.wait_ge(gt_hi, q + (1 + ONE))
                nc.vector.tensor_tensor(gt_l[:], m.ps[:, GT, :], gt_h[:], ALU.subtract).then_inc(gt_lo, 1)
                if more_up:
                    gated(q + 1, 1 - p)
                if i is not None:
                    dve.wait_ge(scattered[p], i * 16)
                dve.wait_ge(y_ready, q + (1 + ONE))
                nc.vector.tensor_scalar(ys[p][:], m.ps[:, Y, 0:D], 1.0 / WS, None, ALU.mult).then_inc(y_taken, 1)

            rows_in(0, 0)
            rows_in(1, 1)
            gated(0, 0)
            expert_loop(nc.vector, body)
            if last_round:
                dve.wait_ge(base_ready, 1 + ONE)
            for u in range(UNITS):
                dve.wait_ge(back[u % 2], 16 * (u // 2 + 1))
                for c in range(2):
                    for j in range(TPU):
                        z = total_out[:, u, j * D:(j + 1) * D]
                        ins = nc.vector.scalar_tensor_tensor(z, yb[u % 2][:, j, c, :], gate[c][:, u * TPU + j:u * TPU + j + 1], z, ALU.mult, ALU.add)
                    if c == 0:
                        chain.link(ins)
                    else:
                        ins.then_inc(used, 1)
            dve.wait_ge(used, UNITS + ONE)


class Memory:
    pass


def build(nc, a, out):
    ctx = ExitStack()
    with ctx:
        m = Memory()
        m.out = out

        def sb(name, shape, dt):
            return ctx.enter_context(nc.sbuf_tensor(name, shape, dt))

        m.x = a["x"]
        m.round = 0
        m.sems = {k: [ctx.enter_context(nc.semaphore(f"{k}_{n}")) for n in names] for k, names in SEMAPHORES.items()}
        m.ps = ctx.enter_context(nc.psum_tensor("ps", [128, 8, 512], F32))
        m.ident, m.minus_half = sb("ident", [128, 128], F32), sb("minus_half", [128, 2 * SEQ], F32)
        m.h, m.n1 = sb("h", [TT, UNITS, TPU * D], F32), sb("n1", [TT, UNITS, TPU * D], F32)
        m.stats, m.mv = sb("stats", [TT, TPU, 6], F32), sb("mv", [TT, TPU, 2], F32)
        m.carry = sb("carry", [TT, 1], F32)
        m.vareps, m.rstd = sb("vareps", [TT, TPU], F32), sb("rstd", [TT, TPU], F32)

        def dram(name, shape, dt):
            return nc.dram_tensor(name, shape, dt, kind="Internal").ap()

        m.gram_d = dram("gram_d", (UNITS, UNIT_IMAGES, H, SEQ, 2 * SEQ), F32)
        m.w_d = dram("w_d", (UNITS, UNIT_IMAGES, H, SEQ, 2 * SEQ), F16)
        m.beta_d, m.alpha_d, m.qn_d = (dram(n, (UNITS, UNIT_IMAGES, H, SEQ), F32) for n in ("beta_d", "alpha_d", "qn_d"))
        batch = "(b v) i h t -> b (v i h) t"
        m.gram_b = m.gram_d.rearrange("(b v) i h s n -> b (v i h) s n", v=2)
        m.w_b = m.w_d.rearrange("(b v) i h s n -> b (v i h) s n", v=2)
        m.beta_b, m.alpha_b, m.qn_b = (t.rearrange(batch, v=2) for t in (m.beta_d, m.alpha_d, m.qn_d))

        with ExitStack() as att:
            def sa(name, shape, dt):
                return att.enter_context(nc.sbuf_tensor(name, shape, dt))

            m.nt_hi, m.nt_lo = sa("nt_hi", [128, UNITS, KD, UT], F16), sa("nt_lo", [128, UNITS, KD, UT], F16)
            m.later, m.same = sa("later", [128, SEQ, SEQ], F32), sa("same", [128, SEQ, SEQ], F32)
            m.head_ones = sa("head_ones", [128, H, H], F32)
            m.wbd = [sa(f"wbd{g}", [SEQ * n, H, n, 2 * SEQ], F16) for g, (_, n) in enumerate(GROUPS)]
            m.qk_hi = [sa(f"qk_hi{p}", [128, 2 * UT + 28], F16) for p in range(2)]
            m.qk_lo = [sa(f"qk_lo{p}", [128, 2 * UT + 28], F16) for p in range(2)]
            jobs, pairs = [], {}
            for name in ("wp", "wq", "wk", "wv", "wba", "wo", "w1", "w2"):
                n = a[name].shape[1]
                pairs[name] = sa(name + "_hi", [128, n], F16), sa(name + "_lo", [128, n], F16)
                jobs.append((a[name], *pairs[name], n))
            m.wp_hi, m.wp_lo = pairs["wp"]
            m.wq_hi, m.wq_lo = pairs["wq"]
            m.wk_hi, m.wk_lo = pairs["wk"]
            m.wv_hi, m.wv_lo = pairs["wv"]
            m.wba_hi, m.wba_lo = pairs["wba"]
            m.wo_hi, m.wo_lo = pairs["wo"]
            m.w1_hi, m.w1_lo = pairs["w1"]
            m.w2_hi, m.w2_lo = pairs["w2"]
            m.pos, m.bproj = sa("pos", [TT, TPU * D], F32), sa("bproj", [TT, TPU * D], F32)
            m.ln1_w, m.ln1_b, m.ln2_w, m.ln2_b, m.b2 = (sa(n, [TT, D], F32) for n in ("ln1_w", "ln1_b", "ln2_w", "ln2_b", "b2"))
            m.b1 = sa("b1", [128, F // 128], F32)
            m.plain = [(m.pos[:], a["pos"]), (m.bproj[:], a["bproj"]), (m.ln1_w[:], a["ln1_w"]), (m.ln1_b[:], a["ln1_b"]),
                       (m.ln2_w[:], a["ln2_w"]), (m.ln2_b[:], a["ln2_b"]), (m.b2[:], a["b2"]), (m.b1[:], a["b1"])]
            m.first = True
            load_weights(nc, ctx, m, jobs)
            phase_tokens(nc, m)
            phase_grams(nc, m)
            phase_solve(nc, m)
            phase_mix(nc, m)
        with ExitStack() as moe:
            def sm(name, shape, dt):
                return moe.enter_context(nc.sbuf_tensor(name, shape, dt))

            m.zn_d, m.y_d = dram("zn_d", (IMAGES * SEQ, D), F32), dram("y_d", (2 * IMAGES * SEQ + ROWS, D), F32)
            jobs, pairs = [], {}
            for name in ("e1", "e3", "e2", "router"):
                n = a[name].shape[1]
                pairs[name] = sm(name + "_hi", [128, n], F16), sm(name + "_lo", [128, n], F16)
                jobs.append((a[name], *pairs[name], n))
            m.e1_hi, m.e1_lo = pairs["e1"]
            m.e3_hi, m.e3_lo = pairs["e3"]
            m.e2_hi, m.e2_lo = pairs["e2"]
            m.router_hi, m.router_lo = pairs["router"]
            m.norm_w = sm("norm_w", [TT, D], F32)
            m.earlier, m.all_ones = sm("earlier", [TT, TT], F32), sm("all_ones", [TT, TT], F32)
            m.expert_no = sm("expert_no", [TT, E], F32)
            m.not_first = sm("not_first", [TT, E, TILES], F32)
            m.by128, m.tile_no, m.ones_row = sm("by128", [TT, IMAGES * SEQ // 128], F32), sm("tile_no", [TT, SLOT_TILES], F32), sm("ones_row", [TT, E], F32)
            m.row_no, m.name_of, m.spare_row = sm("row_no", [TT, 128], F32), sm("name_of", [TT, 2, TILES], F32), sm("spare_row", [128, SLOT_TILES], F32)
            m.plain = [(m.norm_w[:], a["norm_w"])]
            m.first, m.round = False, 1
            load_weights(nc, ctx, m, jobs)
            for m.round in range(1, LOOPS + 1):
                phase_moe(nc, m, m.round == LOOPS)


def kernel(x, L0_tok_W_proj, L0_tok_b_proj, L0_tok_pos_emb, L0_attn_Wq, L0_attn_Wk, L0_attn_Wv, L0_attn_Wb, L0_attn_Wa,
           L0_attn_Wo, L0_attn_ln1_w, L0_attn_ln1_b, L0_attn_ln2_w, L0_attn_ln2_b, L0_attn_W1, L0_attn_b1, L0_attn_W2,
           L0_attn_b2, L0_ffn_norm_w, L0_ffn_router_w, L0_ffn_w1, L0_ffn_w3, L0_ffn_w2):
    import numpy as np
    import concourse.bacc as bacc
    from concourse.bass_utils import run_bass_kernel_spmd

    def rows(w):
        w = np.asarray(w)
        return np.ascontiguousarray(w.reshape(-1, 128, w.shape[1]).transpose(1, 0, 2).reshape(128, -1))

    def experts(w):
        w = np.asarray(w)
        return np.ascontiguousarray(w.reshape(E, -1, 128, w.shape[2]).transpose(2, 0, 1, 3).reshape(128, -1))

    def spread(v, reps=1):
        v = np.asarray(v)
        return np.ascontiguousarray(np.broadcast_to(v, (TT, reps, v.shape[0])).reshape(TT, -1))

    xs = np.asarray(x).reshape(UNITS, UNIT_IMAGES, 6, 16, 6, 48).transpose(0, 3, 5, 1, 2, 4).reshape(UNITS, KP, 128, UT)
    token = (np.arange(TPU)[None, :] * TT + np.arange(TT)[:, None]) % SEQ
    arrays = {
        "x": np.ascontiguousarray(xs.transpose(0, 2, 1, 3)),
        "wp": rows(np.asarray(L0_tok_W_proj).T),
        "pos": np.ascontiguousarray(np.asarray(L0_tok_pos_emb)[token].reshape(TT, TPU * D)),
        "bproj": spread(L0_tok_b_proj, TPU),
        "wq": rows(L0_attn_Wq), "wk": rows(L0_attn_Wk), "wv": rows(L0_attn_Wv),
        "wba": rows(np.concatenate([np.asarray(L0_attn_Wb), np.asarray(L0_attn_Wa)], axis=1)),
        "wo": rows(L0_attn_Wo), "w1": rows(L0_attn_W1), "w2": rows(L0_attn_W2),
        "ln1_w": spread(L0_attn_ln1_w), "ln1_b": spread(L0_attn_ln1_b),
        "ln2_w": spread(L0_attn_ln2_w), "ln2_b": spread(L0_attn_ln2_b), "b2": spread(L0_attn_b2),
        "e1": experts(L0_ffn_w1), "e3": experts(L0_ffn_w3), "e2": experts(L0_ffn_w2),
        "router": rows(L0_ffn_router_w), "norm_w": spread(L0_ffn_norm_w),
        "b1": np.ascontiguousarray(np.asarray(L0_attn_b1).reshape(-1, 128).T),
    }
    nc = bacc.Bacc("TRN2", target_bir_lowering=False, num_devices=1)
    aps = {k: nc.dram_tensor(k + "_dram", v.shape, mybir.dt.from_np(v.dtype), kind="ExternalInput").ap() for k, v in arrays.items()}
    out = nc.dram_tensor("out_dram", (UNITS, TT, TPU * D), F32, kind="ExternalOutput").ap()
    build(nc, aps, out)
    r = run_bass_kernel_spmd(nc, [{k + "_dram": v for k, v in arrays.items()}], core_ids=[0])
    y = np.asarray(r.results[0]["out_dram"])
    return y.reshape(UNITS, TT, TPU, D).transpose(0, 2, 1, 3).reshape(IMAGES, SEQ, D)
```

```python
from contextlib import ExitStack

import concourse.bass as bass
from concourse import mybir

ALU = mybir.AluOpType
ACT = mybir.ActivationFunctionType
F32 = mybir.dt.float32
F16 = mybir.dt.float16
U32 = mybir.dt.uint32
AX_X = mybir.AxisListType.X

IMAGES = 64
SEQ = 36
D = 256
PATCH = 768
H, DK = 8, 128
F = 1024
E, FE = 8, 512
UNIT_IMAGES = 8
UNITS = IMAGES // UNIT_IMAGES
UT = UNIT_IMAGES * SEQ
TPU = 3
TT = UT // TPU
TILES = UNITS * TPU
KD = D // 128
KP = PATCH // 128
BATCH_IMAGES = 128 // H
BATCHES = IMAGES // BATCH_IMAGES
GROUPS = [(0, 3), (3, 3), (6, 2)]
EPS = 1e-5
LOOPS = 2
L2_EPS = 1e-6
WS = 64.0
OS = 16.0
WCOLS = KD * H * DK
WALL = 6 * WCOLS
QS = 256.0


ONE = 1
DMA_SEMAPHORES = ("gathered", "scattered", "back", "stored", "out_stored", "small_stored", "w_stored", "w_loaded", "x_loaded", "loaded")
SEMAPHORES = {
    "grams": """qk_ready qk_act qk_hi qk_lo sq_ready sq_used gram_ready gram_taken logits_ready gates_taken norms_taken
        sums_turned sums inv masks order built mixed w_free stored0 stored1 small_stored loaded w_stored""".split(),
    "tokens": """x_loaded x_hi x_lo tok_ready tok_taken var_ready root_ready n_ready nt_ready nt_hi nt_lo order
        w_hi w_lo w_loaded""".split(),
    "mix": """w_loaded v_ready v_act v_hi v_lo o_ready o_hi o_lo wo_ready x2_taken n_ready nt_ready nt_hi nt_lo
        a_ready a_act a_hi a_lo y_ready y_taken order var_ready root_ready made""".split(),
    "weights": "hi_done lo_done consts made loaded0 loaded1".split(),
}
for round_no in range(1, LOOPS + 1):
    SEMAPHORES[f"moe{round_no}"] = """sq_act sum_ready root_ready zn_ready zt_ready zt_hi zt_lo logit_ready shifted exp_ready
        order picked counted spread_ready spread_used places_ready gathered0 gathered1 gathered2 gathered3 xt_ready xt_hi
        xt_lo up1_ready up3_ready silu_ready g_ready gt_ready gt_hi gt_lo y_ready y_taken scattered0 scattered1 back0 back1
        used stored0 stored1""".split()
SEMAPHORES[f"moe{LOOPS}"] += ["base_ready", "out_stored"]
SEMAPHORES["moe1"] += "w_split w_lo w_loaded0 w_loaded1 w_loaded2".split()


class Chain:

    def __init__(self, engine, sem):
        self.engine, self.sem, self.base, self.n = engine, sem, 0, 0

    def turn(self, base):
        self.base, self.n = base, 0

    def link(self, ins):
        self.n += 1
        ins.then_inc(self.sem, 1)
        self.engine.wait_ge(self.sem, self.base + self.n)

    def behind(self, ins):
        self.n += 1
        ins.then_inc(self.sem, 1)
        self.engine.wait_ge(self.sem, self.base + self.n - 1)


def settle(engine, sem):
    engine.wait_ge(sem, 0)


def passes(hi_a, lo_a, hi_b, lo_b):
    return [(hi_a, hi_b), (lo_a, hi_b), (hi_a, lo_b)]


def load_weights(nc, m, jobs):
    with ExitStack() as own:
        hi_done, lo_done, consts, made, *loaded = m.sems["weights"]
        S = len(loaded)
        stage = [own.enter_context(nc.sbuf_tensor(f"w_stage{i}", [128, 2048], F32)) for i in range(S)]
        pieces = []
        for src, hi, lo, n in jobs:
            for a in range(0, n, 2048):
                b = min(n, a + 2048)
                pieces.append((src[:, a:b], hi[:, a:b], lo[:, a:b], b - a))
        block = own.enter_context(nc.Block())

        @block.sync
        def _(sp):
            def bring(t):
                src, _, _, n = pieces[t]
                if t >= S:
                    sp.wait_ge(lo_done, t - S + 1)
                sp.dma_start(stage[t % S][:, 0:n], src).then_inc(loaded[t % S], 16)

            bring(0)
            for phase, names in SEMAPHORES.items():
                for name, s in zip(names, m.sems[phase]):
                    if phase != "weights" and not name.startswith(DMA_SEMAPHORES):
                        sp.sem_inc(s, ONE)
            for dst, src in m.plain:
                sp.dma_start(dst, src).then_inc(consts, 16)
            for t in range(1, len(pieces)):
                bring(t)
            sp.wait_ge(consts, 16 * len(m.plain))

        @block.scalar
        def _(act):
            for t, (_, hi, _, n) in enumerate(pieces):
                act.wait_ge(loaded[t % S], 16 * (t // S + 1))
                nc.scalar.activation(hi, stage[t % S][:, 0:n], ACT.Copy, scale=WS).then_inc(hi_done, 1)

        @block.vector
        def _(dve):
            for t, (_, hi, lo, n) in enumerate(pieces):
                dve.wait_ge(hi_done, t + 1)
                nc.vector.scalar_tensor_tensor(lo, stage[t % S][:, 0:n], WS, hi, ALU.mult, ALU.subtract).then_inc(lo_done, 1)
            dve.wait_ge(lo_done, len(pieces))

        @block.gpsimd
        def _(pool):
            nc.gpsimd.memset(m.ident[:], 0.0).then_inc(made, 1)
            nc.gpsimd.memset(m.ones[:], 1.0).then_inc(made, 1)
            nc.gpsimd.memset(m.minus_half[:], -0.5).then_inc(made, 1)
            pool.wait_ge(made, 3)
            nc.gpsimd.affine_select(out=m.ident[:], in_=m.ident[:], compare_op=ALU.not_equal, fill=1.0,
                                    base=0, pattern=[[-1, 128]], channel_multiplier=1).then_inc(made, 1)
            pool.wait_ge(made, 4)
            for g in range(3):
                nc.gpsimd.memset(m.wbd[g][:], 0.0).then_inc(made, 1)
            for p in range(2):
                nc.gpsimd.memset(m.qk_hi[p][:], 0.0).then_inc(made, 1)
                nc.gpsimd.memset(m.qk_lo[p][:], 0.0).then_inc(made, 1)
            pool.wait_ge(made, 11)


def route_constants(nc, pool, m, made):
    nc.gpsimd.memset(m.earlier[:], 1.0).then_inc(made, 1)
    nc.gpsimd.memset(m.all_ones[:], 1.0).then_inc(made, 1)
    nc.gpsimd.memset(m.not_first[:], 1.0).then_inc(made, 1)
    nc.gpsimd.memset(m.ones_row[:], 1.0).then_inc(made, 1)
    exact = dict(allow_small_or_imprecise_dtypes=True)
    nc.gpsimd.iota(m.expert_no[:], [[1, E]], base=0, channel_multiplier=0, **exact).then_inc(made, 1)
    nc.gpsimd.iota(m.by128[:], [[128, IMAGES * SEQ // 128]], base=0, channel_multiplier=0, **exact).then_inc(made, 1)
    nc.gpsimd.iota(m.tile_no[:], [[1, SLOT_TILES]], base=0, channel_multiplier=0, **exact).then_inc(made, 1)
    nc.gpsimd.iota(m.row_no[:], [[1, 128]], base=0, channel_multiplier=0, **exact).then_inc(made, 1)
    nc.gpsimd.iota(m.name_of[:], [[1, 2], [2 * TT, TILES]], base=1, channel_multiplier=2, **exact).then_inc(made, 1)
    nc.gpsimd.iota(m.spare_row[:], [[128, SLOT_TILES]], base=2 * IMAGES * SEQ, channel_multiplier=1, **exact).then_inc(made, 1)
    pool.wait_ge(made, 10 + ONE)
    nc.gpsimd.affine_select(out=m.earlier[:], in_=m.earlier[:], compare_op=ALU.is_gt, fill=0.0, base=0,
                            pattern=[[1, TT]], channel_multiplier=-1).then_inc(made, 1)
    nc.gpsimd.affine_select(out=m.not_first[:], in_=m.not_first[:], compare_op=ALU.is_gt, fill=0.0, base=0,
                            pattern=[[0, E], [1, TILES]], channel_multiplier=0).then_inc(made, 1)
    pool.wait_ge(made, 12 + ONE)


def normalise(nc, dve, chain, m, src, dst, turn, k):
    nc.vector.memset(m.carry[:], 0.0)
    for j in range(TPU):
        ins = nc.vector.bn_stats(m.stats[:, j, :], src(j))
    chain.link(ins)
    nc.vector.memset(m.carry[:], 0.0)
    for j in range(TPU):
        ins = nc.vector.bn_aggr(m.mv[:, j, :], m.stats[:, j, :])
    chain.link(ins)
    nc.vector.tensor_scalar(m.vareps[:], m.mv[:, :, 1], EPS, None, ALU.add).then_inc(m.var_ready, 1)
    dve.wait_ge(m.root_ready, ONE + turn * m.roots_per_turn + k)
    for j in range(TPU):
        ins = nc.vector.tensor_scalar(dst(j), src(j), m.mv[:, j, 0:1], m.rstd[:, j:j + 1], ALU.subtract, ALU.mult)
    chain.link(ins)


def unit_roots(nc, pool, m, u, per_unit):
    for k in range(per_unit):
        pool.wait_ge(m.var_ready, ONE + u * per_unit + (k + 1))
        nc.gpsimd.tensor_tensor(m.rstd[0:TT, :], m.vareps[0:TT, :], m.minus_half[0:TT, 0:TPU], ALU.pow).then_inc(m.root_ready, 1)


def phase_tokens(nc, m):
    with ExitStack() as own:
        def sb(name, shape, dt):
            return own.enter_context(nc.sbuf_tensor("t_" + name, shape, dt))

        (x_loaded, x_hi, x_lo, tok_ready, tok_taken, m.var_ready, m.root_ready, n_ready, nt_ready, nt_hi, nt_lo,
         order, w_hi, w_lo, w_loaded) = m.sems["tokens"]
        xin = sb("xin", [128, KP, UT], F32)
        xh, xl = ([sb(f"{n}{p}", [128, KP, UT], F16) for p in range(2)] for n in ("xh", "xl"))
        n_tok = sb("n_tok", [TT, TPU, D], F32)
        piece = sb("piece", [128, WALL // UNITS], F32)
        tok_ps = [m.ps[0:TT, 2 * p:2 * p + 2, :].rearrange("p b n -> p (b n)")[:, 0:TPU * D] for p in range(2)]
        nt_ps = m.ps[:, 4:6, 0:UT]
        LINKS = 8
        m.roots_per_turn = 2

        def all_but_last(engine, body):
            with engine.Fori(0, (UNITS - 2) // 2) as i:
                body(2 * i, 0)
                body(2 * i + 1, 1)
            body(UNITS - 2, 0)

        assert UNITS % 2 == 0
        block = own.enter_context(nc.Block())

        @block.sync
        def _(sp):
            sp.dma_start(xin[:], m.x[0]).then_inc(x_loaded, 16)
            with nc.sync.Fori(1, UNITS) as u:
                sp.wait_ge(x_hi, ONE + u)
                sp.wait_ge(x_lo, ONE + u)
                settle(sp, x_lo)
                sp.dma_start(xin[:], m.x[u]).then_inc(x_loaded, 16)

        @block.scalar
        def _(act):
            def split_x(u, p):
                act.wait_ge(x_loaded, 16 * u + 16)
                if not isinstance(u, int) or u > 1:
                    act.wait_ge(tok_ready, u + (ONE - 1))
                nc.scalar.activation(xh[p][:], xin[:], ACT.Copy).then_inc(x_hi, 1)

            def split_nt(u):
                act.wait_ge(nt_ready, ONE + u + 1)
                nc.scalar.activation(m.nt_hi[:, u, :, :], nt_ps, ACT.Copy).then_inc(nt_hi, 1)

            def weights(u):
                act.wait_ge(w_loaded, 16 * u + 16)
                nc.scalar.activation(m.wall_hi[:, u, :], piece[:], ACT.Copy, scale=WS).then_inc(w_hi, 1)

            def body(u, p):
                split_x(u + 1, 1 - p)
                weights(u)
                split_nt(u)
                act.wait_ge(w_lo, ONE + u + 1)
                act.dma_start(piece[:], m.wall[u + 1]).then_inc(w_loaded, 16)

            split_x(0, 0)
            act.dma_start(piece[:], m.wall[0]).then_inc(w_loaded, 16)
            all_but_last(nc.scalar, body)
            weights(UNITS - 1)
            split_nt(UNITS - 1)

        @block.gpsimd
        def _(pool):
            def split_x(u, p):
                pool.wait_ge(x_hi, ONE + u + 1)
                nc.gpsimd.tensor_tensor(xl[p][:], xin[:], xh[p][:], ALU.subtract).then_inc(x_lo, 1)

            def body(u, p):
                split_x(u + 1, 1 - p)
                unit_roots(nc, pool, m, u, 2)

            split_x(0, 0)
            all_but_last(nc.gpsimd, body)
            unit_roots(nc, pool, m, UNITS - 1, 2)

        @block.tensor
        def _(pe):
            def project(u, p):
                pe.wait_ge(x_hi, ONE + u + 1)
                pe.wait_ge(x_lo, ONE + u + 1)
                if not isinstance(u, int) or u > 0:
                    pe.wait_ge(tok_taken, u + (ONE - 1))
                for j in range(TPU):
                    terms = [t for k in range(KP) for t in passes(
                        xh[p][:, k, j * TT:(j + 1) * TT], xl[p][:, k, j * TT:(j + 1) * TT],
                        m.wp_hi[:, k * D:(k + 1) * D], m.wp_lo[:, k * D:(k + 1) * D])]
                    for i, (a, b) in enumerate(terms):
                        last = nc.tensor.matmul(tok_ps[p][:, j * D:(j + 1) * D], a, b, start=(i == 0), stop=(i == len(terms) - 1))
                last.then_inc(tok_ready, 1)

            def turn_over(u):
                pe.wait_ge(n_ready, ONE + u + 1)
                pe.wait_ge(nt_hi, ONE + u)
                pe.wait_ge(nt_lo, ONE + u)
                for k in range(KD):
                    for j in range(TPU):
                        last = nc.tensor.transpose(nt_ps[:, k, j * TT:(j + 1) * TT], n_tok[:, j, k * 128:(k + 1) * 128],
                                                   m.ident[0:TT, 0:TT])
                last.then_inc(nt_ready, 1)

            def body(u, p):
                project(u + 1, 1 - p)
                turn_over(u)

            project(0, 0)
            all_but_last(nc.tensor, body)
            turn_over(UNITS - 1)

        @block.vector
        def _(dve):
            chain = Chain(dve, order)

            def norms(u, p):
                chain.turn(ONE + u * LINKS)
                dve.wait_ge(tok_ready, ONE + u + 1)
                nc.vector.scalar_tensor_tensor(m.h[:, u, :], tok_ps[p], 1.0 / WS, m.pos[:], ALU.mult, ALU.add).then_inc(tok_taken, 1)
                dve.wait_ge(tok_taken, ONE + u + 1)
                hv = lambda j: m.h[:, u, j * D:(j + 1) * D]
                nv = lambda j: m.n1[:, u, j * D:(j + 1) * D]
                chain.link(nc.vector.tensor_tensor(m.h[:, u, :], m.h[:, u, :], m.bproj[:], ALU.add))
                normalise(nc, dve, chain, m, hv, nv, u, 1)
                dve.wait_ge(nt_ready, ONE + u)
                normalise(nc, dve, chain, m, nv, lambda j: n_tok[:, j, :], u, 2)
                for j in range(TPU):
                    ins = nc.vector.tensor_tensor(n_tok[:, j, :], n_tok[:, j, :], m.ln1_w[:], ALU.mult)
                chain.link(ins)
                for j in range(TPU):
                    ins = nc.vector.tensor_tensor(n_tok[:, j, :], n_tok[:, j, :], m.ln1_b[:], ALU.add)
                ins.then_inc(n_ready, 1)
                assert chain.n == LINKS, chain.n

            def split_nt(u):
                dve.wait_ge(nt_hi, ONE + u + 1)
                nc.vector.tensor_tensor(m.nt_lo[:, u, :, :], nt_ps, m.nt_hi[:, u, :, :], ALU.subtract).then_inc(nt_lo, 1)

            def weights(u):
                dve.wait_ge(w_hi, ONE + u + 1)
                nc.vector.scalar_tensor_tensor(m.wall_lo[:, u, :], piece[:], WS, m.wall_hi[:, u, :], ALU.mult,
                                               ALU.subtract).then_inc(w_lo, 1)

            def body(u, p):
                norms(u, p)
                weights(u)
                split_nt(u)

            all_but_last(nc.vector, body)
            norms(UNITS - 1, 1)
            weights(UNITS - 1)
            split_nt(UNITS - 1)
            dve.wait_ge(w_lo, ONE + UNITS)


def phase_grams(nc, m):
    (qk_ready, qk_act, qk_hi, qk_lo, sq_ready, sq_used, gram_ready, gram_taken, logits_ready, gates_taken,
     norms_taken, sums_turned, sums, inv, masks, order, built, mixed, w_free, stored0, stored1, small_stored, loaded, w_stored) = m.sems["grams"]
    stored = [stored0, stored1]
    with ExitStack() as own:
        def sb(name, shape, dt):
            return own.enter_context(nc.sbuf_tensor("g_" + name, shape, dt))

        qks = [sb(f"qks{p}", [128, 2, UT], F32) for p in range(2)]
        sq = [sb(f"sq{p}", [128, UT], F32) for p in range(2)]
        gsb = [sb(f"gsb{p}", [128, 4, UNIT_IMAGES // 2, 2 * SEQ], F32) for p in range(2)]
        PAIRS = UNIT_IMAGES // 2
        sums_sb, qn_sb = sb("sums_sb", [2 * SEQ, PAIRS * H], F32), sb("qn_sb", [PAIRS * H, 2 * SEQ], F32)
        sum_ps, turned_ps = m.ps[0:2 * SEQ, 7, 0:PAIRS * H], m.ps[0:PAIRS * H, 7, 64:64 + 2 * SEQ]
        ba_sb = sb("ba_sb", [2 * H, UT], F32)
        gram = sb("gram", [128, SEQ, 2 * SEQ], F32)
        gate = sb("gate", [128, 2, SEQ], F32)
        qn, norm2, rk = sb("qn", [128, SEQ], F32), sb("norm2", [128, 2, SEQ], F32), sb("rk", [128, 2, SEQ], F32)
        beta_k = sb("beta_k", [128, SEQ], F32)
        pool_carry = sb("pool_carry", [128, 1], F32)
        decay = sb("decay", [128, SEQ, SEQ], F32)
        mask_alpha, mask_beta = sb("mask_alpha", [128, SEQ, SEQ], F32), sb("mask_beta", [128, SEQ, SEQ], F32)
        at, wt = mask_alpha, mask_beta
        prod = [sb(f"prod{i}", [128, SEQ * SEQ // 8 + SEQ], F32) for i in range(2)]
        w_out = sb("w_out", [128, SEQ, 2 * SEQ], F16)
        SMALL = 2 + PAIRS
        SLOTS = 2 * H
        LOADED, BUILD = 3, 7
        LINKS = 4 + 4 * (SEQ - 2) + 2 + 1

        def before(base, n):
            return ONE if isinstance(base, int) and base + n == 0 else base + (n - 1 + ONE)

        block = own.enter_context(nc.Block())

        @block.tensor
        def _(pe):
            def project(u, h):
                p = h % 2
                pe.wait_ge(qk_act, before(u * H, h))
                for c, (whi, wlo) in enumerate([(m.wq_hi, m.wq_lo), (m.wk_hi, m.wk_lo)]):
                    terms = [t for k in range(KD) for t in passes(
                        whi[:, k * H * DK + h * DK:k * H * DK + (h + 1) * DK],
                        wlo[:, k * H * DK + h * DK:k * H * DK + (h + 1) * DK],
                        m.nt_hi[:, u, k, :], m.nt_lo[:, u, k, :])]
                    for i, (a, b) in enumerate(terms):
                        last = nc.tensor.matmul(m.ps[:, 2 * p + c, 0:UT], a, b, start=(i == 0), stop=(i == len(terms) - 1))
                last.then_inc(qk_ready, 1)

            def products(u, h):
                p = h % 2
                qh, ql = m.qk_hi[p], m.qk_lo[p]
                pe.wait_ge(qk_hi, ONE + u * H + h + 1)
                pe.wait_ge(qk_lo, ONE + u * H + h + 1)
                pe.wait_ge(gram_taken, before(u * H, h))
                for i in range(UNIT_IMAGES):
                    out = m.ps[64 * (i % 2):64 * (i % 2) + 64, 4 + p, (i // 2) * 72:(i // 2) * 72 + 72]
                    k0 = UT + i * SEQ
                    kh, kl = qh[:, k0:k0 + 64], ql[:, k0:k0 + 64]
                    rh = qh[:, 0:2 * UT].rearrange("p (c t) -> p c t", c=2)[:, :, i * SEQ:(i + 1) * SEQ]
                    rl = ql[:, 0:2 * UT].rearrange("p (c t) -> p c t", c=2)[:, :, i * SEQ:(i + 1) * SEQ]
                    for n, (a, b) in enumerate(passes(kh, kl, rh, rl)):
                        last = nc.tensor.matmul(out, a, b, start=(n == 0), stop=(n == 2))
                last.then_inc(gram_ready, 1)
                pe.wait_ge(sq_ready, ONE + u * H + h + 1)
                if h == 0:
                    pe.wait_ge(norms_taken, ONE + 2 * u)
                for j in range(PAIRS):
                    last = nc.tensor.matmul(sum_ps[:, j * H + h:j * H + h + 1], sq[p][:, j * 2 * SEQ:(j + 1) * 2 * SEQ], m.ones[:],
                                            start=True, stop=True)
                last.then_inc(sq_used, 1)

            def turn_sums(u):
                pe.wait_ge(norms_taken, ONE + 2 * u + 1)
                nc.tensor.transpose(turned_ps, sums_sb[:], m.ident[0:2 * SEQ, 0:2 * SEQ]).then_inc(sums_turned, 1)

            def logits(u):
                terms = [t for k in range(KD) for t in passes(
                    m.wba_hi[:, k * 16:(k + 1) * 16], m.wba_lo[:, k * 16:(k + 1) * 16],
                    m.nt_hi[:, u, k, :], m.nt_lo[:, u, k, :])]
                for i, (a, b) in enumerate(terms):
                    last = nc.tensor.matmul(m.ps[0:2 * H, 6, 0:UT], a, b, start=(i == 0), stop=(i == len(terms) - 1))
                last.then_inc(logits_ready, 1)

            def unit(u, last):
                for h in range(H):
                    if h + 2 < H:
                        project(u, h + 2)
                    elif not last:
                        project(u + 1, h + 2 - H)
                    if h == H - 1:
                        pe.wait_ge(gates_taken, ONE + u + 1)
                    products(u, h)
                if not last:
                    logits(u + 1)
                turn_sums(u)

            logits(0)
            project(0, 0)
            project(0, 1)
            with nc.tensor.Fori(0, UNITS - 1) as u:
                unit(u, False)
            unit(UNITS - 1, True)

        @block.scalar
        def _(act):
            def take(u, h, first):
                if h % 4 == 0 and not first:
                    act.wait_ge(stored[h // 4], u * 128)
                act.wait_ge(gram_ready, ONE + u * H + h + 1)
                nc.scalar.activation(gsb[h // 4][:, h % 4, :, :].rearrange("p c n -> p (c n)"),
                                     m.ps[:, 4 + h % 2, 0:PAIRS * 72], ACT.Copy).then_inc(gram_taken, 1)

            def head(u, h):
                p = h % 2
                act.wait_ge(qk_ready, ONE + u * H + h + 1)
                act.wait_ge(qk_lo, before(u * H, h))
                nc.scalar.activation(qks[p][:], m.ps[:, 2 * p:2 * p + 2, 0:UT], ACT.Silu, scale=1.0 / WS).then_inc(qk_act, 1)
                act.wait_ge(qk_act, ONE + u * H + h + 1)
                act.wait_ge(gram_ready, before(u * H, h))
                nc.scalar.activation(m.qk_hi[p][:, 0:2 * UT].rearrange("p (c t) -> p c t", c=2), qks[p][:], ACT.Copy).then_inc(qk_hi, 1)
                act.wait_ge(sq_used, before(u * H, h))
                nc.scalar.activation(sq[p][:], qks[p][:, 0, :], ACT.Square).then_inc(sq_ready, 1)

            def gates(u, first):
                if not first:
                    act.wait_ge(small_stored, u * 16 * SMALL)
                act.wait_ge(logits_ready, ONE + u + 1)
                nc.scalar.activation(ba_sb[:], m.ps[0:2 * H, 6, 0:UT], ACT.Sigmoid, scale=1.0 / WS).then_inc(gates_taken, 1)

            def unit(u, first, last):
                for h in range(H):
                    if h + 2 < H:
                        head(u, h + 2)
                    elif not last:
                        head(u + 1, h + 2 - H)
                    if h == H // 2:
                        gates(u, first)
                    take(u, h, first)
                act.wait_ge(sq_used, ONE + u * H + H)
                nc.scalar.activation(sums_sb[:], sum_ps, ACT.Copy).then_inc(norms_taken, 1)
                act.wait_ge(sums_turned, ONE + u + 1)
                nc.scalar.activation(qn_sb[:], turned_ps, ACT.Copy).then_inc(norms_taken, 1)

            head(0, 0)
            head(0, 1)
            unit(0, True, False)
            with nc.scalar.Fori(1, UNITS - 1) as u:
                unit(u, False, False)
            unit(UNITS - 1, False, True)

        @block.gpsimd
        def _(pool):
            def decays(b):
                pool.wait_ge(loaded, 64 * b + 64)
                pool.wait_ge(mixed, ONE + b)
                nc.gpsimd.tensor_tensor(pool_carry[:], m.minus_half[:, 0:1], m.minus_half[:, 0:1], ALU.mult)
                nc.gpsimd.affine_select(out=mask_alpha[:], in_=gate[:, 1, :].unsqueeze(1).to_broadcast([128, SEQ, SEQ]),
                                        compare_op=ALU.is_gt, fill=0.0, base=0, pattern=[[-1, SEQ], [1, SEQ]],
                                        channel_multiplier=0).then_inc(masks, 1)

            def inverse_root(b, c):
                nc.gpsimd.tensor_tensor(rk[:, c, :], norm2[:, c, :], m.minus_half[:, 0:SEQ], ALU.pow).then_inc(inv, 1)

            with nc.gpsimd.Fori(0, BATCHES) as b:
                decays(b)
                pool.wait_ge(sums, ONE + b + 1)
                inverse_root(b, 0)
                pool.wait_ge(inv, ONE + 3 * b + 1)
                nc.gpsimd.tensor_tensor(beta_k[:], gate[:, 0, :], rk[:, 0, :], ALU.mult).then_inc(inv, 1)
                pool.wait_ge(inv, ONE + 3 * b + 2)
                nc.gpsimd.tensor_tensor(pool_carry[:], m.minus_half[:, 0:1], m.minus_half[:, 0:1], ALU.mult)
                nc.gpsimd.affine_select(out=mask_beta[:], in_=beta_k[:].unsqueeze(2).to_broadcast([128, SEQ, SEQ]),
                                        compare_op=ALU.is_equal, fill=0.0, base=0, pattern=[[-1, SEQ], [1, SEQ]],
                                        channel_multiplier=0).then_inc(masks, 1)
                kk = gram[:, :, SEQ:2 * SEQ]
                nc.gpsimd.tensor_tensor(kk, kk, rk[:, 0, :].unsqueeze(1).to_broadcast([128, SEQ, SEQ]), ALU.mult).then_inc(masks, 1)
                inverse_root(b, 1)

        @block.vector
        def _(dve):
            chain = Chain(dve, order)
            flat = lambda a: a.rearrange("p s t -> p (s t)")

            def low(b, slot):
                n, h, p = b * SLOTS + slot, slot % H, slot % 2
                dve.wait_ge(qk_hi, ONE + n + 1)
                dve.wait_ge(gram_ready, before(b * SLOTS, slot))
                nc.vector.tensor_tensor(m.qk_lo[p][:, 0:2 * UT].rearrange("p (c t) -> p c t", c=2), qks[p][:],
                                        m.qk_hi[p][:, 0:2 * UT].rearrange("p (c t) -> p c t", c=2), ALU.subtract).then_inc(qk_lo, 1)

            def squares(b):
                chain.turn(ONE + b * LINKS)
                dve.wait_ge(loaded, 64 * b + 64)
                diag = flat(gram[:])[:, SEQ:SEQ + (SEQ - 1) * (2 * SEQ + 1) + 1:2 * SEQ + 1]
                chain.link(nc.vector.tensor_scalar(norm2[:, 0, :], diag, L2_EPS, None, ALU.add))
                nc.vector.tensor_scalar(norm2[:, 1, :], qn[:], L2_EPS, None, ALU.add).then_inc(sums, 1)

            def matrices(b):
                dve.wait_ge(masks, ONE + 3 * b + 2)
                chain.link(nc.vector.tensor_tensor_scan(flat(decay[:]), flat(mask_alpha[:]), flat(mask_beta[:]), 0.0, ALU.mult, ALU.add))
                dve.wait_ge(masks, ONE + 3 * b + 3)
                chain.link(nc.vector.tensor_tensor(at[:], decay[:], gram[:, :, SEQ:2 * SEQ], ALU.mult))
                nc.vector.tensor_tensor(wt[:], decay[:], gram[:, :, 0:SEQ], ALU.mult).then_inc(built, 1)
                dve.wait_ge(built, ONE + b + 1)

            def column(s):
                n, far = SEQ - s, s // 2
                parts = [(prod[0], far, s), (prod[1], 0, far)] if far else [(prod[0], 0, s)]
                link = chain.behind if far else chain.link
                for buf, c0, c1 in parts:
                    share = buf[:, 0:(c1 - c0) * n].rearrange("p (c t) -> p c t", t=n)
                    link(nc.vector.tensor_tensor(share, wt[:, s, s:SEQ].unsqueeze(1).to_broadcast([128, c1 - c0, n]),
                                                 at[:, c0:c1, s].unsqueeze(2).to_broadcast([128, c1 - c0, n]), ALU.mult))
                for buf, c0, c1 in parts:
                    share = buf[:, 0:(c1 - c0) * n].rearrange("p (c t) -> p c t", t=n)
                    link(nc.vector.tensor_tensor(wt[:, c0:c1, s:SEQ], wt[:, c0:c1, s:SEQ], share, ALU.subtract))
                if s == 2:
                    dve.wait_ge(order, chain.base + chain.n)

            def finish(b):
                dve.wait_ge(inv, ONE + 3 * b + 3)
                chain.link(nc.vector.tensor_tensor(wt[:], wt[:], rk[:, 1, :].unsqueeze(1).to_broadcast([128, SEQ, SEQ]), ALU.mult))
                dve.wait_ge(w_free, ONE + b)
                chain.link(nc.vector.tensor_scalar(w_out[:, :, 0:SEQ], wt[:], QS, None, ALU.mult))
                nc.vector.scalar_tensor_tensor(w_out[:, :, SEQ:2 * SEQ], wt[:], QS, w_out[:, :, 0:SEQ], ALU.mult, ALU.subtract).then_inc(mixed, 1)
                assert chain.n == LINKS, chain.n

            def batch(b, solve):
                for slot in range(SLOTS):
                    low(b, slot)
                    if solve:
                        if slot == LOADED:
                            squares(b - 1)
                        if slot == BUILD:
                            matrices(b - 1)
                        if slot >= BUILD:
                            todo, k = SLOTS - BUILD, slot - BUILD
                            for i in range((SEQ - 1) * k // todo, (SEQ - 1) * (k + 1) // todo):
                                column(SEQ - 1 - i)
                if solve:
                    finish(b - 1)

            batch(0, False)
            with nc.vector.Fori(1, BATCHES) as b:
                batch(b, True)
            squares(BATCHES - 1)
            matrices(BATCHES - 1)
            for s in range(SEQ - 1, 0, -1):
                column(s)
            finish(BATCHES - 1)

        @block.sync
        def _(sp):
            def store_unit(u):
                sp.wait_ge(gates_taken, ONE + u + 1)
                settle(sp, gates_taken)
                for c, dst in enumerate([m.beta_d, m.alpha_d]):
                    sp.dma_start(dst[u].rearrange("i h t -> h i t"),
                                 ba_sb[c * H:(c + 1) * H, :].rearrange("h (i t) -> h i t", t=SEQ)).then_inc(small_stored, 16)
                for b in range(2):
                    sp.wait_ge(gram_taken, ONE + u * H + 4 * b + 4)
                    settle(sp, gram_taken)
                    for par in range(2):
                        dst = m.gram_d[u].rearrange("(c par) h s n -> par h s c n", par=2)
                        for hh in range(4):
                            sp.dma_start(dst[par, 4 * b + hh], gsb[b][64 * par:64 * par + SEQ, hh, :, :]).then_inc(stored[b], 16)
                sp.wait_ge(norms_taken, ONE + 2 * u + 2)
                settle(sp, norms_taken)
                for j in range(PAIRS):
                    sp.dma_start(m.qn_d[u, 2 * j:2 * j + 2].rearrange("i h t -> h i t"),
                                 qn_sb[j * H:(j + 1) * H, :].rearrange("h (i t) -> h i t", t=SEQ)).then_inc(small_stored, 16)


            def load_batch(b):
                sp.wait_ge(small_stored, 32 * SMALL * b + 32 * SMALL)
                sp.wait_ge(stored[0], 256 * b + 256)
                sp.wait_ge(stored[1], 256 * b + 256)
                settle(sp, stored[1])
                sp.dma_start(gate[:, 0, :], m.beta_b[b]).then_inc(loaded, 16)
                sp.dma_start(gate[:, 1, :], m.alpha_b[b]).then_inc(loaded, 16)
                sp.dma_start(qn[:], m.qn_b[b]).then_inc(loaded, 16)
                sp.dma_start(gram[:], m.gram_b[b]).then_inc(loaded, 16)

            def store_batch(b):
                dst = m.w_b[b]
                sp.wait_ge(mixed, ONE + b + 1)
                sp.dma_start(dst, w_out[:]).then_inc(w_stored, 16)
                sp.wait_ge(w_stored, 16 * b + 16)
                sp.sem_inc(w_free, 1)

            def store_units(b):
                for v in range(2):
                    store_unit(2 * b + v)

            store_units(0)
            load_batch(0)
            with nc.sync.Fori(1, BATCHES) as b:
                store_units(b)
                sp.wait_ge(built, ONE + b)
                load_batch(b)
                store_batch(b - 1)
            store_batch(BATCHES - 1)


def phase_mix(nc, m):
    with ExitStack() as own:
        def sb(name, shape, dt):
            return own.enter_context(nc.sbuf_tensor("m_" + name, shape, dt))

        (w_loaded, v_ready, v_act, v_hi, v_lo, o_ready, o_hi, o_lo, wo_ready, x2_taken, n_ready, nt_ready, nt_hi, nt_lo,
         a_ready, a_act, a_hi, a_lo, y_ready, y_taken, order, m.var_ready, m.root_ready, made) = m.sems["mix"]
        m.roots_per_turn = 2
        vs = sb("vs", [128, 2, 512], F32)
        v_h = [sb(f"v_h{g}", [128, 1024], F16) for g in range(3)]
        v_l = [sb(f"v_l{g}", [128, 1024], F16) for g in range(3)]
        ot_h, ot_l = sb("ot_h", [128, H, UT], F16), sb("ot_l", [128, H, UT], F16)
        x2 = sb("x2", [TT, TPU * D], F32)
        n_tok = sb("n_tok", [TT, TPU, D], F32)
        ht_h, ht_l = sb("ht_h", [128, KD, UT], F16), sb("ht_l", [128, KD, UT], F16)
        a_s = [sb(f"a_s{p}", [128, UT], F32) for p in range(2)]
        at_h, at_l = sb("at_h", [128, F // 128, UT], F16), sb("at_l", [128, F // 128, UT], F16)
        tok_ps = m.ps[0:TT, 4:6, :].rearrange("p b n -> p (b n)")[:, 0:TPU * D]
        nt_ps = m.ps[:, 6:8, 0:UT]
        FC = F // 128
        VH = len(GROUPS) * 2
        LINKS = 9
        block = own.enter_context(nc.Block())

        @block.sync
        def _(sp):
            with nc.sync.Fori(0, UNITS) as u:
                sp.wait_ge(o_ready, ONE + H * u)
                settle(sp, o_ready)
                for g, (i0, n) in enumerate(GROUPS):
                    for j in range(n):
                        sp.dma_start(m.wbd[g][SEQ * j:SEQ * (j + 1), :, j, :],
                                     m.w_d[u, i0 + j].rearrange("h s n -> s h n")).then_inc(w_loaded, 16)

        @block.gpsimd
        def _(pool):
            route_constants(nc, pool, m, made)
            with nc.gpsimd.Fori(0, UNITS) as u:
                unit_roots(nc, pool, m, u, 2)

        @block.tensor
        def _(pe):
            def values(u):
                for g, (i0, n) in enumerate(GROUPS):
                    rows = n * SEQ
                    for half in range(2):
                        t = 2 * g + half
                        pe.wait_ge(v_act, ONE + u * VH + max(t - 1, 0))
                        terms = [x for k in range(KD) for x in passes(
                            m.nt_hi[:, u, k, i0 * SEQ:i0 * SEQ + rows], m.nt_lo[:, u, k, i0 * SEQ:i0 * SEQ + rows],
                            m.wv_hi[:, k * 1024 + half * 512:k * 1024 + half * 512 + 512],
                            m.wv_lo[:, k * 1024 + half * 512:k * 1024 + half * 512 + 512])]
                        for i, (a, b) in enumerate(terms):
                            last = nc.tensor.matmul(m.ps[0:rows, half, :], a, b, start=(i == 0), stop=(i == len(terms) - 1))
                        last.then_inc(v_ready, 1)

            def mix(u, fed):
                pe.wait_ge(w_loaded, 128 * u + 128)
                pe.wait_ge(v_hi, ONE + u * VH + VH)
                pe.wait_ge(v_lo, ONE + u * VH + VH)
                pe.wait_ge(a_act, ONE + fed * FC)
                for h in range(H):
                    pe.wait_ge(o_lo, ONE + u * H + max(h - 1, 0))
                    pe.wait_ge(o_hi, ONE + u * H + max(h - 1, 0))
                    for g, (i0, n) in enumerate(GROUPS):
                        rows = n * SEQ
                        out = m.ps[:, 2 + h % 2, i0 * SEQ:i0 * SEQ + rows]
                        w = m.wbd[g][0:rows, h, 0:n, :]
                        for i, (a, b) in enumerate(passes(v_h[g][0:rows, h * DK:(h + 1) * DK], v_l[g][0:rows, h * DK:(h + 1) * DK],
                                                          w[:, :, 0:SEQ], w[:, :, SEQ:2 * SEQ])):
                            last = nc.tensor.matmul(out, a, b, start=(i == 0), stop=(i == 2))
                    last.then_inc(o_ready, 1)

            def out_project(u):
                pe.wait_ge(o_hi, ONE + u * H + H)
                pe.wait_ge(o_lo, ONE + u * H + H)
                pe.wait_ge(y_taken, ONE + u)
                for j in range(TPU):
                    terms = [x for h in range(H) for x in passes(
                        ot_h[:, h, j * TT:(j + 1) * TT], ot_l[:, h, j * TT:(j + 1) * TT],
                        m.wo_hi[:, h * D:(h + 1) * D], m.wo_lo[:, h * D:(h + 1) * D])]
                    for i, (a, b) in enumerate(terms):
                        last = nc.tensor.matmul(tok_ps[:, j * D:(j + 1) * D], a, b, start=(i == 0), stop=(i == len(terms) - 1))
                last.then_inc(wo_ready, 1)

            def feed(u, mixed):
                pe.wait_ge(n_ready, ONE + u + 1)
                pe.wait_ge(nt_hi, ONE + u)
                pe.wait_ge(nt_lo, ONE + u)
                for k in range(KD):
                    for j in range(TPU):
                        last = nc.tensor.transpose(nt_ps[:, k, j * TT:(j + 1) * TT], n_tok[:, j, k * 128:(k + 1) * 128],
                                                   m.ident[0:TT, 0:TT])
                last.then_inc(nt_ready, 1)
                pe.wait_ge(nt_hi, ONE + u + 1)
                pe.wait_ge(nt_lo, ONE + u + 1)
                for f in range(FC):
                    if f == 0:
                        pe.wait_ge(o_hi, ONE + mixed * H)
                        pe.wait_ge(o_lo, ONE + mixed * H)
                    pe.wait_ge(a_act, ONE + u * FC + max(f - 1, 0))
                    terms = [x for k in range(KD) for x in passes(
                        m.w1_hi[:, k * F + f * 128:k * F + f * 128 + 128], m.w1_lo[:, k * F + f * 128:k * F + f * 128 + 128],
                        ht_h[:, k, :], ht_l[:, k, :])]
                    for i, (a, b) in enumerate(terms):
                        last = nc.tensor.matmul(m.ps[:, 2 + f % 2, 0:UT], a, b, start=(i == 0), stop=(i == len(terms) - 1))
                    last.then_inc(a_ready, 1)
                pe.wait_ge(a_hi, ONE + u * FC + FC)
                pe.wait_ge(a_lo, ONE + u * FC + FC)
                pe.wait_ge(x2_taken, ONE + u + 1)
                for j in range(TPU):
                    terms = [x for f in range(FC) for x in passes(
                        at_h[:, f, j * TT:(j + 1) * TT], at_l[:, f, j * TT:(j + 1) * TT],
                        m.w2_hi[:, f * D:(f + 1) * D], m.w2_lo[:, f * D:(f + 1) * D])]
                    for i, (a, b) in enumerate(terms):
                        last = nc.tensor.matmul(tok_ps[:, j * D:(j + 1) * D], a, b, start=(i == 0), stop=(i == len(terms) - 1))
                last.then_inc(y_ready, 1)

            values(0)
            mix(0, 0)
            with nc.tensor.Fori(0, UNITS - 1) as u:
                out_project(u)
                values(u + 1)
                mix(u + 1, u)
                feed(u, u + 2)
            out_project(UNITS - 1)
            feed(UNITS - 1, UNITS)

        @block.scalar
        def _(act):
            def values(u):
                for t in range(VH):
                    g, half = t // 2, t % 2
                    rows = GROUPS[g][1] * SEQ
                    act.wait_ge(v_ready, ONE + u * VH + t + 1)
                    act.wait_ge(v_lo, ONE + u * VH + max(t - 1, 0))
                    nc.scalar.activation(vs[0:rows, half, :], m.ps[0:rows, half, :], ACT.Silu, scale=1.0 / WS).then_inc(v_act, 1)
                    act.wait_ge(v_act, ONE + u * VH + t + 1)
                    if t == 0:
                        act.wait_ge(o_ready, ONE + u * H)
                    nc.scalar.activation(v_h[g][0:rows, half * 512:half * 512 + 512], vs[0:rows, half, :], ACT.Copy).then_inc(v_hi, 1)

            def heads(u):
                act.wait_ge(wo_ready, ONE + u)
                for h in range(H):
                    act.wait_ge(o_ready, ONE + u * H + h + 1)
                    nc.scalar.activation(ot_h[:, h, :], m.ps[:, 2 + h % 2, 0:UT], ACT.Copy, scale=OS / QS).then_inc(o_hi, 1)

            def feed(u):
                act.wait_ge(nt_ready, ONE + u + 1)
                act.wait_ge(a_ready, ONE + u * FC)
                nc.scalar.activation(ht_h[:], nt_ps, ACT.Copy).then_inc(nt_hi, 1)
                act.wait_ge(y_ready, ONE + u)
                for f in range(FC):
                    act.wait_ge(a_ready, ONE + u * FC + f + 1)
                    act.wait_ge(a_lo, ONE + u * FC + max(f - 1, 0))
                    nc.scalar.activation(a_s[f % 2][:], m.ps[:, 2 + f % 2, 0:UT], ACT.Gelu, scale=1.0 / WS,
                                         bias=m.b1[:, f:f + 1]).then_inc(a_act, 1)
                    act.wait_ge(a_act, ONE + u * FC + f + 1)
                    nc.scalar.activation(at_h[:, f, :], a_s[f % 2][:], ACT.Copy).then_inc(a_hi, 1)

            values(0)
            heads(0)
            with nc.scalar.Fori(0, UNITS - 1) as u:
                values(u + 1)
                heads(u + 1)
                feed(u)
            feed(UNITS - 1)

        @block.vector
        def _(dve):
            chain = Chain(dve, order)

            def values(u):
                for t in range(VH):
                    g, half = t // 2, t % 2
                    rows = GROUPS[g][1] * SEQ
                    dve.wait_ge(v_hi, ONE + u * VH + t + 1)
                    nc.vector.tensor_tensor(v_l[g][0:rows, half * 512:half * 512 + 512], vs[0:rows, half, :],
                                            v_h[g][0:rows, half * 512:half * 512 + 512], ALU.subtract).then_inc(v_lo, 1)

            def heads(u):
                for h in range(H):
                    dve.wait_ge(o_hi, ONE + u * H + h + 1)
                    nc.vector.scalar_tensor_tensor(ot_l[:, h, :], m.ps[:, 2 + h % 2, 0:UT], OS / QS, ot_h[:, h, :],
                                                   ALU.mult, ALU.subtract).then_inc(o_lo, 1)

            def second_norm(u):
                chain.turn(ONE + u * LINKS)
                dve.wait_ge(wo_ready, ONE + u + 1)
                nc.vector.scalar_tensor_tensor(x2[:], tok_ps, 1.0 / (WS * OS), m.n1[:, u, :], ALU.mult, ALU.add).then_inc(x2_taken, 1)
                dve.wait_ge(x2_taken, ONE + u + 1)
                normalise(nc, dve, chain, m, lambda j: x2[:, j * D:(j + 1) * D], lambda j: n_tok[:, j, :], u, 1)
                for j in range(TPU):
                    ins = nc.vector.tensor_tensor(n_tok[:, j, :], n_tok[:, j, :], m.ln2_w[:], ALU.mult)
                chain.link(ins)
                for j in range(TPU):
                    ins = nc.vector.tensor_tensor(n_tok[:, j, :], n_tok[:, j, :], m.ln2_b[:], ALU.add)
                ins.then_inc(n_ready, 1)
                chain.link(nc.vector.tensor_tensor(m.h[:, u, :], m.h[:, u, :], x2[:], ALU.add))
                for j in range(TPU):
                    ins = nc.vector.tensor_tensor(m.h[:, u, j * D:(j + 1) * D], m.h[:, u, j * D:(j + 1) * D], m.b2[:], ALU.add)
                chain.link(ins)

            def feed(u):
                dve.wait_ge(nt_hi, ONE + u + 1)
                nc.vector.tensor_tensor(ht_l[:], nt_ps, ht_h[:], ALU.subtract).then_inc(nt_lo, 1)
                for f in range(FC):
                    dve.wait_ge(a_hi, ONE + u * FC + f + 1)
                    nc.vector.tensor_tensor(at_l[:, f, :], a_s[f % 2][:], at_h[:, f, :], ALU.subtract).then_inc(a_lo, 1)
                dve.wait_ge(y_ready, ONE + u + 1)
                nc.vector.scalar_tensor_tensor(m.h[:, u, :], tok_ps, 1.0 / WS, m.h[:, u, :], ALU.mult, ALU.add).then_inc(y_taken, 1)
                dve.wait_ge(y_taken, ONE + u + 1)
                normalise(nc, dve, chain, m, lambda j: m.h[:, u, j * D:(j + 1) * D],
                          lambda j: m.n1[:, u, j * D:(j + 1) * D], u, 2)
                assert chain.n == LINKS, chain.n

            values(0)
            heads(0)
            with nc.vector.Fori(0, UNITS - 1) as u:
                second_norm(u)
                values(u + 1)
                heads(u + 1)
                feed(u)
            second_norm(UNITS - 1)
            feed(UNITS - 1)


RMS_EPS = 1e-6
GATE_EPS = 1e-9
SLOT_TILES = (2 * IMAGES * SEQ + E * 127) // 128
ROWS = SLOT_TILES * 128
PIECES = 24
PIECE = 3 * E * KD * FE // PIECES


def phase_moe(nc, m):
    sems = m.sems[f"moe{m.round}"]
    first_round, last_round = m.round == 1, m.round == LOOPS
    with ExitStack() as own:
        def sb(name, shape, dt):
            return own.enter_context(nc.sbuf_tensor(f"e{m.round}_" + name, shape, dt))

        (sq_act, sum_ready, root_ready, zn_ready, zt_ready, zt_hi, zt_lo, logit_ready, shifted, exp_ready, order, picked, counted,
         spread_ready, spread_used, places_ready, gathered0, gathered1, gathered2, gathered3, xt_ready, xt_hi, xt_lo,
         up1_ready, up3_ready, silu_ready, g_ready, gt_ready, gt_hi, gt_lo, y_ready, y_taken, scattered0, scattered1,
         back0, back1, used, stored0, stored1, *extra) = sems
        if last_round:
            base_ready, out_stored = extra
        if first_round:
            w_split, w_lo, *w_loaded = extra
        gathered, scattered, back, zn_stored = [gathered0, gathered1, gathered2, gathered3], [scattered0, scattered1], [back0, back1], [stored0, stored1]
        ss, ssv, rms = sb("ss", [TT, TILES], F32), sb("ssv", [TT, TILES], F32), sb("rms", [TT, TILES], F32)
        wide = [sb(f"wide{i}", [TT, TPU * 2 * D], F32) for i in range(2)]
        stage = [w[:, 0:TPU * D].rearrange("p (j d) -> p j d", d=D) for w in wide]
        yb = [w[:].rearrange("p (j c d) -> p j c d", c=2, d=D) for w in wide]
        scratch = [sb(f"scratch{i}", [TT, D], F32) for i in range(3)]
        zt_h, zt_l = [sb(f"zt_h{i}", [128, KD, UT], F16) for i in range(2)], [sb(f"zt_l{i}", [128, KD, UT], F16) for i in range(2)]
        logit, ex = sb("logit", [TT, TILES, E], F32), sb("ex", [TT, TILES, E], F32)
        top, index = sb("top", [TT, TILES, 8], F32), sb("index", [TT, TILES, 8], U32)
        total, inv, den = sb("total", [TT, TILES], F32), sb("inv", [TT, TILES], F32), sb("den", [TT, TILES], F32)
        score = sb("score", [TT, 2, TILES], F32)
        pick = sb("pick", [TT, TILES, 2], F32)
        mask = [sb(f"mask{c}", [TT, E, TILES], F32) for c in range(2)]
        both = sb("both", [TT, E, TILES], F32)
        counts, running = sb("counts", [TT, E, TILES], F32), sb("running", [TT, E, TILES], F32)
        place, chosen = sb("place", [TT, E, TILES], F32), sb("chosen", [TT, E, TILES], F32)
        slot_f, slot_i = sb("slot_f", [TT, 2, TILES], F32), sb("slot_i", [TT, 2, TILES], U32)
        part_i, row_f, tile_f = sb("part_i", [TT, 2, TILES], U32), sb("row_f", [TT, 2, TILES], F32), sb("tile_f", [TT, 2, TILES], F32)
        TPE = IMAGES * SEQ // 128
        more = sb("more", [TT, E, TPE], F32)
        tiles, upto, before = sb("tiles", [TT, E], F32), sb("upto", [TT, E], F32), sb("before", [TT, E], F32)
        past, tab = sb("past", [1, SLOT_TILES, E], F32), sb("tab", [1, SLOT_TILES], F32)
        table = sb("table", [1, SLOT_TILES], mybir.dt.int32)
        TC = 4
        at_row = [sb(f"at_row{i}", [TT, TC, 128], F32) for i in range(2)]
        at_tile = [sb(f"at_tile{i}", [TT, TC, SLOT_TILES], F32) for i in range(2)]
        who, empty, goes = sb("who", [128, SLOT_TILES], F32), sb("empty", [128, SLOT_TILES], F32), sb("goes", [128, SLOT_TILES], F32)
        token, target = sb("token", [128, SLOT_TILES], U32), sb("target", [128, SLOT_TILES], U32)
        gate = [sb(f"gate{c}", [TT, TILES], F32) for c in range(2)]
        raw = sb("raw", [128, 3, PIECE], F32)
        cut = lambda i, n: raw[:].rearrange("p s n -> p (s n)")[:, i:i + n]
        xs = [cut(p * D, D) for p in range(4)]
        xt_h, xt_l = [sb(f"xt_h{p}", [128, D], F16) for p in range(2)], [sb(f"xt_l{p}", [128, D], F16) for p in range(2)]
        si = [cut(4 * D + p * FE, FE) for p in range(2)]
        g = [cut(4 * D + 2 * FE + p * FE, FE) for p in range(2)]
        assert 4 * D + 4 * FE <= 3 * PIECE
        gt_h, gt_l = sb("gt_h", [128, FE], F16), sb("gt_l", [128, FE], F16)
        ys = [sb(f"ys{p}", [128, D], F32) for p in range(2)]
        Q = SLOT_TILES
        assert Q % 2 == 1
        XT, GT, Y = 4, 5, 6
        log_ps, pre_ps, cnt_ps = m.ps[0:TT, 4, 0:TILES * E], m.ps[0:TT, 5, 0:E * TILES], m.ps[0:TT, 6, 0:E * TILES]
        who_ps = m.ps[:, 7, 0:Q]
        flat = lambda a: a.rearrange("p a b -> p (a b)")
        STEPS = [(c, t) for c in range(2) for t in range(0, TILES, TC)]
        total_out = m.h if last_round else m.n1
        zn_rows = m.zn_d.rearrange("(u j p) d -> u p j d", j=TPU, p=TT)
        y_rows = m.y_d[0:2 * IMAGES * SEQ, :].rearrange("(u j p c) d -> u p j c d", j=TPU, p=TT, c=2)
        block = own.enter_context(nc.Block())

        @block.sync
        def _(sp):
            with nc.sync.Fori(0, UNITS // 2) as i:
                for b in range(2):
                    sp.wait_ge(zn_ready, i * 2 + (b + 1 + ONE))
                    settle(sp, zn_ready)
                    sp.dma_start(zn_rows[i * 2 + b], stage[b]).then_inc(zn_stored[b], 16)
            for p in range(2):
                sp.wait_ge(scattered[p], 16 * ((Q + 1 - p) // 2))
            for u in range(UNITS):
                if u >= 2:
                    sp.wait_ge(used, u - 1 + ONE)
                sp.dma_start(yb[u % 2], y_rows[u]).then_inc(back[u % 2], 16)
            if last_round:
                for u in range(UNITS):
                    sp.wait_ge(used, u + 1 + ONE)
                    sp.dma_start(m.out[u], m.h[:, u, :]).then_inc(out_stored, 16)
                sp.wait_ge(out_stored, 16 * UNITS)

        @block.gpsimd
        def _(pool):
            pool.wait_ge(sum_ready, 1 + ONE)
            nc.gpsimd.tensor_tensor(rms[:], ssv[:], m.minus_half[0:TT, 0:TILES], ALU.pow).then_inc(root_ready, 1)
            if last_round:
                for u in range(UNITS):
                    last = nc.gpsimd.tensor_tensor(m.h[:, u, :], m.h[:, u, :], m.n1[:, u, :], ALU.add)
                last.then_inc(base_ready, 1)
            if first_round:
                for t in range(PIECES):
                    pool.wait_ge(w_split, 2 * t + 2 + ONE)
                    nc.gpsimd.tensor_tensor(m.experts_lo[:, t, :], raw[:, t % 3, :], m.experts_hi[:, t, :], ALU.subtract).then_inc(w_lo, 1)
                pool.wait_ge(w_lo, PIECES + ONE)
            for b in range(2):
                pool.wait_ge(zn_stored[b], 16 * UNITS // 2)
            pool.wait_ge(places_ready, 1 + ONE)

            def gather(q):
                if q >= 4:
                    pool.wait_ge(xt_ready, q - 3 + ONE)
                nc.gpsimd.indirect_dma_start(xs[q % 4][:], None, m.zn_d,
                                             bass.IndirectOffsetOnAxis(ap=token[:, q:q + 1], axis=0)).then_inc(gathered[q % 4], 16)

            for q in range(4):
                gather(q)
            for q in range(Q):
                pool.wait_ge(y_taken, q + 1 + ONE)
                nc.gpsimd.indirect_dma_start(m.y_d, bass.IndirectOffsetOnAxis(ap=target[:, q:q + 1], axis=0),
                                             ys[q % 2][:], None).then_inc(scattered[q % 2], 16)
                if q + 4 < Q:
                    gather(q + 4)
            for p in range(2):
                pool.wait_ge(scattered[p], 16 * ((Q + 1 - p) // 2))

        def expert_loop(engine, body):
            body(0, 0, None, True, True)
            body(1, 1, None, True, True)
            with engine.Fori(1, (Q - 3) // 2) as i:
                body(i * 2, 0, i, True, True)
                body(i * 2 + 1, 1, i, True, True)
            body(Q - 3, 0, (Q - 3) // 2, True, True)
            body(Q - 2, 1, (Q - 3) // 2, False, True)
            body(Q - 1, 0, (Q - 1) // 2, False, False)

        @block.tensor
        def _(pe):
            def turn_over(u, b):
                pe.wait_ge(zn_ready, u + (1 + ONE))
                for k in range(KD):
                    for j in range(TPU):
                        last = nc.tensor.transpose(m.ps[:, 2 * b + k, j * TT:(j + 1) * TT], stage[b][:, j, k * 128:(k + 1) * 128],
                                                   m.ident[0:TT, 0:TT])
                last.then_inc(zt_ready, 1)

            def logits(u, b):
                pe.wait_ge(zt_hi, u + (1 + ONE))
                pe.wait_ge(zt_lo, u + (1 + ONE))
                for j in range(TPU):
                    terms = [x for k in range(KD) for x in passes(
                        zt_h[b][:, k, j * TT:(j + 1) * TT], zt_l[b][:, k, j * TT:(j + 1) * TT],
                        m.router_hi[:, k * E:(k + 1) * E], m.router_lo[:, k * E:(k + 1) * E])]
                    for i, (x, w) in enumerate(terms):
                        last = nc.tensor.matmul(log_ps[:, (u * TPU + j) * E:(u * TPU + j + 1) * E], x, w,
                                                start=(i == 0), stop=(i == len(terms) - 1))
                last.then_inc(logit_ready, 1)

            turn_over(0, 0)
            for u in range(1, UNITS):
                if u >= 2:
                    pe.wait_ge(zt_lo, u - 1 + ONE)
                    pe.wait_ge(zt_hi, u - 1 + ONE)
                turn_over(u, u % 2)
                logits(u - 1, (u - 1) % 2)
            logits(UNITS - 1, (UNITS - 1) % 2)
            pe.wait_ge(picked, 1 + ONE)
            nc.tensor.matmul(pre_ps, m.earlier[:], flat(both[:]), start=True, stop=True)
            nc.tensor.matmul(cnt_ps, m.all_ones[:], flat(both[:]), start=True, stop=True).then_inc(counted, 1)
            for n, (c, t0) in enumerate(STEPS):
                pe.wait_ge(spread_ready, n + 1 + ONE)
                for t in range(TC):
                    last = nc.tensor.matmul(who_ps, at_row[n % 2][:, t, :], at_tile[n % 2][:, t, :],
                                            start=(n == 0 and t == 0), stop=(n == len(STEPS) - 1 and t == TC - 1))
                last.then_inc(spread_used, 1)

            def expert(q):
                return nc.tensor.value_load(table[0:1, bass.ds(q, 1)], min_val=0, max_val=E - 1)

            def rows_over(q, buf, nth):
                pe.wait_ge(gathered[buf], nth * 16 + 16)
                pe.wait_ge(xt_hi, q + ONE)
                pe.wait_ge(xt_lo, q + ONE)
                for k in range(KD):
                    last = nc.tensor.transpose(m.ps[:, XT, k * 128:(k + 1) * 128], xs[buf][:, k * 128:(k + 1) * 128], m.ident[:])
                last.then_inc(xt_ready, 1)

            def up(q, p, c, e):
                pe.wait_ge(xt_hi, q + (1 + ONE))
                pe.wait_ge(xt_lo, q + (1 + ONE))
                whi, wlo = ((m.e1_hi, m.e1_lo), (m.e3_hi, m.e3_lo))[c]
                n = 0
                for k in range(KD):
                    for x, w in passes(xt_h[p][:, k * 128:(k + 1) * 128], xt_l[p][:, k * 128:(k + 1) * 128], whi, wlo):
                        last = nc.tensor.matmul(m.ps[:, 2 * p + c, :], x, w[:, bass.ds(e * (KD * FE) + k * FE, FE)],
                                                start=(n == 0), stop=(n == 3 * KD - 1))
                        n += 1
                last.then_inc((up1_ready, up3_ready)[c], 1)

            def inner_over(q, p):
                pe.wait_ge(g_ready, q + (1 + ONE))
                pe.wait_ge(gt_hi, q + ONE)
                pe.wait_ge(gt_lo, q + ONE)
                for f in range(FE // 128):
                    last = nc.tensor.transpose(m.ps[:, GT, f * 128:(f + 1) * 128], g[p][:, f * 128:(f + 1) * 128], m.ident[:])
                last.then_inc(gt_ready, 1)

            def down(q, e):
                pe.wait_ge(gt_hi, q + (1 + ONE))
                pe.wait_ge(gt_lo, q + (1 + ONE))
                pe.wait_ge(y_taken, q + ONE)
                n = 0
                for f in range(FE // 128):
                    for x, w in passes(gt_h[:, f * 128:(f + 1) * 128], gt_l[:, f * 128:(f + 1) * 128], m.e2_hi, m.e2_lo):
                        last = nc.tensor.matmul(m.ps[:, Y, 0:D], x, w[:, bass.ds(e * (FE // 128 * D) + f * D, D)],
                                                start=(n == 0), stop=(n == 3 * FE // 128 - 1))
                        n += 1
                last.then_inc(y_ready, 1)

            pe.wait_ge(places_ready, 1 + ONE)
            if first_round:
                pe.wait_ge(w_lo, PIECES + ONE)
            for q in range(2):
                rows_over(q, q, 0)
            e0 = expert(0)
            up(0, 0, 0, e0)
            up(0, 0, 1, e0)

            def turn(q, p, e, rows_buf, nth, more_rows, more_up):
                e_next = expert(q + 1) if more_up else None
                inner_over(q, p)
                if more_rows:
                    rows_over(q + 2, rows_buf, nth)
                if more_up:
                    up(q + 1, 1 - p, 0, e_next)
                    up(q + 1, 1 - p, 1, e_next)
                down(q, e)
                return e_next

            assert (Q - 3) % 4 == 0
            with nc.tensor.Fori(0, (Q - 3) // 4) as i:
                e = expert(i * 4)
                for r in range(4):
                    e = turn(i * 4 + r, r % 2, e, (r + 2) % 4, i + (r + 2) // 4, True, True)
            e = turn(Q - 3, 0, expert(Q - 3), 2, (Q - 3) // 4, True, True)
            e = turn(Q - 2, 1, e, 0, 0, False, True)
            turn(Q - 1, 0, e, 0, 0, False, False)

        @block.scalar
        def _(act):
            def bring(t):
                if t >= 3:
                    act.wait_ge(w_lo, t - 2 + ONE)
                act.dma_start(raw[:, t % 3, :], m.experts[t]).then_inc(w_loaded[t % 3], 16)

            def split(t):
                act.wait_ge(w_loaded[t % 3], 16 * (t // 3 + 1))
                nc.scalar.activation(m.experts_hi[:, t, :], raw[:, t % 3, :], ACT.Copy, scale=WS).then_inc(w_split, 1)
                act.wait_ge(w_split, 2 * t + 1 + ONE)
                nc.scalar.activation(raw[:, t % 3, :], raw[:, t % 3, :], ACT.Copy, scale=WS).then_inc(w_split, 1)
                if t >= 1 and t + 2 < PIECES:
                    bring(t + 2)

            if first_round:
                for t in range(3):
                    bring(t)
            for u in range(UNITS):
                last = nc.scalar.activation(scratch[2][:], m.n1[:, u, 2 * D:3 * D], ACT.Square, accum_out=ss[:, u * TPU + 2:u * TPU + 3])
                last.then_inc(sq_act, 1)
                act.wait_ge(sq_act, u + 1 + ONE)
            for u in range(UNITS):
                act.wait_ge(zt_ready, u + 1 + ONE)
                if u >= 2:
                    act.wait_ge(logit_ready, u - 1 + ONE)
                nc.scalar.activation(zt_h[u % 2][:], m.ps[:, 2 * (u % 2):2 * (u % 2) + 2, 0:UT], ACT.Copy).then_inc(zt_hi, 1)
                if first_round:
                    split(u)
            if first_round:
                for t in range(UNITS, PIECES // 2):
                    split(t)
            act.wait_ge(shifted, 1 + ONE)
            nc.scalar.activation(ex[:], ex[:], ACT.Exp).then_inc(exp_ready, 1)
            if first_round:
                for t in range(PIECES // 2, PIECES):
                    split(t)

            def rows_in(q, p):
                act.wait_ge(xt_ready, q + (1 + ONE))
                nc.scalar.activation(xt_h[p][:], m.ps[:, XT, 0:D], ACT.Copy).then_inc(xt_hi, 1)

            def gated(q, p):
                act.wait_ge(up1_ready, q + (1 + ONE))
                nc.scalar.activation(si[p][:], m.ps[:, 2 * p, :], ACT.Silu, scale=1.0 / WS).then_inc(silu_ready, 1)

            def body(q, p, i, more_rows, more_up):
                act.wait_ge(gt_ready, q + (1 + ONE))
                act.wait_ge(y_ready, q + ONE)
                nc.scalar.activation(gt_h[:], m.ps[:, GT, :], ACT.Copy).then_inc(gt_hi, 1)
                if more_rows:
                    act.wait_ge(up3_ready, q + (1 + ONE))
                    rows_in(q + 2, p)
                if more_up:
                    gated(q + 1, 1 - p)

            rows_in(0, 0)
            rows_in(1, 1)
            gated(0, 0)
            expert_loop(nc.scalar, body)

        @block.vector
        def _(dve):
            chain = Chain(dve, order)
            chain.turn(ONE)
            for u in range(UNITS):
                for j in range(2):
                    z = m.n1[:, u, j * D:(j + 1) * D]
                    ins = nc.vector.scalar_tensor_tensor(scratch[j][:], z, 1.0, z, ALU.mult, ALU.mult,
                                                         accum_out=ss[:, u * TPU + j:u * TPU + j + 1])
                chain.link(ins)
            dve.wait_ge(sq_act, UNITS + ONE)
            nc.vector.tensor_scalar(ssv[:], ss[:], 1.0 / D, RMS_EPS, ALU.mult, ALU.add).then_inc(sum_ready, 1)
            dve.wait_ge(root_ready, 1 + ONE)

            def normed(u):
                b = u % 2
                if u >= 2:
                    dve.wait_ge(zt_ready, u - 1 + ONE)
                    dve.wait_ge(zn_stored[b], 16 * (u // 2))
                for j in range(TPU):
                    ins = nc.vector.scalar_tensor_tensor(stage[b][:, j, :], m.n1[:, u, j * D:(j + 1) * D],
                                                         rms[:, u * TPU + j:u * TPU + j + 1], m.norm_w[:], ALU.mult, ALU.mult)
                ins.then_inc(zn_ready, 1)

            normed(0)
            for u in range(UNITS):
                if u + 1 < UNITS:
                    normed(u + 1)
                dve.wait_ge(zt_hi, u + 1 + ONE)
                nc.vector.tensor_tensor(zt_l[u % 2][:], m.ps[:, 2 * (u % 2):2 * (u % 2) + 2, 0:UT], zt_h[u % 2][:], ALU.subtract).then_inc(zt_lo, 1)
            dve.wait_ge(logit_ready, UNITS + ONE)
            chain.link(nc.vector.tensor_scalar(flat(logit[:]), log_ps, 1.0 / WS, None, ALU.mult))
            for t in range(TILES):
                ins = nc.vector.max(top[:, t, :], logit[:, t, :])
            chain.link(ins)
            for t in range(TILES):
                ins = nc.vector.max_index(index[:, t, :], top[:, t, :], logit[:, t, :])
            chain.link(ins)
            chain.link(nc.vector.tensor_copy(pick[:], index[:, :, 0:2]))
            for c in range(2):
                ins = nc.vector.tensor_tensor(mask[c][:], pick[:, :, c].unsqueeze(1).to_broadcast([TT, E, TILES]),
                                              m.expert_no[:].unsqueeze(2).to_broadcast([TT, E, TILES]), ALU.is_equal)
            chain.link(ins)
            nc.vector.tensor_tensor(both[:], mask[0][:], mask[1][:], ALU.add).then_inc(picked, 1)
            nc.vector.tensor_tensor(ex[:], logit[:], top[:, :, 0:1].to_broadcast([TT, TILES, E]), ALU.subtract).then_inc(shifted, 1)
            dve.wait_ge(counted, 1 + ONE)
            chain.link(nc.vector.tensor_copy(flat(counts[:]), cnt_ps))
            chain.link(nc.vector.tensor_tensor_scan(flat(running[:]), flat(m.not_first[:]), flat(counts[:]), 0.0, ALU.mult, ALU.add))
            n_e = running[:, :, TILES - 1]
            chain.link(nc.vector.tensor_tensor(more[:], n_e.unsqueeze(2).to_broadcast([TT, E, TPE]),
                                               m.by128[:].unsqueeze(1).to_broadcast([TT, E, TPE]), ALU.is_gt))
            chain.link(nc.vector.tensor_reduce(tiles[:], more[:], AX_X, ALU.add))
            chain.link(nc.vector.tensor_tensor_scan(upto[:], m.ones_row[:], tiles[:], 0.0, ALU.mult, ALU.add))
            chain.link(nc.vector.tensor_tensor(before[:], upto[:], tiles[:], ALU.subtract))
            chain.link(nc.vector.tensor_scalar(before[:], before[:], 128.0, None, ALU.mult))
            chain.link(nc.vector.tensor_tensor(flat(place[:]), pre_ps, flat(running[:]), ALU.add))
            chain.link(nc.vector.tensor_tensor(place[:], place[:], counts[:], ALU.subtract))
            chain.link(nc.vector.tensor_tensor(place[:], place[:], before[:].unsqueeze(2).to_broadcast([TT, E, TILES]), ALU.add))
            for c in range(2):
                chain.link(nc.vector.tensor_tensor(chosen[:], mask[c][:], place[:], ALU.mult))
                chain.link(nc.vector.tensor_reduce(slot_f[:, c, :], chosen[:].rearrange("p e t -> p t e"), AX_X, ALU.add))
            chain.link(nc.vector.tensor_copy(slot_i[:], slot_f[:]))
            chain.link(nc.vector.tensor_scalar(part_i[:], slot_i[:], 127, None, ALU.bitwise_and))
            chain.link(nc.vector.tensor_copy(row_f[:], part_i[:]))
            chain.link(nc.vector.tensor_scalar(slot_i[:], slot_i[:], 7, None, ALU.logical_shift_right))
            chain.link(nc.vector.tensor_copy(tile_f[:], slot_i[:]))
            for n, (c, t0) in enumerate(STEPS):
                if n >= 2:
                    dve.wait_ge(spread_used, n - 1 + ONE)
                nc.vector.tensor_tensor(at_row[n % 2][:], m.row_no[:].unsqueeze(1).to_broadcast([TT, TC, 128]),
                                        row_f[:, c, t0:t0 + TC].unsqueeze(2).to_broadcast([TT, TC, 128]), ALU.is_equal)
                chain.link(nc.vector.tensor_tensor(at_tile[n % 2][:], m.tile_no[:].unsqueeze(1).to_broadcast([TT, TC, Q]),
                                                   tile_f[:, c, t0:t0 + TC].unsqueeze(2).to_broadcast([TT, TC, Q]), ALU.is_equal))
                nc.vector.tensor_tensor(at_tile[n % 2][:], at_tile[n % 2][:], m.name_of[:, c, t0:t0 + TC].unsqueeze(2).to_broadcast([TT, TC, Q]),
                                        ALU.mult).then_inc(spread_ready, 1)
            shape = [1, SLOT_TILES, E]
            chain.link(nc.vector.tensor_tensor(past[:], m.tile_no[0:1].unsqueeze(2).to_broadcast(shape),
                                               upto[0:1].unsqueeze(1).to_broadcast(shape), ALU.is_ge))
            chain.link(nc.vector.tensor_reduce(tab[:], past[:], AX_X, ALU.add))
            chain.link(nc.vector.tensor_scalar(tab[:], tab[:], float(E - 1), None, ALU.min))
            chain.link(nc.vector.tensor_copy(table[:], tab[:]))
            dve.wait_ge(spread_used, len(STEPS) + ONE)
            chain.link(nc.vector.tensor_copy(who[:], who_ps))
            chain.link(nc.vector.tensor_scalar(empty[:], who[:], 0.0, None, ALU.is_equal))
            chain.link(nc.vector.scalar_tensor_tensor(goes[:], who[:], -1.0, empty[:], ALU.add, ALU.add))
            chain.link(nc.vector.tensor_copy(token[:], goes[:]))
            chain.link(nc.vector.tensor_scalar(token[:], token[:], 1, None, ALU.logical_shift_right))
            chain.link(nc.vector.tensor_tensor(empty[:], empty[:], m.spare_row[:], ALU.mult))
            chain.link(nc.vector.tensor_tensor(goes[:], goes[:], empty[:], ALU.add))
            nc.vector.tensor_copy(target[:], goes[:]).then_inc(places_ready, 1)
            dve.wait_ge(exp_ready, 1 + ONE)
            chain.link(nc.vector.tensor_reduce(total[:], ex[:], AX_X, ALU.add))
            chain.link(nc.vector.reciprocal(inv[:], total[:]))
            for c in range(2):
                chain.link(nc.vector.tensor_tensor(chosen[:].rearrange("p e t -> p t e"), ex[:], mask[c][:].rearrange("p e t -> p t e"), ALU.mult))
                chain.link(nc.vector.tensor_reduce(score[:, c, :], chosen[:].rearrange("p e t -> p t e"), AX_X, ALU.add))
                chain.link(nc.vector.tensor_tensor(score[:, c, :], score[:, c, :], inv[:], ALU.mult))
            chain.link(nc.vector.scalar_tensor_tensor(den[:], score[:, 0, :], GATE_EPS, score[:, 1, :], ALU.add, ALU.add))
            chain.link(nc.vector.reciprocal(den[:], den[:]))
            for c in range(2):
                chain.link(nc.vector.tensor_tensor(gate[c][:], score[:, c, :], den[:], ALU.mult))

            def rows_in(q, p):
                dve.wait_ge(xt_hi, q + (1 + ONE))
                nc.vector.tensor_tensor(xt_l[p][:], m.ps[:, XT, 0:D], xt_h[p][:], ALU.subtract).then_inc(xt_lo, 1)

            def gated(q, p):
                dve.wait_ge(silu_ready, q + (1 + ONE))
                dve.wait_ge(up3_ready, q + (1 + ONE))
                nc.vector.scalar_tensor_tensor(g[p][:], m.ps[:, 2 * p + 1, :], 1.0 / WS, si[p][:], ALU.mult, ALU.mult).then_inc(g_ready, 1)

            def body(q, p, i, more_rows, more_up):
                dve.wait_ge(gt_hi, q + (1 + ONE))
                nc.vector.tensor_tensor(gt_l[:], m.ps[:, GT, :], gt_h[:], ALU.subtract).then_inc(gt_lo, 1)
                if more_rows:
                    rows_in(q + 2, p)
                if more_up:
                    gated(q + 1, 1 - p)
                if i is not None:
                    dve.wait_ge(scattered[p], i * 16)
                dve.wait_ge(y_ready, q + (1 + ONE))
                nc.vector.tensor_scalar(ys[p][:], m.ps[:, Y, 0:D], 1.0 / WS, None, ALU.mult).then_inc(y_taken, 1)

            rows_in(0, 0)
            rows_in(1, 1)
            gated(0, 0)
            expert_loop(nc.vector, body)
            if last_round:
                dve.wait_ge(base_ready, 1 + ONE)
            for u in range(UNITS):
                dve.wait_ge(back[u % 2], 16 * (u // 2 + 1))
                for c in range(2):
                    for j in range(TPU):
                        z = total_out[:, u, j * D:(j + 1) * D]
                        ins = nc.vector.scalar_tensor_tensor(z, yb[u % 2][:, j, c, :], gate[c][:, u * TPU + j:u * TPU + j + 1], z, ALU.mult, ALU.add)
                    if c == 0:
                        chain.link(ins)
                    else:
                        ins.then_inc(used, 1)
            dve.wait_ge(used, UNITS + ONE)


class Memory:
    pass


def build(nc, a, out):
    ctx = ExitStack()
    with ctx:
        m = Memory()
        m.out = out

        def sb(name, shape, dt):
            return ctx.enter_context(nc.sbuf_tensor(name, shape, dt))

        m.x = a["x"]
        m.sems = {k: [ctx.enter_context(nc.semaphore(f"{k}_{n}")) for n in names] for k, names in SEMAPHORES.items()}
        m.ps = ctx.enter_context(nc.psum_tensor("ps", [128, 8, 512], F32))
        m.ident, m.minus_half = sb("ident", [128, 128], F32), sb("minus_half", [128, 2 * SEQ], F32)
        m.h, m.n1 = sb("h", [TT, UNITS, TPU * D], F32), sb("n1", [TT, UNITS, TPU * D], F32)
        m.stats, m.mv = sb("stats", [TT, TPU, 6], F32), sb("mv", [TT, TPU, 2], F32)
        m.carry = sb("carry", [TT, 1], F32)
        m.vareps, m.rstd = sb("vareps", [TT, TPU], F32), sb("rstd", [TT, TPU], F32)

        m.router_hi, m.router_lo = sb("router_hi", [128, KD * E], F16), sb("router_lo", [128, KD * E], F16)
        m.norm_w = sb("norm_w", [TT, D], F32)
        m.earlier, m.all_ones = sb("earlier", [TT, TT], F32), sb("all_ones", [TT, TT], F32)
        m.expert_no = sb("expert_no", [TT, E], F32)
        m.not_first = sb("not_first", [TT, E, TILES], F32)
        m.by128, m.tile_no, m.ones_row = sb("by128", [TT, IMAGES * SEQ // 128], F32), sb("tile_no", [TT, SLOT_TILES], F32), sb("ones_row", [TT, E], F32)
        m.row_no, m.name_of, m.spare_row = sb("row_no", [TT, 128], F32), sb("name_of", [TT, 2, TILES], F32), sb("spare_row", [128, SLOT_TILES], F32)

        def dram(name, shape, dt):
            return nc.dram_tensor(name, shape, dt, kind="Internal").ap()

        m.gram_d = dram("gram_d", (UNITS, UNIT_IMAGES, H, SEQ, 2 * SEQ), F32)
        m.w_d = dram("w_d", (UNITS, UNIT_IMAGES, H, SEQ, 2 * SEQ), F16)
        m.beta_d, m.alpha_d, m.qn_d = (dram(n, (UNITS, UNIT_IMAGES, H, SEQ), F32) for n in ("beta_d", "alpha_d", "qn_d"))
        batch = "(b v) i h t -> b (v i h) t"
        m.gram_b = m.gram_d.rearrange("(b v) i h s n -> b (v i h) s n", v=2)
        m.w_b = m.w_d.rearrange("(b v) i h s n -> b (v i h) s n", v=2)
        m.beta_b, m.alpha_b, m.qn_b = (t.rearrange(batch, v=2) for t in (m.beta_d, m.alpha_d, m.qn_d))

        with ExitStack() as att:
            def sa(name, shape, dt):
                return att.enter_context(nc.sbuf_tensor(name, shape, dt))

            m.nt_hi, m.nt_lo = sa("nt_hi", [128, UNITS, KD, UT], F16), sa("nt_lo", [128, UNITS, KD, UT], F16)
            m.ones = sa("ones", [128, 1], F32)
            m.wbd = [sa(f"wbd{g}", [SEQ * n, H, n, 2 * SEQ], F16) for g, (_, n) in enumerate(GROUPS)]
            m.qk_hi = [sa(f"qk_hi{p}", [128, 2 * UT + 28], F16) for p in range(2)]
            m.qk_lo = [sa(f"qk_lo{p}", [128, 2 * UT + 28], F16) for p in range(2)]
            jobs, pairs = [], {}
            for name in ("wp", "wba"):
                n = a[name].shape[1]
                pairs[name] = sa(name + "_hi", [128, n], F16), sa(name + "_lo", [128, n], F16)
                jobs.append((a[name], *pairs[name], n))
            m.wp_hi, m.wp_lo = pairs["wp"]
            m.wba_hi, m.wba_lo = pairs["wba"]
            m.wall = a["wall"]
            m.wall_hi, m.wall_lo = (sa("wall_" + n, [128, UNITS, WALL // UNITS], F16) for n in ("hi", "lo"))
            halves = [w.rearrange("p u n -> p (u n)") for w in (m.wall_hi, m.wall_lo)]
            (m.wq_hi, m.wq_lo), (m.wk_hi, m.wk_lo), (m.wv_hi, m.wv_lo), (m.wo_hi, m.wo_lo), (m.w1_hi, m.w1_lo), (m.w2_hi, m.w2_lo) = (
                [w[:, i * WCOLS:(i + 1) * WCOLS] for w in halves] for i in range(WALL // WCOLS))
            m.pos, m.bproj = sa("pos", [TT, TPU * D], F32), sa("bproj", [TT, TPU * D], F32)
            m.ln1_w, m.ln1_b, m.ln2_w, m.ln2_b, m.b2 = (sa(n, [TT, D], F32) for n in ("ln1_w", "ln1_b", "ln2_w", "ln2_b", "b2"))
            m.b1 = sa("b1", [128, F // 128], F32)
            m.plain = [(m.pos[:], a["pos"]), (m.bproj[:], a["bproj"]), (m.ln1_w[:], a["ln1_w"]), (m.ln1_b[:], a["ln1_b"]),
                       (m.ln2_w[:], a["ln2_w"]), (m.ln2_b[:], a["ln2_b"]), (m.b2[:], a["b2"]), (m.b1[:], a["b1"]), (m.norm_w[:], a["norm_w"])]
            jobs.append((a["router"], m.router_hi, m.router_lo, KD * E))
            load_weights(nc, m, jobs)
            phase_tokens(nc, m)
            phase_grams(nc, m)
            phase_mix(nc, m)
        with ExitStack() as moe:
            def sm(name, shape, dt):
                return moe.enter_context(nc.sbuf_tensor(name, shape, dt))

            m.zn_d, m.y_d = dram("zn_d", (IMAGES * SEQ, D), F32), dram("y_d", (2 * IMAGES * SEQ + ROWS, D), F32)
            m.experts = a["experts"]
            m.experts_hi, m.experts_lo = (sm("experts_" + n, [128, PIECES, PIECE], F16) for n in ("hi", "lo"))
            halves = [w.rearrange("p t n -> p (t n)") for w in (m.experts_hi, m.experts_lo)]
            EC = E * KD * FE
            (m.e1_hi, m.e1_lo), (m.e3_hi, m.e3_lo), (m.e2_hi, m.e2_lo) = ([w[:, i * EC:(i + 1) * EC] for w in halves] for i in range(3))
            for m.round in range(1, LOOPS + 1):
                phase_moe(nc, m)


def kernel(x, L0_tok_W_proj, L0_tok_b_proj, L0_tok_pos_emb, L0_attn_Wq, L0_attn_Wk, L0_attn_Wv, L0_attn_Wb, L0_attn_Wa,
           L0_attn_Wo, L0_attn_ln1_w, L0_attn_ln1_b, L0_attn_ln2_w, L0_attn_ln2_b, L0_attn_W1, L0_attn_b1, L0_attn_W2,
           L0_attn_b2, L0_ffn_norm_w, L0_ffn_router_w, L0_ffn_w1, L0_ffn_w3, L0_ffn_w2):
    import numpy as np
    import concourse.bacc as bacc
    from concourse.bass_utils import run_bass_kernel_spmd

    def rows(w):
        w = np.asarray(w)
        return np.ascontiguousarray(w.reshape(-1, 128, w.shape[1]).transpose(1, 0, 2).reshape(128, -1))

    def experts(w):
        w = np.asarray(w)
        return np.ascontiguousarray(w.reshape(E, -1, 128, w.shape[2]).transpose(2, 0, 1, 3).reshape(128, -1))

    def spread(v, reps=1):
        v = np.asarray(v)
        return np.ascontiguousarray(np.broadcast_to(v, (TT, reps, v.shape[0])).reshape(TT, -1))

    xs = np.asarray(x).reshape(UNITS, UNIT_IMAGES, 6, 16, 6, 48).transpose(0, 3, 5, 1, 2, 4).reshape(UNITS, KP, 128, UT)
    token = (np.arange(TPU)[None, :] * TT + np.arange(TT)[:, None]) % SEQ
    arrays = {
        "x": np.ascontiguousarray(xs.transpose(0, 2, 1, 3)),
        "wp": rows(np.asarray(L0_tok_W_proj).T),
        "pos": np.ascontiguousarray(np.asarray(L0_tok_pos_emb)[token].reshape(TT, TPU * D)),
        "bproj": spread(L0_tok_b_proj, TPU),
        "wall": np.ascontiguousarray(np.concatenate([rows(w) for w in (
            L0_attn_Wq, L0_attn_Wk, L0_attn_Wv, L0_attn_Wo, L0_attn_W1, L0_attn_W2)], axis=1).reshape(
                128, UNITS, -1).transpose(1, 0, 2)),
        "wba": rows(np.concatenate([np.asarray(L0_attn_Wb), np.asarray(L0_attn_Wa)], axis=1)),
        "ln1_w": spread(L0_attn_ln1_w), "ln1_b": spread(L0_attn_ln1_b),
        "ln2_w": spread(L0_attn_ln2_w), "ln2_b": spread(L0_attn_ln2_b), "b2": spread(L0_attn_b2),
        "experts": np.ascontiguousarray(np.concatenate([experts(w) for w in (L0_ffn_w1, L0_ffn_w3, L0_ffn_w2)], axis=1).reshape(
            128, PIECES, PIECE).transpose(1, 0, 2)),
        "router": rows(L0_ffn_router_w), "norm_w": spread(L0_ffn_norm_w),
        "b1": np.ascontiguousarray(np.asarray(L0_attn_b1).reshape(-1, 128).T),
    }
    nc = bacc.Bacc("TRN2", target_bir_lowering=False, num_devices=1)
    aps = {k: nc.dram_tensor(k + "_dram", v.shape, mybir.dt.from_np(v.dtype), kind="ExternalInput").ap() for k, v in arrays.items()}
    out = nc.dram_tensor("out_dram", (UNITS, TT, TPU * D), F32, kind="ExternalOutput").ap()
    build(nc, aps, out)
    r = run_bass_kernel_spmd(nc, [{k + "_dram": v for k, v in arrays.items()}], core_ids=[0])
    y = np.asarray(r.results[0]["out_dram"])
    return y.reshape(UNITS, TT, TPU, D).transpose(0, 2, 1, 3).reshape(IMAGES, SEQ, D)
```
